# Optimizing a Trainium2 kernel written in Bass

```python
import numpy as np
import jax
import jax.numpy as jnp

def _softmax(x, axis=-1):
    return jax.nn.softmax(x, axis=axis)

def _gelu(x):
    return jax.nn.gelu(x, approximate=True)

def _silu(x):
    return jax.nn.silu(x)

def _sigmoid(x):
    return jax.nn.sigmoid(x)

def _layernorm(x, axis=-1, eps=1e-05):
    m = jnp.mean(x, axis=axis, keepdims=True)
    v = jnp.var(x, axis=axis, keepdims=True)
    return (x - m) / jnp.sqrt(v + eps)

def _scatter_add(tgt, idx, src, axis=0):
    return tgt.at[idx].add(src)

def _segment_sum(src, seg, n):
    return jax.ops.segment_sum(src, seg, n)
kernel_name = 'mk_gnn_preln_d4_gnn_r8_0139c0'

def setup_inputs(seed: int=0):
    np.random.seed(seed)
    _w = jnp.asarray

    def _rec_inputs():
        import jax
        import jax.numpy as jnp
        _gk = jax.random.key(seed)
        x = -0.000202 + 1 * jax.random.normal(jax.random.fold_in(_gk, 1), (12500, 64), jnp.float32)
        _s = jax.random.randint(jax.random.fold_in(_gk, 2), (100000,), 0, 12500, jnp.int32)
        _d = jax.random.randint(jax.random.fold_in(_gk, 3), (100000,), 0, 12500, jnp.int32)
        _loop = jnp.arange(12500, dtype=jnp.int32)
        src = jnp.concatenate([_s, _d, _loop])
        dst = jnp.concatenate([_d, _s, _loop])
        _o = jnp.argsort(dst, stable=True)
        src = src[_o]
        dst = dst[_o]
        edge_attr_16 = 0.000196303 + 1.00016 * jax.random.normal(jax.random.fold_in(_gk, 12), (212500, 16), jnp.float32)
        edge_attr_64 = -6.74381e-05 + 0.999835 * jax.random.normal(jax.random.fold_in(_gk, 13), (212500, 64), jnp.float32)
        return (x, src, dst, edge_attr_16, edge_attr_64)
    x, src, dst, edge_attr_16, edge_attr_64 = _rec_inputs()

    def _L0_gnn_setup():
        import jax, jax.numpy as jnp
        import numpy as np
        N_NODES = 12500
        N_EDGES = 156250
        D = 64
        H = 128
        key = jax.random.key(seed)
        ks = jax.random.split(key, 8)
        s = 1.0 / np.sqrt(D)
        return {'nodes': jax.random.normal(ks[0], (N_NODES, D), jnp.float32), 'edges': jax.random.normal(ks[1], (N_EDGES, D), jnp.float32), 'senders': jax.random.randint(ks[2], (N_EDGES,), 0, N_NODES, jnp.int32), 'receivers': jax.random.randint(ks[3], (N_EDGES,), 0, N_NODES, jnp.int32), 'We_w': jax.random.normal(ks[4], (D, D), jnp.float32) * s, 'We_b': jnp.zeros((D,), jnp.float32), 'eps': jnp.zeros((1, 1), jnp.float32), 'W1': jax.random.normal(ks[5], (D, H), jnp.float32) * s, 'b1': jnp.zeros((H,), jnp.float32), 'W2': jax.random.normal(ks[6], (H, D), jnp.float32) * (1.0 / np.sqrt(H)), 'b2': jnp.zeros((D,), jnp.float32)}
    _L0_gnn_all = _L0_gnn_setup()
    _L0_gnn_in = {k: v for k, v in _L0_gnn_all.items() if k in ('We_w', 'We_b', 'eps', 'W1', 'b1', 'W2', 'b2')}
    del _L0_gnn_all

    def _L1_gnn_setup():
        import jax, jax.numpy as jnp
        import numpy as np
        N = 12500
        E = 200000
        H = 64
        EF = 16
        EPS = 1e-05

        def _layer_norm(x, gamma, beta):
            mu = jnp.mean(x, axis=-1, keepdims=True)
            var = jnp.mean(jnp.square(x - mu), axis=-1, keepdims=True)
            return (x - mu) * jax.lax.rsqrt(var + EPS) * gamma + beta
        key = jax.random.key(seed)
        ks = jax.random.split(key, 12)
        s = 0.05
        return {'node_features': jax.random.normal(ks[0], (N, H), jnp.float32), 'edge_index': jax.random.randint(ks[1], (2, E), 0, N, dtype=jnp.int64), 'edge_features': jax.random.normal(ks[2], (E, EF), jnp.float32), 'W_m1': jax.random.normal(ks[3], (2 * H + EF, H), jnp.float32) * s, 'b_m1': jnp.zeros((H,), jnp.float32), 'W_m2': jax.random.normal(ks[4], (H, H), jnp.float32) * s, 'b_m2': jnp.zeros((H,), jnp.float32), 'W_u1': jax.random.normal(ks[5], (2 * H, H), jnp.float32) * s, 'b_u1': jnp.zeros((H,), jnp.float32), 'W_u2': jax.random.normal(ks[6], (H, H), jnp.float32) * s, 'b_u2': jnp.zeros((H,), jnp.float32), 'gamma': jnp.ones((H,), jnp.float32), 'beta': jnp.zeros((H,), jnp.float32)}
    _L1_gnn_all = _L1_gnn_setup()
    _L1_gnn_in = {k: v for k, v in _L1_gnn_all.items() if k in ('W_m1', 'b_m1', 'W_m2', 'b_m2', 'W_u1', 'b_u1', 'W_u2', 'b_u2', 'gamma', 'beta')}
    del _L1_gnn_all

    def _L2_gnn_setup():
        import jax, jax.numpy as jnp
        import numpy as np
        N_NODES = 12500
        N_EDGES = 200000
        IN_FEAT = 64
        OUT_FEAT = 64
        key = jax.random.key(seed)
        k_feat, k_src, k_dst, k_tw, k_tb, k_pw, k_pb = jax.random.split(key, 7)
        bound = 1.0 / np.sqrt(IN_FEAT)
        return {'feat': jax.random.normal(k_feat, (N_NODES, IN_FEAT), dtype=jnp.float32), 'src': jax.random.randint(k_src, (N_EDGES,), 0, N_NODES, dtype=jnp.int32), 'dst': jax.random.randint(k_dst, (N_EDGES,), 0, N_NODES, dtype=jnp.int32), 'theta_w': jax.random.uniform(k_tw, (OUT_FEAT, IN_FEAT), jnp.float32, -bound, bound), 'theta_b': jax.random.uniform(k_tb, (OUT_FEAT,), jnp.float32, -bound, bound), 'phi_w': jax.random.uniform(k_pw, (OUT_FEAT, IN_FEAT), jnp.float32, -bound, bound), 'phi_b': jax.random.uniform(k_pb, (OUT_FEAT,), jnp.float32, -bound, bound)}
    _L2_gnn_all = _L2_gnn_setup()
    _L2_gnn_in = {k: v for k, v in _L2_gnn_all.items() if k in ('theta_w', 'theta_b', 'phi_w', 'phi_b')}
    del _L2_gnn_all

    def _L3_gnn_setup():
        import jax, jax.numpy as jnp
        import numpy as np
        N_NODES = 12500
        N_EDGES = 200000

        def _mean_agg(h, src, dst, deg):
            summed = jax.ops.segment_sum(h[src], dst, num_segments=N_NODES)
            return summed / deg[:, None]

        def _sage_layer(h, src, dst, deg, w_self, w_neigh, b):
            h_neigh = _mean_agg(h, src, dst, deg)
            return jax.nn.relu(h @ w_self + h_neigh @ w_neigh + b)
        key = jax.random.key(seed)
        ks = jax.random.split(key, 10)
        feat = jax.random.normal(ks[0], (N_NODES, 64), dtype=jnp.float32)
        src = jax.random.randint(ks[1], (N_EDGES,), 0, N_NODES, dtype=jnp.int32)
        dst = jax.random.randint(ks[2], (N_EDGES,), 0, N_NODES, dtype=jnp.int32)

        def lin(k, din, dout):
            return jax.random.normal(k, (din, dout), dtype=jnp.float32) * (1.0 / np.sqrt(din))
        return {'feat': feat, 'src': src, 'dst': dst, 'ws0': lin(ks[3], 64, 128), 'wn0': lin(ks[4], 64, 128), 'b0': jnp.zeros((128,), jnp.float32), 'ws1': lin(ks[5], 128, 128), 'wn1': lin(ks[6], 128, 128), 'b1': jnp.zeros((128,), jnp.float32), 'ws2': lin(ks[7], 128, 64), 'wn2': lin(ks[8], 128, 64), 'b2': jnp.zeros((64,), jnp.float32)}
    _L3_gnn_all = _L3_gnn_setup()
    _L3_gnn_in = {k: v for k, v in _L3_gnn_all.items() if k in ('ws0', 'wn0', 'b0', 'ws1', 'wn1', 'b1', 'ws2', 'wn2', 'b2')}
    del _L3_gnn_all
    return {'x': x, 'src': src, 'dst': dst, 'edge_attr_16': edge_attr_16, 'edge_attr_64': edge_attr_64, 'L0_gnn_We_w': _L0_gnn_in['We_w'], 'L0_gnn_We_b': _L0_gnn_in['We_b'], 'L0_gnn_eps': _L0_gnn_in['eps'], 'L0_gnn_W1': _L0_gnn_in['W1'], 'L0_gnn_b1': _L0_gnn_in['b1'], 'L0_gnn_W2': _L0_gnn_in['W2'], 'L0_gnn_b2': _L0_gnn_in['b2'], 'L1_gnn_W_m1': _L1_gnn_in['W_m1'], 'L1_gnn_b_m1': _L1_gnn_in['b_m1'], 'L1_gnn_W_m2': _L1_gnn_in['W_m2'], 'L1_gnn_b_m2': _L1_gnn_in['b_m2'], 'L1_gnn_W_u1': _L1_gnn_in['W_u1'], 'L1_gnn_b_u1': _L1_gnn_in['b_u1'], 'L1_gnn_W_u2': _L1_gnn_in['W_u2'], 'L1_gnn_b_u2': _L1_gnn_in['b_u2'], 'L1_gnn_gamma': _L1_gnn_in['gamma'], 'L1_gnn_beta': _L1_gnn_in['beta'], 'L2_gnn_theta_w': _L2_gnn_in['theta_w'], 'L2_gnn_theta_b': _L2_gnn_in['theta_b'], 'L2_gnn_phi_w': _L2_gnn_in['phi_w'], 'L2_gnn_phi_b': _L2_gnn_in['phi_b'], 'L3_gnn_ws0': _L3_gnn_in['ws0'], 'L3_gnn_wn0': _L3_gnn_in['wn0'], 'L3_gnn_b0': _L3_gnn_in['b0'], 'L3_gnn_ws1': _L3_gnn_in['ws1'], 'L3_gnn_wn1': _L3_gnn_in['wn1'], 'L3_gnn_b1': _L3_gnn_in['b1'], 'L3_gnn_ws2': _L3_gnn_in['ws2'], 'L3_gnn_wn2': _L3_gnn_in['wn2'], 'L3_gnn_b2': _L3_gnn_in['b2']}

def reference(x, src, dst, edge_attr_16, edge_attr_64, L0_gnn_We_w, L0_gnn_We_b, L0_gnn_eps, L0_gnn_W1, L0_gnn_b1, L0_gnn_W2, L0_gnn_b2, L1_gnn_W_m1, L1_gnn_b_m1, L1_gnn_W_m2, L1_gnn_b_m2, L1_gnn_W_u1, L1_gnn_b_u1, L1_gnn_W_u2, L1_gnn_b_u2, L1_gnn_gamma, L1_gnn_beta, L2_gnn_theta_w, L2_gnn_theta_b, L2_gnn_phi_w, L2_gnn_phi_b, L3_gnn_ws0, L3_gnn_wn0, L3_gnn_b0, L3_gnn_ws1, L3_gnn_wn1, L3_gnn_b1, L3_gnn_ws2, L3_gnn_wn2, L3_gnn_b2):
    import jax
    import jax.numpy as jnp

    def _L0_gnn_ref(nodes, edges, senders, receivers, We_w, We_b, eps, W1, b1, W2, b2):
        import jax, jax.numpy as jnp
        import numpy as np
        N_NODES = 12500
        N_EDGES = 156250
        D = 64
        H = 128
        msg = nodes[senders] + (edges @ We_w + We_b)
        agg = jax.ops.segment_sum(msg, receivers, num_segments=N_NODES)
        h = (1.0 + eps) * nodes + agg
        h = jax.nn.relu(h @ W1 + b1)
        out = h @ W2 + b2
        return out

    def _L1_gnn_ref(node_features, edge_index, edge_features, W_m1, b_m1, W_m2, b_m2, W_u1, b_u1, W_u2, b_u2, gamma, beta):
        import jax, jax.numpy as jnp
        import numpy as np
        N = 12500
        E = 200000
        H = 64
        EF = 16
        EPS = 1e-05

        def _layer_norm(x, gamma, beta):
            mu = jnp.mean(x, axis=-1, keepdims=True)
            var = jnp.mean(jnp.square(x - mu), axis=-1, keepdims=True)
            return (x - mu) * jax.lax.rsqrt(var + EPS) * gamma + beta
        src_idx = edge_index[0]
        dst_idx = edge_index[1]
        h_src = node_features[src_idx]
        h_dst = node_features[dst_idx]
        msg_in = jnp.concatenate([h_dst, h_src, edge_features], axis=1)
        messages = jax.nn.relu(msg_in @ W_m1 + b_m1) @ W_m2 + b_m2
        aggregated = jax.ops.segment_sum(messages, dst_idx, num_segments=node_features.shape[0])
        upd_in = jnp.concatenate([node_features, aggregated], axis=1)
        updated = jax.nn.relu(upd_in @ W_u1 + b_u1) @ W_u2 + b_u2
        return _layer_norm(node_features + updated, gamma, beta)

    def _L2_gnn_ref(feat, src, dst, theta_w, theta_b, phi_w, phi_b):
        import jax, jax.numpy as jnp
        import numpy as np
        N_NODES = 12500
        N_EDGES = 200000
        IN_FEAT = 64
        OUT_FEAT = 64
        h_theta = feat @ theta_w.T + theta_b
        h_phi = feat @ phi_w.T + phi_b
        diff = h_phi - h_theta
        e = h_theta[src] + diff[dst]
        out = jax.ops.segment_max(e, dst, num_segments=N_NODES)
        return jnp.where(jnp.isfinite(out), out, jnp.float32(0))

    def _L3_gnn_ref(feat, src, dst, ws0, wn0, b0, ws1, wn1, b1, ws2, wn2, b2):
        import jax, jax.numpy as jnp
        import numpy as np
        N_NODES = 12500
        N_EDGES = 200000

        def _mean_agg(h, src, dst, deg):
            summed = jax.ops.segment_sum(h[src], dst, num_segments=N_NODES)
            return summed / deg[:, None]

        def _sage_layer(h, src, dst, deg, w_self, w_neigh, b):
            h_neigh = _mean_agg(h, src, dst, deg)
            return jax.nn.relu(h @ w_self + h_neigh @ w_neigh + b)
        deg_i = jax.ops.segment_sum(jnp.ones_like(dst, dtype=jnp.float32), dst, num_segments=N_NODES)
        deg = jnp.maximum(deg_i, 1.0)
        h = _sage_layer(feat, src, dst, deg, ws0, wn0, b0)
        h = _sage_layer(h, src, dst, deg, ws1, wn1, b1)
        h = _sage_layer(h, src, dst, deg, ws2, wn2, b2)
        return h
    edge_index = jnp.stack([src, dst])
    h = jnp.maximum(_layernorm(x, axis=-1), 0.0)
    x = x + _L0_gnn_ref(h, edge_attr_64, src, dst, L0_gnn_We_w, L0_gnn_We_b, L0_gnn_eps, L0_gnn_W1, L0_gnn_b1, L0_gnn_W2, L0_gnn_b2)
    h = jnp.maximum(_layernorm(x, axis=-1), 0.0)
    x = x + _L1_gnn_ref(h, edge_index, edge_attr_16, L1_gnn_W_m1, L1_gnn_b_m1, L1_gnn_W_m2, L1_gnn_b_m2, L1_gnn_W_u1, L1_gnn_b_u1, L1_gnn_W_u2, L1_gnn_b_u2, L1_gnn_gamma, L1_gnn_beta)
    h = jnp.maximum(_layernorm(x, axis=-1), 0.0)
    x = x + _L2_gnn_ref(h, src, dst, L2_gnn_theta_w, L2_gnn_theta_b, L2_gnn_phi_w, L2_gnn_phi_b)
    h = jnp.maximum(_layernorm(x, axis=-1), 0.0)
    x = x + _L3_gnn_ref(h, src, dst, L3_gnn_ws0, L3_gnn_wn0, L3_gnn_b0, L3_gnn_ws1, L3_gnn_wn1, L3_gnn_b1, L3_gnn_ws2, L3_gnn_wn2, L3_gnn_b2)
    return x

_drawn_inputs = setup_inputs


def setup_inputs(seed=0):
    import zlib

    import numpy as np

    out = dict(_drawn_inputs(seed))
    spreads = {'L0_gnn_We_b': (0.0, 0.1),
     'L0_gnn_b1': (0.0, 0.653),
     'L0_gnn_b2': (0.0, 0.517),
     'L1_gnn_b_m1': (0.0, 2.0),
     'L1_gnn_b_m2': (0.0, 0.419),
     'L1_gnn_b_u1': (0.0, 2.0),
     'L1_gnn_b_u2': (0.0, 0.385),
     'L1_gnn_gamma': (1.0, 0.2),
     'L1_gnn_beta': (0.0, 0.507),
     'L3_gnn_b0': (0.0, 0.8),
     'L3_gnn_b1': (0.0, 0.8),
     'L3_gnn_b2': (0.0, 0.8)}
    factors = {'edge_attr_16': 25.601, 'L2_gnn_theta_b': 200.0, 'L2_gnn_phi_b': 4.757}
    for name, (base, spread) in spreads.items():
        noise = np.random.default_rng([zlib.crc32(name.encode()), seed]).standard_normal(out[name].shape)
        drawn = base * np.exp(spread * noise) if base else spread * noise
        out[name] = jnp.asarray(drawn.astype(out[name].dtype))
    for name, factor in factors.items():
        out[name] = (out[name] * factor).astype(out[name].dtype)
    return out
```

```python
import numpy as np
import concourse.bass as bass
from concourse import mybir
from contextlib import ExitStack

N = 12500
E = 212500
D = 64
H = 128
P = 128
LN_EPS = 1e-5

U = 16
HALF = U // 2
NT = -(-E // (P * U)) * U
NIT = NT // U
CHUNKS = -(-N // P)
ROWS = CHUNKS * P
COLS = ROWS + P
C7 = 7
NLOOP = CHUNKS // C7
NC = C7 * P
NF = C7 * D
assert C7 * NLOOP == CHUNKS

F32 = mybir.dt.float32
BF16 = mybir.dt.bfloat16
I32 = mybir.dt.int32
ALU = mybir.AluOpType
ACT = mybir.ActivationFunctionType
AX = mybir.AxisListType

PACK = dict(ident=(128, 128), iota=(128, 128), we=(128, 64), w1=(64, 128), b1=(128, 1), w2=(128, 64), b2=(1, 64),
            ones=(1, 128), we_b=(128, 64), eps=(128, 1), wa2=(64, 128), wb=(64, 64), wc=(17, 64), wm2=(65, 65),
            wu1a=(64, 64), wu1b=(64, 64), bu1=(64, 1), wu2=(65, 64), e64=(65, 1), gamma=(128, 64),
            beta=(128, 64), theta=(65, 64), phi=(65, 64), ws0=(65, 128), wn0=(64, 128), ws1=(128, 128),
            sb1=(1, 128), wn1=(128, 128), wn2=(128, 64), ws2=(128, 64), sb2=(1, 64), zero=(128, 1))
AT = {}
WCOLS = 0
for _name, (_rows, _cols) in PACK.items():
    AT[_name] = WCOLS
    WCOLS += _cols


def gnn(nc, x_in, src_in, dst_in, next_in, dstrow_in, prevrow_in, ea_in, ef_in, pack_in, out):
    ctx = ExitStack()
    with ctx:
        def sb(name, shape, dt=F32):
            return ctx.enter_context(nc.sbuf_tensor(name, shape, dt))

        def sem(name):
            return ctx.enter_context(nc.semaphore(name))

        widths = [D, D, D, D, H, D]
        table = [nc.dram_tensor(f"table{k}", (ROWS, w), F32).ap() for k, w in enumerate(widths)]
        table_nm = [t.rearrange("(p c) f -> p (c f)", p=P) for t in table]
        ew_dram = nc.dram_tensor("edge_term", (NT // HALF * P, HALF * D), F32).ap()
        mask_dram = nc.dram_tensor("scan_mask", (1, NT * P), BF16).ap()

        agg = sb("agg", [P, COLS])
        big = sb("big", [P, COLS])
        part_hm = big[:, 0:COLS // 2].bitcast(BF16)
        part_lo = big[0:D, COLS // 2:COLS].bitcast(BF16)
        x_nm = sb("x_nm", [P, CHUNKS * D])
        h_nm = sb("h_nm", [P, CHUNKS * D])
        src_idx = sb("src_idx", [P, NT + U], I32)
        base = sb("base", [1, NT], I32)
        rel = sb("rel", [P, NT], BF16)
        rel_end = sb("rel_end", [P, NT], BF16)
        deg = sb("deg", [P, CHUNKS])
        rdeg = sb("rdeg", [P, CHUNKS, 1])
        has_in = sb("has_in", [P, CHUNKS, 1])
        idxw = sb("idxw", [P, U], I32)
        W = sb("W", [P, WCOLS])
        ident_e = sb("ident_e", [P, P])
        ident_b = sb("ident_b", [P, P], BF16)
        stat = sb("stat", [P, 4, C7, 1])
        AR = 7168
        arena = sb("arena", [P, AR])
        PS = ctx.enter_context(nc.psum_tensor("PS", [P, 8 * 512], F32))

        def w(name):
            r, c = PACK[name]
            return W[0:r, AT[name]:AT[name] + c]

        def carve(*sizes):
            at, got = 0, []
            for s in sizes:
                got.append(arena[:, at:at + s])
                at += s
            assert at <= AR, at
            return got

        def bank(b, n=512, o=0, rows=P):
            return PS[0:rows, b * 512 + o:b * 512 + o + n]

        def n3(ap):
            return ap.rearrange("p (c f) -> p c f", c=C7)

        msg_f, rest, S_f = arena[:, 0:U * H], arena[:, U * D:AR - U * P], arena[:, AR - U * P:AR]
        S = S_f.rearrange("p (t w) -> p t w", t=U)

        gathered = [sem(f"gathered{j}") for j in range(U)]
        phase = sem("phase")
        phases = dict(sp=0, act=0, pool=0, dve=0, pe=0)

        def hold(eng):
            eng.nop(nofuse=True)

        def barrier(eng, who):
            phases[who] += 1
            eng.drain().then_inc(phase, 1)
            eng.wait_ge(phase, 5 * phases[who])

        class Pass:

            def __init__(self, k, name, rows):
                self.k, self.rows, self.width = k, rows, widths[k]
                self.msg = (msg_f[:, 0:U * self.width]).rearrange("p (t f) -> p t f", t=U)
                self.idx_ready = sem(f"{name}_idx_ready")
                self.s_ready = sem(f"{name}_s_ready")
                self.summed = sem(f"{name}_summed")
                self.used = self.summed
                self.added = sem(f"{name}_added")

        PL0, PL1, PL2, PL3a, PL3b, PL3c = (Pass(k, n, r) for k, (n, r) in enumerate(
            [("l0", P), ("l1", D + 1), ("l2", D), ("l3a", D), ("l3b", H), ("l3c", D)]))
        PL1.used = sem("l1_used")
        PL2.used = sem("l2_used")

        def acc_slot(T, rows):
            return bank((2, 3, 6, 7)[T % 4], P, 0, rows)

        def pool_gathers(pool, ps, used, unit):
            n, h = U // unit, HALF // unit
            with pool.Fori(0, NIT) as i:
                for half in range(2):
                    pool.wait_ge(used, i * n + (half + 1) * h)
                    pool.wait_ge(ps.idx_ready, i * 2 + half + 1)
                    hold(pool)
                    for j in range(half * HALF, (half + 1) * HALF):
                        pool.indirect_dma_start(
                            out=ps.msg[:, j, :], out_offset=None, in_=table[ps.k],
                            in_offset=bass.IndirectOffsetOnAxis(ap=idxw[:, j:j + 1], axis=0)
                        ).then_inc(gathered[j], 16)

        def act_idx(act, ps, col, half):
            act.activation(idxw[:, half * HALF:(half + 1) * HALF], src_idx[:, bass.ds(col, HALF)],
                           ACT.Copy).then_inc(ps.idx_ready, 1)

        def tile_landed(eng, ps, i, j):
            eng.wait_ge(gathered[j], i * 16 + (ps.k * NIT + 1) * 16)

        def dve_bases(i):
            _, b = nc.values_load_multi_w_load_instructions(
                base[0:1, bass.ds(i * U, U)], engines=[mybir.EngineType.DVE], min_val=0, max_val=N,
                skip_runtime_bounds_check_because="dst holds node numbers below N, the padding N")
            return b

        def dve_s(dve, ps, i, column):
            for j in range(U):
                dve.tensor_scalar(out=S[:, j, :], in0=w("iota"), scalar1=column[:, bass.ds(i * U + j, 1)],
                                  scalar2=None, op0=ALU.is_equal).then_inc(ps.s_ready, 1)

        def dve_add(dve, ps, b, i, js):
            for j in js:
                dve.wait_ge(ps.summed, i * U + j + 1 + U)
                dve.wait_ge(ps.added, i * U + j + 4)
                win = agg[0:ps.rows, bass.ds(b[j], P)]
                dve.tensor_tensor(out=win, in0=acc_slot(j, ps.rows), in1=win, op=ALU.add).then_inc(ps.added, 1)

        ea_in_sem = [sem(f"ea_loaded{h}") for h in range(2)]
        ef_in_sem = [sem(f"ef_loaded{h}") for h in range(2)]
        ew_mm = sem("ew_mm")
        ew_sb = sem("ew_sb")
        ew_stored = sem("ew_stored")
        ew_free = sem("ew_free")
        ew_in_sem = [sem(f"ew_loaded{h}") for h in range(2)]
        win_t = sem("win_t")
        win_sb = sem("win_sb")
        pre_mm = sem("pre_mm")
        pre_ew = sem("pre_ew")
        relued = sem("relued")
        mask_in_sem = [sem(f"mask_loaded{h}") for h in range(2)]
        scanned = sem("scanned")
        back_t = sem("back_t")
        back_sb = sem("back_sb")
        s_load = sem("s_load")
        s_setup = sem("s_setup")
        s_mask = sem("s_mask")
        s_zero = sem("s_zero")

        ea_f, ef_f, ews_f = rest[:, 0:U * D], rest[:, U * D:3 * U * D], rest[:, 3 * U * D:4 * U * D]
        ea = ea_f.rearrange("p (t f) -> p t f", t=U)
        ef = ef_f.rearrange("p (h e) -> p h e", h=2)
        ews = ews_f.rearrange("p (h f) -> p h f", h=2)
        WIN = 3 * D + P
        at_l1 = [0, U * D, U * D + 4 * WIN, U * D + 4 * WIN + 8 * D, U * D + 4 * WIN + 8 * D + U * (D + 1)]
        ewl = rest[:, at_l1[0]:at_l1[1]].rearrange("p (h f) -> p h f", h=2)
        win = rest[:, at_l1[1]:at_l1[2]].bitcast(BF16).rearrange("p (t f) -> p t f", t=8)
        pre = rest[:, at_l1[2]:at_l1[3]].rearrange("p (g f) -> p g f", g=2)
        msg1 = rest[:, at_l1[3]:at_l1[4]].rearrange("p (t f) -> p t f", t=U)
        at_l2 = [0, U * P // 2, U * P // 2 + 8 * P, U * P // 2 + 8 * P + 8 * D]
        mask = rest[0:D, at_l2[0]:at_l2[1]].bitcast(BF16).rearrange("p (h e) -> p h e", h=2)
        run = rest[0:D, at_l2[1]:at_l2[2]].rearrange("p (g e) -> p g e", g=2)
        back = rest[:, at_l2[2]:at_l2[3]].rearrange("p (g f) -> p g f", g=2)

        class Loop:

            def __init__(self, name, **steps):
                self.steps = {who: names.split() for who, names in steps.items()}
                self.sem = {who: sem(f"{name}_{who}") for who in steps}
                self.told = {who: 0 for who in steps}

            def start(self, eng, who):
                eng.sem_inc(self.sem[who], len(self.steps[who]))

            def done(self, ins, who, name):
                assert self.steps[who][self.told[who]] == name, (who, name)
                self.told[who] += 1
                ins.then_inc(self.sem[who], 1)

            def stored(self, eng):
                self.told["sp"] += 1
                eng.sem_inc(self.sem["sp"], 1)

            def after(self, eng, i, *whos):
                for what in whos:
                    who, name = what.rstrip("<").split(".")
                    k = len(self.steps[who])
                    back = 0 if what.endswith("<") else k
                    eng.wait_ge(self.sem[who], i * k + back + self.steps[who].index(name) + 1)

        NORM = "{0}sum {0}mean {0}centred {0}squared {0}sumsq {0}var {0}rstd {0}normed"
        A = Loop("a", dve=NORM.format("") + " h tab", act="std", sp="stored")
        B = Loop("b", pe="U Z O HT TAB APT", act="hc uT zT std hT tab high rounded mid",
                 dve="x " + NORM.format("") + " h rest1 mid lo", pool="zero x h", sp="stored")
        C = Loop("c", pe="AG H1T RU O HT TH PH", act="hc agT h1T rT vstd std hT tab",
                 dve="deg v " + NORM.format("v") + " scaled shifted x " + NORM.format("") + " h diff",
                 pool="zero x", sp="stored")
        Dl = Loop("d", pe="T HT SELF", act="aggc std hT self",
                  dve="y times0 finite keep zero y0 x " + NORM.format("") + " h", pool="zero x", sp="stored")
        El = Loop("e", pe="M ZT SELF", act="aggc z zT self", dve="mean sum", pool="zero", sp="stored")
        Fl = Loop("f", pe="M ZT PROJ SELF", act="aggc z zT tab self", dve="mean sum", pool="zero", sp="stored")
        Gl = Loop("g", pe="T", act="aggc", dve="mean sum relu x", sp="stored")

        (hc_f, uT, zT, xt_f, xc_f, sq_f, hs_f, hT, tb_f, rounded_f, r1, mid_f) = carve(
            NF, NC, NC, NF, NF, NF, NF, NC, NF, NC // 2, NC, NC // 2)
        v_f = rounded_f
        hc, xt, xc, sq, hs, tb, vv = (n3(a) for a in (hc_f, xt_f, xc_f, sq_f, hs_f, tb_f, v_f))
        rounded, mid = rounded_f.bitcast(BF16), mid_f[0:D].bitcast(BF16)
        aggc, z_f, zr_f, zT3 = uT, r1, zT, hT
        zr = zr_f.rearrange("p (c f) -> p c f", c=C7)

        def nf(i):
            return bass.ds(i * NF, NF)

        def ncol(i):
            return bass.ds(i * NC, NC)

        def halves():
            return [(0, 512), (512, NC)]

        def chunk(c, n=P):
            return slice(c * n, (c + 1) * n)

        block = ctx.enter_context(nc.Block())

        @block.sync
        def _(sp):
            sp.dma_start(W[:, :], pack_in).then_inc(s_load, 16)
            sp.dma_start(x_nm[:, :], x_in).then_inc(s_load, 16)
            sp.dma_start(src_idx[:, 0:NT], src_in).then_inc(s_load, 16)
            sp.dma_start(base[:, :], dst_in[0:1, :]).then_inc(s_load, 16)
            for k, a in enumerate((dst_in, next_in, dstrow_in, prevrow_in, dst_in[0:1, :].to_broadcast([P, NT]))):
                sp.dma_start(agg[:, k * NT:(k + 1) * NT].bitcast(I32), a).then_inc(s_load, 16)
            sp.wait_ge(s_mask, 1)
            sp.dma_start(mask_dram[0, :].rearrange("(c q e) -> q c e", q=P, e=P),
                         big[:, 0:NT // 2].bitcast(BF16).rearrange("q (c e) -> q c e", e=P)).then_inc(s_mask, 16)
            sp.wait_ge(s_mask, 17)
            barrier(sp, "sp")

            def store_loop(lp, what, src, dst, n):
                with sp.Fori(0, NLOOP) as i:
                    lp.after(sp, i, what)
                    sp.dma_start(dst[:, bass.ds(i * n, n)], src).then_inc(s_tab[lp], 16)
                    sp.wait_ge(s_tab[lp], i * 16 + 16)
                    sp.sem_inc(lp.sem["sp"], 1)
                barrier(sp, "sp")

            s_tab = {lp: sem(f"rows_stored{n}") for n, lp in enumerate((A, B, C, Dl, El, Fl, Gl))}
            for lp in s_tab:
                lp.start(sp, "sp")
            store_loop(A, "dve.tab", tb_f, table_nm[0], NF)

            with sp.Fori(0, NIT) as i:
                for h in range(2):
                    sp.wait_ge(PL0.summed, i * U + (h + 1) * HALF)
                    sp.dma_start(ea_f[:, h * HALF * D:(h + 1) * HALF * D],
                                 ea_in[bass.ds((i * 2 + h) * P, P), :]).then_inc(ea_in_sem[h], 16)
                    sp.dma_start(ef[0:16, h, :], ef_in[:, bass.ds((i * 2 + h) * HALF * P, HALF * P)]
                                 ).then_inc(ef_in_sem[h], 16)
                    sp.wait_ge(ew_sb, i * 2 + h + 3)
                    sp.dma_start(ew_dram[bass.ds((i * 2 + h) * P, P), :], ews[:, h, :]).then_inc(ew_stored, 16)
                    sp.wait_ge(ew_stored, i * 32 + h * 16 + 16)
                    sp.sem_inc(ew_free, 1)
            barrier(sp, "sp")
            store_loop(B, "act.tab", tb_f, table_nm[1], NF)

            with sp.Fori(0, NIT) as i:
                for h in range(2):
                    sp.wait_ge(PL1.used, i * 4 + h * 2 + 2)
                    sp.dma_start(ewl[:, h, :], ew_dram[bass.ds((i * 2 + h) * P, P), :]).then_inc(ew_in_sem[h], 16)
            barrier(sp, "sp")
            store_loop(C, "act.tab", tb_f, table_nm[2], NF)

            with sp.Fori(0, NIT) as i:
                for h in range(2):
                    sp.wait_ge(scanned, i * 4 + h * 2 + 2)
                    sp.dma_start(mask[:, h, :], mask_dram[0:1, bass.ds((i * 2 + h) * HALF * P, HALF * P)]
                                 .to_broadcast([D, HALF * P])).then_inc(mask_in_sem[h], 16)
            barrier(sp, "sp")
            store_loop(Dl, "dve.h", hs_f, table_nm[3], NF)
            barrier(sp, "sp")
            store_loop(El, "act.z", zr_f, table_nm[4], NC)
            barrier(sp, "sp")
            store_loop(Fl, "act.tab", tb_f, table_nm[5], NF)
            barrier(sp, "sp")
            store_loop(Gl, "dve.x", xt_f, out, NF)

        @block.gpsimd
        def _(pool):
            pool.memset(src_idx[:, NT:NT + U], 0).then_inc(s_zero, 1)
            barrier(pool, "pool")
            pool.memset(agg[:, :], 0.0).then_inc(s_zero, 1)
            pool.wait_ge(s_zero, 2)
            barrier(pool, "pool")

            def node_copies(lp, consumer, x=True, h=False):
                lp.start(pool, "pool")
                with pool.Fori(0, NLOOP) as i:
                    lp.after(pool, i, consumer)
                    lp.done(pool.tensor_copy(agg[:, ncol(i)], w("zero").to_broadcast([P, NC])), "pool", "zero")
                    if x:
                        lp.after(pool, i, "dve.x")
                        lp.done(pool.tensor_copy(x_nm[:, nf(i)], xt_f), "pool", "x")
                    if h:
                        lp.after(pool, i, "dve.h", "act.hc")
                        lp.done(pool.tensor_copy(h_nm[:, nf(i)], hs_f), "pool", "h")
                barrier(pool, "pool")

            pool_gathers(pool, PL0, PL0.used, 1)
            barrier(pool, "pool")
            node_copies(B, "pe.U", h=True)
            pool_gathers(pool, PL1, PL1.used, 4)
            barrier(pool, "pool")
            node_copies(C, "pe.AG")
            pool_gathers(pool, PL2, PL2.used, 1)
            barrier(pool, "pool")
            node_copies(Dl, "act.aggc")
            pool_gathers(pool, PL3a, PL3a.used, 1)
            barrier(pool, "pool")
            node_copies(El, "act.aggc", x=False)
            pool_gathers(pool, PL3b, PL3b.used, 1)
            barrier(pool, "pool")
            node_copies(Fl, "act.aggc", x=False)
            pool_gathers(pool, PL3c, PL3c.used, 1)
            barrier(pool, "pool")
            barrier(pool, "pool")

        @block.scalar
        def _(act):
            def std(lp, i, pre=""):
                lp.after(act, i, f"dve.{pre}var")
                lp.done(act.activation(stat[:, 3], stat[:, 2], ACT.Sqrt), "act", pre + "std")

            def copy(lp, i, name, dst, src, *waits, func=ACT.Copy, **kw):
                lp.after(act, i, *waits)
                lp.done(act.activation(dst, src, func, **kw), "act", name)

            def sum_pass(ps):
                act_idx(act, ps, 0, 0)
                with act.Fori(0, NIT) as i:
                    act.wait_ge(ps.used, i * U + U)
                    act_idx(act, ps, i * U + HALF, 1)
                    act.wait_ge(ps.used, i * U + HALF + U)
                    act_idx(act, ps, i * U + U, 0)
                barrier(act, "act")

            barrier(act, "act")
            A.start(act, "act")
            with act.Fori(0, NLOOP) as i:
                std(A, i)
            barrier(act, "act")

            def store_terms(i, h):
                act.wait_ge(ew_mm, i * 2 + h + 1)
                act.wait_ge(ew_free, i * 2 + h + 1)
                act.activation(ews[:, h, :], bank(4 + h), ACT.Copy).then_inc(ew_sb, 1)

            act.sem_inc(ew_sb, 2)
            act_idx(act, PL0, 0, 0)
            with act.Fori(0, NIT) as i:
                act.wait_ge(PL0.used, i * U + U)
                act_idx(act, PL0, i * U + HALF, 1)
                store_terms(i, 0)
                act.wait_ge(PL0.used, i * U + HALF + U)
                act_idx(act, PL0, i * U + U, 0)
                store_terms(i, 1)
            barrier(act, "act")

            B.start(act, "act")
            with act.Fori(0, NLOOP) as i:
                copy(B, i, "hc", hc_f, h_nm[:, nf(i)], "pe.U<")
                copy(B, i, "uT", uT[0:D], bank(0, NC, rows=D), "pe.U", "pe.Z<")
                copy(B, i, "zT", zT, bank(2, NC), "pe.Z", "pe.O<", func=ACT.Relu, bias=w("b1"))
                std(B, i)
                copy(B, i, "hT", hT[0:D], bank(5, NC, rows=D), "pe.HT", "pe.APT<")
                copy(B, i, "tab", tb_f, bank(7, NF), "pe.TAB", "sp.stored<")
                copy(B, i, "high", part_hm[0:D, ncol(i)], bank(0, NC, rows=D), "pe.APT")
                copy(B, i, "rounded", rounded, bank(0, NC), "pe.APT", "dve.rest1<")
                copy(B, i, "mid", part_hm[D:P, ncol(i)], r1[D:P], "dve.rest1")
            barrier(act, "act")

            act.sem_inc(win_sb, 4)
            act.sem_inc(relued, 2)

            def win_copy(i, g):
                for j in range(4 * g, 4 * g + 4):
                    act.wait_ge(win_t, i * U + j + 1)
                    act.wait_ge(pre_mm, i * U + j + 1)
                    act.activation(win[:, j % 8, :], bank(j % 2, WIN), ACT.Copy).then_inc(win_sb, 1)

            def relu_sums(i, g):
                act.wait_ge(PL1.used, i * 4 + g + 5)
                act.wait_ge(PL1.summed, i * U + 4 * g + 4)
                act.activation(msg1[:, 4 * g:4 * g + 4, 0:D],
                               pre[:, g % 2, :].rearrange("p (t f) -> p t f", t=4), ACT.Relu).then_inc(relued, 1)

            act_idx(act, PL1, 0, 0)
            with act.Fori(0, NIT) as i:
                act.wait_ge(PL1.used, i * 4 + 4)
                act_idx(act, PL1, i * U + HALF, 1)
                win_copy(i, 0)
                win_copy(i, 1)
                relu_sums(i, 0)
                win_copy(i, 2)
                relu_sums(i, 1)
                act_idx(act, PL1, i * U + U, 0)
                win_copy(i, 3)
                relu_sums(i, 2)
                relu_sums(i, 3)
            barrier(act, "act")

            C.start(act, "act")
            with act.Fori(0, NLOOP) as i:
                copy(C, i, "hc", hc_f, h_nm[:, nf(i)], "pe.H1T<", "dve.v<")
                copy(C, i, "agT", uT[0:D + 1], bank(0, NC, rows=D + 1), "pe.AG", "pe.O<")
                copy(C, i, "h1T", r1[0:D], bank(2, NC, rows=D), "pe.H1T", "pe.RU<")
                copy(C, i, "rT", zT[0:D], bank(4, NC, rows=D), "pe.RU", "pe.O<", func=ACT.Relu, bias=w("bu1"))
                std(C, i, "v")
                std(C, i)
                copy(C, i, "hT", hT[0:D], bank(2, NC, rows=D), "pe.HT", "pe.PH<")
                copy(C, i, "tab", tb_f, bank(0, NF), "pe.TH", "sp.stored<", "dve.diff<")
            barrier(act, "act")

            def back_copy(i, g):
                act.wait_ge(back_t, i * 4 + g + 3)
                act.wait_ge(PL2.summed, i * U + 4 * g + 12)
                act.activation(back[:, g % 2, :], bank(4 + g % 2, 4 * D), ACT.Copy).then_inc(back_sb, 1)

            act.sem_inc(back_sb, 2)
            act_idx(act, PL2, 0, 0)
            with act.Fori(0, NIT) as i:
                act.wait_ge(PL2.used, i * U + U)
                act_idx(act, PL2, i * U + HALF, 1)
                back_copy(i, 0)
                back_copy(i, 1)
                act_idx(act, PL2, i * U + U, 0)
                back_copy(i, 2)
                back_copy(i, 3)
            barrier(act, "act")

            Dl.start(act, "act")
            with act.Fori(0, NLOOP) as i:
                copy(Dl, i, "aggc", aggc[0:D], agg[0:D, ncol(i)], "pe.T<")
                std(Dl, i)
                copy(Dl, i, "hT", hT[0:D], bank(2, NC, rows=D), "pe.HT", "pe.SELF<")
                copy(Dl, i, "self", big[:, ncol(i)], bank(4, NC), "pe.SELF")
            barrier(act, "act")
            sum_pass(PL3a)

            El.start(act, "act")
            with act.Fori(0, NLOOP) as i:
                copy(El, i, "aggc", aggc[0:D], agg[0:D, ncol(i)], "pe.M<")
                copy(El, i, "z", zr_f, z_f, "dve.sum", "pe.ZT<", "sp.stored<", func=ACT.Relu)
                copy(El, i, "zT", zT3, bank(2, NC), "pe.ZT", "pe.SELF<")
                copy(El, i, "self", big[:, ncol(i)], bank(4, NC), "pe.SELF")
            barrier(act, "act")
            sum_pass(PL3b)

            Fl.start(act, "act")
            with act.Fori(0, NLOOP) as i:
                copy(Fl, i, "aggc", aggc, agg[:, ncol(i)], "pe.M<")
                copy(Fl, i, "z", zr_f, z_f, "dve.sum", "pe.ZT<", func=ACT.Relu)
                copy(Fl, i, "zT", zT3, bank(2, NC), "pe.ZT", "pe.SELF<")
                copy(Fl, i, "tab", tb_f, bank(4, NF), "pe.PROJ", "sp.stored<")
                copy(Fl, i, "self", h_nm[:, nf(i)], bank(5, NF), "pe.SELF")
            barrier(act, "act")
            sum_pass(PL3c)

            Gl.start(act, "act")
            with act.Fori(0, NLOOP) as i:
                copy(Gl, i, "aggc", aggc[0:D], agg[0:D, ncol(i)], "pe.T<")
            barrier(act, "act")

        @block.vector
        def _(dve):
            count = [0]

            def setup(ins):
                count[0] += 1
                ins.then_inc(s_setup, 1)
                dve.wait_ge(s_setup, count[0])

            def chain(lp, i, name, ins):
                lp.done(ins, "dve", name)
                lp.after(dve, i, "dve." + name)

            def norm(lp, i, src, dst, pre=""):
                mean, rstd = stat[:, 0], stat[:, 1]

                def link(name, ins):
                    chain(lp, i, pre + name, ins)

                link("sum", dve.reduce_sum(mean, src, AX.X))
                link("mean", dve.tensor_scalar(mean, mean, 1.0 / D, None, ALU.mult))
                link("centred", dve.tensor_tensor(xc, src, mean.to_broadcast([P, C7, D]), ALU.subtract))
                link("squared", dve.tensor_tensor(sq, xc, xc, ALU.mult))
                link("sumsq", dve.reduce_sum(rstd, sq, AX.X))
                link("var", dve.tensor_scalar(stat[:, 2], rstd, 1.0 / D, LN_EPS, ALU.mult, ALU.add))
                lp.after(dve, i, f"act.{pre}std")
                link("rstd", dve.reciprocal(rstd, stat[:, 3]))
                link("normed", dve.tensor_tensor(dst, xc, rstd.to_broadcast([P, C7, D]), ALU.mult))

            dve.wait_ge(s_load, 9 * 16)
            dst, nxt, dstrow, prevrow, base_b = (agg[:, k * NT:(k + 1) * NT].bitcast(I32) for k in range(5))
            f0, f1 = agg[:, 5 * NT:6 * NT], agg[:, 6 * NT:7 * NT]
            rel_f, m_f = big[:, NT:2 * NT], big[:, 2 * NT:3 * NT]
            hi_i, lo_i = f0.bitcast(I32), f1.bitcast(I32)
            setup(dve.tensor_scalar(hi_i, src_idx[:, 0:NT], 7, None, ALU.logical_shift_right))
            setup(dve.tensor_scalar(lo_i, src_idx[:, 0:NT], P - 1, None, ALU.bitwise_and))
            setup(dve.scalar_tensor_tensor(out=src_idx[:, 0:NT], in0=lo_i, scalar=float(CHUNKS), in1=hi_i,
                                           op0=ALU.mult, op1=ALU.add))
            setup(dve.tensor_tensor(rel_f, dst, base_b, ALU.subtract))
            setup(dve.tensor_copy(rel[:, :], rel_f))
            setup(dve.tensor_tensor(m_f, dst, nxt, ALU.not_equal))
            setup(dve.scalar_tensor_tensor(out=rel_f, in0=rel_f, scalar=1.0, in1=m_f, op0=ALU.add, op1=ALU.mult))
            setup(dve.tensor_scalar(rel_end[:, :], rel_f, -1.0, None, ALU.add))
            setup(dve.tensor_tensor(m_f, dstrow, prevrow, ALU.is_equal))
            setup(dve.tensor_scalar(m_f, m_f, -0.5, 3.3895313892515355e38, ALU.add, ALU.mult))
            dve.tensor_scalar(big[:, 0:NT // 2].bitcast(BF16), m_f, 2.0, None, ALU.mult).then_inc(s_mask, 1)
            setup(dve.tensor_copy(ident_b[:, :], w("ident")))
            setup(dve.tensor_scalar(stat[:, 0, 0], w("eps"), 1.0, None, ALU.add))
            setup(dve.tensor_scalar(ident_e[:, :], w("ident"), stat[:, 0, 0], None, ALU.mult))
            barrier(dve, "dve")

            bias = w("we_b").rearrange("p (c f) -> p c f", c=1).to_broadcast([P, C7, D])
            A.start(dve, "dve")
            with dve.Fori(0, NLOOP) as i:
                norm(A, i, n3(x_nm[:, nf(i)]), hs)
                chain(A, i, "h", dve.tensor_scalar(h_nm[:, nf(i)], hs_f, 0.0, None, ALU.max))
                A.after(dve, i, "sp.stored<")
                chain(A, i, "tab", dve.tensor_tensor(tb, n3(h_nm[:, nf(i)]), bias, ALU.add))
            setup(dve.memset(ef_f[:, :], 1.0))
            barrier(dve, "dve")

            def sum_pass(ps):
                dve.sem_inc(ps.added, 4)
                with dve.Fori(0, NIT) as i:
                    b = dve_bases(i)
                    dve_s(dve, ps, i, rel)
                    dve_add(dve, ps, b, i, range(U))
                barrier(dve, "dve")

            sum_pass(PL0)

            setup(dve.memset(part_hm[:, ROWS:COLS], 0.0))
            setup(dve.memset(part_lo[:, ROWS:COLS], 0.0))
            B.start(dve, "dve")
            with dve.Fori(0, NLOOP) as i:
                B.after(dve, i, "pe.O", "pool.x<")
                chain(B, i, "x", dve.tensor_tensor(xt_f, bank(4, NF), x_nm[:, nf(i)], ALU.add))
                B.after(dve, i, "pe.HT<", "pool.h<")
                norm(B, i, xt, hs)
                chain(B, i, "h", dve.tensor_scalar(hs_f, hs_f, 0.0, None, ALU.max))
                B.after(dve, i, "act.rounded", "act.mid<")
                chain(B, i, "rest1", dve.tensor_tensor(r1, bank(0, NC), rounded, ALU.subtract))
                chain(B, i, "mid", dve.tensor_copy(mid, r1[0:D]))
                chain(B, i, "lo", dve.tensor_tensor(part_lo[:, ncol(i)], r1[0:D], mid, ALU.subtract))
            barrier(dve, "dve")

            setup(dve.memset(msg1[:, :, D:D + 1], 1.0))
            dve.sem_inc(PL1.added, 4)
            dve.sem_inc(PL1.used, 4)

            def edge_sums(i, g):
                dve.wait_ge(pre_mm, i * U + 4 * g + 4 + 8)
                dve.wait_ge(relued, i * 4 + g + 1)
                if g % 2 == 0:
                    dve.wait_ge(ew_in_sem[g // 2], i * 16 + 16)
                dve.tensor_tensor(pre[:, g % 2, :], bank(4 + g % 2, 4 * D),
                                  ewl[:, g // 2, (g % 2) * 4 * D:(g % 2 + 1) * 4 * D], ALU.add).then_inc(pre_ew, 1)
                dve.wait_ge(pre_ew, i * 4 + g + 1)
                for j in range(4 * g, 4 * g + 4):
                    tile_landed(dve, PL1, i, j)
                dve.tensor_tensor(pre[:, g % 2, :], pre[:, g % 2, :],
                                  msg_f[:, 4 * g * D:4 * (g + 1) * D], ALU.add).then_inc(PL1.used, 1)

            with dve.Fori(0, NIT) as i:
                b = dve_bases(i)
                dve_s(dve, PL1, i, rel)
                edge_sums(i, 0)
                edge_sums(i, 1)
                dve_add(dve, PL1, b, i, range(0, 4))
                edge_sums(i, 2)
                dve_add(dve, PL1, b, i, range(4, 8))
                edge_sums(i, 3)
                dve_add(dve, PL1, b, i, range(8, 16))
            barrier(dve, "dve")

            setup(dve.memset(zT[D:D + 1], 1.0))
            setup(dve.memset(hT[D:D + 1], 1.0))
            C.start(dve, "dve")
            gamma = w("gamma").rearrange("p (c f) -> p c f", c=1).to_broadcast([P, C7, D])
            beta = w("beta").rearrange("p (c f) -> p c f", c=1).to_broadcast([P, C7, D])
            with dve.Fori(0, NLOOP) as i:
                C.after(dve, i, "pe.O", "act.hc")
                chain(C, i, "deg", dve.tensor_copy(deg[:, bass.ds(i * C7, C7)], bank(7, C7)))
                chain(C, i, "v", dve.tensor_tensor(vv, n3(bank(6, NF)), hc, ALU.add))
                norm(C, i, vv, vv, "v")
                chain(C, i, "scaled", dve.tensor_tensor(vv, vv, gamma, ALU.mult))
                chain(C, i, "shifted", dve.tensor_tensor(vv, vv, beta, ALU.add))
                C.after(dve, i, "pool.x<")
                chain(C, i, "x", dve.tensor_tensor(xt_f, v_f, x_nm[:, nf(i)], ALU.add))
                C.after(dve, i, "pe.HT<")
                norm(C, i, xt, hs)
                chain(C, i, "h", dve.tensor_scalar(hs_f, hs_f, 0.0, None, ALU.max))
                C.after(dve, i, "pe.PH", "act.tab")
                chain(C, i, "diff", dve.tensor_tensor(h_nm[:, nf(i)], bank(1, NF), tb_f, ALU.subtract))
            setup(dve.tensor_scalar(rdeg[:, :, 0], deg[:, :], 1.0, None, ALU.max))
            setup(dve.reciprocal(rdeg[:, :, 0], rdeg[:, :, 0]))
            setup(dve.tensor_scalar(has_in[:, :, 0], deg[:, :], 1.0, None, ALU.min))
            barrier(dve, "dve")

            setup(dve.memset(run[:, 1, :], 0.0))
            dve.sem_inc(PL2.added, 4)
            dve.sem_inc(scanned, 4)

            def scan(i, g):
                dve.wait_ge(PL2.used, i * U + 4 * g + 4 + U)
                dve.wait_ge(back_t, i * 4 + g + 1)
                dve.wait_ge(scanned, i * 4 + g + 4)
                if g % 2 == 0:
                    dve.wait_ge(mask_in_sem[g // 2], i * 16 + 16)
                dve.tensor_tensor_scan(out=run[:, g % 2, :], data0=mask[:, g // 2, (g % 2) * 4 * P:(g % 2 + 1) * 4 * P],
                                       data1=bank(g % 2, 4 * P, rows=D), initial=run[:, (g + 1) % 2, 4 * P - 1:4 * P],
                                       op0=ALU.min, op1=ALU.max).then_inc(scanned, 1)

            with dve.Fori(0, NIT) as i:
                b = dve_bases(i)
                dve_s(dve, PL2, i, rel_end)
                scan(i, 0)
                scan(i, 1)
                dve_add(dve, PL2, b, i, range(0, 4))
                scan(i, 2)
                dve_add(dve, PL2, b, i, range(4, 8))
                scan(i, 3)
                dve_add(dve, PL2, b, i, range(8, 16))
            barrier(dve, "dve")

            setup(dve.memset(hT[D:D + 1], 1.0))
            Dl.start(dve, "dve")
            with dve.Fori(0, NLOOP) as i:
                Dl.after(dve, i, "pe.T")
                chain(Dl, i, "y", dve.tensor_tensor(v_f, bank(0, NF), h_nm[:, nf(i)], ALU.add))
                chain(Dl, i, "times0", dve.tensor_scalar(xc_f, v_f, 0.0, None, ALU.mult))
                chain(Dl, i, "finite", dve.tensor_scalar(xc_f, xc_f, 0.0, None, ALU.is_equal))
                chain(Dl, i, "keep", dve.tensor_tensor(
                    xc, xc, has_in[:, bass.ds(i * C7, C7), :].to_broadcast([P, C7, D]), ALU.mult))
                chain(Dl, i, "zero", dve.memset(sq_f, 0.0))
                hold(dve)
                chain(Dl, i, "y0", dve.copy_predicated(sq_f, xc_f.bitcast(I32), v_f))
                Dl.after(dve, i, "pool.x<")
                chain(Dl, i, "x", dve.tensor_tensor(xt_f, sq_f, x_nm[:, nf(i)], ALU.add))
                Dl.after(dve, i, "pe.HT<", "sp.stored<")
                norm(Dl, i, xt, hs)
                chain(Dl, i, "h", dve.tensor_scalar(hs_f, hs_f, 0.0, None, ALU.max))
            barrier(dve, "dve")

            def mean_and_self(lp, i):
                lp.after(dve, i, "pe.M", "act.z<")
                chain(lp, i, "mean", dve.tensor_tensor(
                    z_f.rearrange("p (c f) -> p c f", c=C7), bank(0, NC).rearrange("p (c f) -> p c f", c=C7),
                    rdeg[:, bass.ds(i * C7, C7), :].to_broadcast([P, C7, H]), ALU.mult))
                chain(lp, i, "sum", dve.tensor_tensor(z_f, z_f, big[:, ncol(i)], ALU.add))

            sum_pass(PL3a)
            El.start(dve, "dve")
            with dve.Fori(0, NLOOP) as i:
                mean_and_self(El, i)
            barrier(dve, "dve")
            sum_pass(PL3b)
            Fl.start(dve, "dve")
            with dve.Fori(0, NLOOP) as i:
                mean_and_self(Fl, i)
            barrier(dve, "dve")
            sum_pass(PL3c)
            Gl.start(dve, "dve")
            with dve.Fori(0, NLOOP) as i:
                Gl.after(dve, i, "pe.T")
                chain(Gl, i, "mean", dve.tensor_tensor(
                    vv, n3(bank(0, NF)), rdeg[:, bass.ds(i * C7, C7), :].to_broadcast([P, C7, D]), ALU.mult))
                chain(Gl, i, "sum", dve.tensor_tensor(v_f, v_f, h_nm[:, nf(i)], ALU.add))
                chain(Gl, i, "relu", dve.tensor_scalar(v_f, v_f, 0.0, None, ALU.max))
                Gl.after(dve, i, "sp.stored<")
                chain(Gl, i, "x", dve.tensor_tensor(xt_f, v_f, x_nm[:, nf(i)], ALU.add))
            barrier(dve, "dve")

        @block.tensor
        def _(pe):
            def mm(out_, lhsT, rhs, start=True, stop=True):
                return pe.matmul(out_, lhsT, rhs, start=start, stop=stop)

            def transposes(dst_bank, src3, rows_in, cols_in):
                hold(pe)
                for c in range(C7):
                    last = pe.transpose(bank(dst_bank, rows_in, c * rows_in, cols_in), src3(c),
                                        w("ident")[0:rows_in, 0:rows_in])
                return last

            barrier(pe, "pe")
            barrier(pe, "pe")

            def sum_tiles(ps, i, js, message, waits=None):
                for j in js:
                    if waits:
                        waits(j)
                    pe.wait_ge(ps.s_ready, i * U + j + 1)
                    pe.wait_ge(ps.added, i * U + j + 1)
                    mm(acc_slot(j, ps.rows), message(j), S[:, j, :]).then_inc(ps.summed, 1)

            pe.sem_inc(PL0.summed, U)
            pe.sem_inc(ew_free, 2)
            with pe.Fori(0, NIT) as i:
                for h in range(2):
                    pe.wait_ge(ef_in_sem[h], i * 16 + 16)
                    pe.wait_ge(ew_sb, i * 2 + h + 1)
                    for t in range(HALF):
                        last = mm(bank(4 + h, D, t * D), ef[0:17, h, t * P:(t + 1) * P], w("wc"))
                    last.then_inc(ew_mm, 1)
                    pe.wait_ge(ea_in_sem[h], i * 16 + 16)
                    for j in range(h * HALF, (h + 1) * HALF):
                        pe.wait_ge(PL0.s_ready, i * U + j + 1)
                        pe.wait_ge(PL0.added, i * U + j + 1)
                        mm(acc_slot(j, P)[D:P], ea[:, j, :], S[:, j, :])
                        tile_landed(pe, PL0, i, j)
                        mm(acc_slot(j, P)[0:D], PL0.msg[:, j, :], S[:, j, :]).then_inc(PL0.summed, 1)
            barrier(pe, "pe")

            B.start(pe, "pe")
            with pe.Fori(0, NLOOP) as i:
                B.after(pe, i, "act.hc", "act.rounded<", "act.high<", "dve.rest1<")
                for c in range(C7):
                    mm(bank(0, P, c * P, D), w("we"), agg[:, bass.ds(i * NC + c * P, P)], stop=False)
                    last = mm(bank(0, P, c * P, D), hc[:, c, :], ident_e[:, :], start=False)
                B.done(last, "pe", "U")
                B.after(pe, i, "act.uT", "act.zT<")
                for a, b in halves():
                    last = mm(bank(2, b - a, a), w("w1"), uT[0:D, a:b])
                B.done(last, "pe", "Z")
                B.after(pe, i, "act.zT", "dve.x<")
                for c in range(C7):
                    mm(bank(4, D, c * D), zT[:, chunk(c)], w("w2"), stop=False)
                    last = mm(bank(4, D, c * D), w("ones"), w("b2"), start=False)
                B.done(last, "pe", "O")
                B.after(pe, i, "dve.h", "act.hT<")
                B.done(transposes(5, lambda c: hs[:, c, :], P, D), "pe", "HT")
                B.after(pe, i, "act.hT", "act.tab<")
                hold(pe)
                for c in range(C7):
                    last = mm(bank(7, D, c * D), hT[0:D, chunk(c)], w("wb"))
                B.done(last, "pe", "TAB")
                B.after(pe, i, "act.uT")
                for a, b in halves():
                    last = mm(bank(0, b - a, a), w("wa2"), hT[0:D, a:b])
                B.done(last, "pe", "APT")
            barrier(pe, "pe")

            pe.sem_inc(PL1.summed, U)
            pe.sem_inc(pre_mm, 8)

            def windows(i, b, g):
                for j in range(4 * g, 4 * g + 4):
                    pe.wait_ge(PL1.s_ready, i * U + j + 1)
                    pe.wait_ge(win_sb, i * U + j + 3)
                    at = bass.ds(b[j], P)
                    mm(bank(j % 2, P), part_hm[:, at], ident_b[:, :])
                    mm(bank(j % 2, D, P), part_lo[:, at], ident_b[0:D, 0:D])
                    pe.transpose(bank(j % 2, P, 3 * D), S[:, j, :], w("ident")).then_inc(win_t, 1)

            def dst_terms(i, g):
                pe.wait_ge(PL1.used, i * 4 + g + 3)
                for j in range(4 * g, 4 * g + 4):
                    pe.wait_ge(win_sb, i * U + j + 5)
                    for k in range(3):
                        last = mm(bank(4 + g % 2, D, j % 4 * D), win[:, j % 8, 3 * D:WIN],
                                  win[:, j % 8, k * D:(k + 1) * D], start=k == 0, stop=k == 2)
                    last.then_inc(pre_mm, 1)

            def sums1(i, g):
                pe.wait_ge(relued, i * 4 + g + 3)
                sum_tiles(PL1, i, range(4 * g, 4 * g + 4), lambda j: msg1[:, j, :])

            with pe.Fori(0, NIT) as i:
                _, b = nc.values_load_multi_w_load_instructions(
                    base[0:1, bass.ds(i * U, U)], engines=[mybir.EngineType.PE], min_val=0, max_val=N,
                    skip_runtime_bounds_check_because="dst holds node numbers below N, the padding N")
                windows(i, b, 0)
                windows(i, b, 1)
                dst_terms(i, 0)
                windows(i, b, 2)
                dst_terms(i, 1)
                sums1(i, 0)
                windows(i, b, 3)
                dst_terms(i, 2)
                sums1(i, 1)
                dst_terms(i, 3)
                sums1(i, 2)
                sums1(i, 3)
            barrier(pe, "pe")

            C.start(pe, "pe")
            with pe.Fori(0, NLOOP) as i:
                C.after(pe, i, "act.tab<", "dve.diff<")
                for a, b in halves():
                    last = mm(bank(0, b - a, a, D + 1), w("wm2"), agg[0:D + 1, bass.ds(i * NC + a, b - a)])
                C.done(last, "pe", "AG")
                C.after(pe, i, "act.hc", "act.hT<")
                C.done(transposes(2, lambda c: hc[:, c, :], P, D), "pe", "H1T")
                C.after(pe, i, "act.agT", "act.h1T", "act.rT<")
                hold(pe)
                for a, b in halves():
                    mm(bank(4, b - a, a, D), w("wu1a"), r1[0:D, a:b], stop=False)
                    last = mm(bank(4, b - a, a, D), w("wu1b"), uT[0:D, a:b], start=False)
                C.done(last, "pe", "RU")
                C.after(pe, i, "act.rT", "dve.v<")
                for c in range(C7):
                    mm(bank(7, 1, c), uT[0:D + 1, chunk(c)], w("e64"))
                    last = mm(bank(6, D, c * D), zT[0:D + 1, chunk(c)], w("wu2"))
                C.done(last, "pe", "O")
                C.after(pe, i, "dve.h", "act.h1T")
                C.done(transposes(2, lambda c: hs[:, c, :], P, D), "pe", "HT")
                C.after(pe, i, "act.hT")
                for c in range(C7):
                    last = mm(bank(0, D, c * D), hT[0:D + 1, chunk(c)], w("theta"))
                C.done(last, "pe", "TH")
                for c in range(C7):
                    last = mm(bank(1, D, c * D), hT[0:D + 1, chunk(c)], w("phi"))
                C.done(last, "pe", "PH")
            barrier(pe, "pe")

            pe.sem_inc(PL2.used, U)
            pe.sem_inc(PL2.summed, U)
            pe.sem_inc(back_t, 2)

            def forth(i, g):
                pe.wait_ge(scanned, i * 4 + g + 3)
                for j in range(4 * g, 4 * g + 4):
                    tile_landed(pe, PL2, i, j)
                    hold(pe)
                    pe.transpose(bank(g % 2, P, j % 4 * P, D), PL2.msg[:, j, :], w("ident")).then_inc(PL2.used, 1)

            def back_and_sums(i, g):
                pe.wait_ge(scanned, i * 4 + g + 5)
                pe.wait_ge(back_sb, i * 4 + g + 1)
                hold(pe)
                for j in range(4):
                    last = pe.transpose(bank(4 + g % 2, D, j * D), run[:, g % 2, j * P:(j + 1) * P],
                                        w("ident")[0:D, 0:D])
                last.then_inc(back_t, 1)
                pe.wait_ge(back_sb, i * 4 + g + 3)
                sum_tiles(PL2, i, range(4 * g, 4 * g + 4), lambda j: back[:, g % 2, j % 4 * D:(j % 4 + 1) * D])

            with pe.Fori(0, NIT) as i:
                forth(i, 0)
                forth(i, 1)
                back_and_sums(i, 0)
                forth(i, 2)
                back_and_sums(i, 1)
                forth(i, 3)
                back_and_sums(i, 2)
                back_and_sums(i, 3)
            barrier(pe, "pe")

            Dl.start(pe, "pe")
            with pe.Fori(0, NLOOP) as i:
                Dl.after(pe, i, "act.aggc", "dve.y<")
                hold(pe)
                for c in range(C7):
                    last = pe.transpose(bank(0, D, c * D), aggc[0:D, chunk(c)], w("ident")[0:D, 0:D])
                Dl.done(last, "pe", "T")
                Dl.after(pe, i, "dve.h", "act.hT<")
                Dl.done(transposes(2, lambda c: hs[:, c, :], P, D), "pe", "HT")
                Dl.after(pe, i, "act.hT", "act.self<")
                for c in range(C7):
                    last = mm(bank(4, H, c * H), hT[0:D + 1, chunk(c)], w("ws0"))
                Dl.done(last, "pe", "SELF")
            barrier(pe, "pe")

            def sage_pass(ps):
                pe.sem_inc(ps.summed, U)
                with pe.Fori(0, NIT) as i:
                    sum_tiles(ps, i, range(U), lambda j: ps.msg[:, j, :], waits=lambda j: tile_landed(pe, ps, i, j))
                barrier(pe, "pe")

            sage_pass(PL3a)
            El.start(pe, "pe")
            with pe.Fori(0, NLOOP) as i:
                El.after(pe, i, "act.aggc", "dve.mean<")
                for c in range(C7):
                    last = mm(bank(0, H, c * H), aggc[0:D, chunk(c)], w("wn0"))
                El.done(last, "pe", "M")
                El.after(pe, i, "act.z", "act.zT<")
                El.done(transposes(2, lambda c: zr[:, c, :], P, H), "pe", "ZT")
                El.after(pe, i, "act.zT", "act.self<")
                for c in range(C7):
                    mm(bank(4, H, c * H), zT3[:, chunk(c)], w("ws1"), stop=False)
                    last = mm(bank(4, H, c * H), w("ones"), w("sb1"), start=False)
                El.done(last, "pe", "SELF")
            barrier(pe, "pe")

            sage_pass(PL3b)
            Fl.start(pe, "pe")
            with pe.Fori(0, NLOOP) as i:
                Fl.after(pe, i, "act.aggc", "dve.mean<")
                for c in range(C7):
                    last = mm(bank(0, H, c * H), aggc[:, chunk(c)], w("wn1"))
                Fl.done(last, "pe", "M")
                Fl.after(pe, i, "act.z", "act.zT<")
                Fl.done(transposes(2, lambda c: zr[:, c, :], P, H), "pe", "ZT")
                Fl.after(pe, i, "act.zT", "act.tab<")
                for c in range(C7):
                    last = mm(bank(4, D, c * D), zT3[:, chunk(c)], w("wn2"))
                Fl.done(last, "pe", "PROJ")
                Fl.after(pe, i, "act.self<")
                for c in range(C7):
                    mm(bank(5, D, c * D), zT3[:, chunk(c)], w("ws2"), stop=False)
                    last = mm(bank(5, D, c * D), w("ones"), w("sb2"), start=False)
                Fl.done(last, "pe", "SELF")
            barrier(pe, "pe")

            sage_pass(PL3c)
            Gl.start(pe, "pe")
            with pe.Fori(0, NLOOP) as i:
                Gl.after(pe, i, "act.aggc", "dve.mean<")
                hold(pe)
                for c in range(C7):
                    last = pe.transpose(bank(0, D, c * D), aggc[0:D, chunk(c)], w("ident")[0:D, 0:D])
                Gl.done(last, "pe", "T")
            barrier(pe, "pe")


def kernel(x, src, dst, edge_attr_16, edge_attr_64, L0_gnn_We_w, L0_gnn_We_b, L0_gnn_eps, L0_gnn_W1, L0_gnn_b1,
           L0_gnn_W2, L0_gnn_b2, L1_gnn_W_m1, L1_gnn_b_m1, L1_gnn_W_m2, L1_gnn_b_m2, L1_gnn_W_u1, L1_gnn_b_u1,
           L1_gnn_W_u2, L1_gnn_b_u2, L1_gnn_gamma, L1_gnn_beta, L2_gnn_theta_w, L2_gnn_theta_b, L2_gnn_phi_w,
           L2_gnn_phi_b, L3_gnn_ws0, L3_gnn_wn0, L3_gnn_b0, L3_gnn_ws1, L3_gnn_wn1, L3_gnn_b1, L3_gnn_ws2,
           L3_gnn_wn2, L3_gnn_b2):
    import concourse.bacc as bacc
    from concourse.bass_utils import run_bass_kernel_spmd

    a = np.asarray
    pad = NT * P - E

    def tiles(v):
        return np.ascontiguousarray(v.reshape(NT, P).T)

    def rows(v):
        return np.ascontiguousarray(v.reshape(NT // P, P, P).transpose(1, 0, 2).reshape(P, NT))

    src_p = np.pad(a(src), (0, pad))
    dst_p = np.pad(a(dst), (0, pad), constant_values=N)
    next_p = np.concatenate([dst_p[1:], np.full(1, -1, dst_p.dtype)])
    prev_p = np.concatenate([np.full(1, -1, dst_p.dtype), dst_p[:-1]])
    x_p = np.pad(a(x), ((0, ROWS - N), (0, 0))).reshape(CHUNKS, P, D).transpose(1, 0, 2).reshape(P, CHUNKS * D)
    ea_p = np.pad(a(edge_attr_64), ((0, pad), (0, 0))).reshape(NT // HALF, HALF, P, D).transpose(0, 2, 1, 3)
    ef_p = np.pad(a(edge_attr_16), ((0, pad), (0, 0))).T

    eye = np.eye(P, dtype=np.float32)
    row = lambda v: a(v).reshape(1, -1)
    col = lambda v: a(v).reshape(-1, 1)
    every = lambda v, c: np.broadcast_to(a(v).reshape(1, -1), (P, c))
    wm1 = a(L1_gnn_W_m1)
    wm2 = np.zeros((D + 1, D + 1), np.float32)
    wm2[0:D, 0:D], wm2[D, 0:D], wm2[D, D] = a(L1_gnn_W_m2), a(L1_gnn_b_m2), 1.0
    parts = dict(
        ident=eye, iota=np.broadcast_to(np.arange(P, dtype=np.float32), (P, P)),
        we=np.concatenate([eye[0:D, 0:D], a(L0_gnn_We_w)]), w1=a(L0_gnn_W1), b1=col(L0_gnn_b1), w2=a(L0_gnn_W2),
        b2=row(L0_gnn_b2), ones=np.ones((1, P), np.float32), we_b=every(L0_gnn_We_b, D), eps=every(L0_gnn_eps, 1),
        wa2=np.concatenate([wm1[0:D], wm1[0:D]], axis=1), wb=wm1[D:2 * D],
        wc=np.concatenate([wm1[2 * D:], row(L1_gnn_b_m1)]), wm2=wm2,
        wu1a=a(L1_gnn_W_u1)[0:D], wu1b=a(L1_gnn_W_u1)[D:], bu1=col(L1_gnn_b_u1),
        wu2=np.concatenate([a(L1_gnn_W_u2), row(L1_gnn_b_u2)]), e64=eye[0:D + 1, D:D + 1],
        gamma=every(L1_gnn_gamma, D), beta=every(L1_gnn_beta, D),
        theta=np.concatenate([a(L2_gnn_theta_w).T, row(L2_gnn_theta_b)]),
        phi=np.concatenate([a(L2_gnn_phi_w).T, row(L2_gnn_phi_b)]),
        ws0=np.concatenate([a(L3_gnn_ws0), row(L3_gnn_b0)]), wn0=a(L3_gnn_wn0), ws1=a(L3_gnn_ws1),
        sb1=row(L3_gnn_b1), wn1=a(L3_gnn_wn1), wn2=a(L3_gnn_wn2), ws2=a(L3_gnn_ws2), sb2=row(L3_gnn_b2), zero=np.zeros((P, 1), np.float32))
    pack = np.zeros((P, WCOLS), np.float32)
    for name, (r, c) in PACK.items():
        pack[0:r, AT[name]:AT[name] + c] = parts[name]

    arrays = dict(x_nm_in=np.ascontiguousarray(x_p), src_in=tiles(src_p), dst_in=tiles(dst_p),
                  next_in=tiles(next_p), dstrow_in=rows(dst_p), prevrow_in=rows(prev_p),
                  ea_in=np.ascontiguousarray(ea_p.reshape(NT // HALF * P, HALF * D)),
                  ef_in=np.ascontiguousarray(ef_p), pack_in=pack)
    nc = bacc.Bacc("TRN2", target_bir_lowering=False, num_devices=1)
    args = [nc.dram_tensor(n, v.shape, mybir.dt.from_np(v.dtype), kind="ExternalInput").ap()
            for n, v in arrays.items()]
    out = nc.dram_tensor("x_out", (P, CHUNKS * D), F32, kind="ExternalOutput").ap()
    gnn(nc, *args, out)
    r = run_bass_kernel_spmd(nc, [arrays], core_ids=[0])
    y = np.asarray(r.results[0]["x_out"]).reshape(P, CHUNKS, D).transpose(1, 0, 2).reshape(ROWS, D)
    return np.ascontiguousarray(y[0:N])
```

```python
import numpy as np
import concourse.bass as bass
from concourse import mybir
from contextlib import ExitStack

N = 12500
E = 212500
D = 64
H = 128
P = 128
LN_EPS = 1e-5

U = 16
HALF = U // 2
NT = -(-E // (P * U)) * U
NIT = NT // U
CHUNKS = -(-N // P)
ROWS = CHUNKS * P
COLS = ROWS + P
C7 = 7
NLOOP = CHUNKS // C7
NC = C7 * P
NF = C7 * D
assert C7 * NLOOP == CHUNKS

F32 = mybir.dt.float32
BF16 = mybir.dt.bfloat16
I32 = mybir.dt.int32
ALU = mybir.AluOpType
ACT = mybir.ActivationFunctionType
AX = mybir.AxisListType

PACK = dict(ident=(128, 128), iota=(128, 128), we=(128, 64), w1=(64, 128), b1=(128, 1), w2=(128, 64), b2=(128, 64),
            we_b=(128, 64), eps=(128, 1), wa2=(64, 128), wb=(64, 64), wc=(17, 64), wm2=(65, 65),
            wu1a=(64, 64), wu1b=(64, 64), bu1=(64, 1), wu2=(65, 64), gamma=(128, 64),
            beta=(128, 64), thph=(65, 128), ws0=(65, 128), wn0=(64, 128), ws1=(128, 128),
            sb1=(128, 128), wn1=(128, 128), wns2=(128, 128), sb2=(128, 64), zero=(128, 1))
AT = {}
WCOLS = 0
for _name, (_rows, _cols) in PACK.items():
    AT[_name] = WCOLS
    WCOLS += _cols


def gnn(nc, x_in, src_in, dst_in, next_in, dstrow_in, prevrow_in, ea_in, ef_in, pack_in, out):
    ctx = ExitStack()
    with ctx:
        def sb(name, shape, dt=F32):
            return ctx.enter_context(nc.sbuf_tensor(name, shape, dt))

        def sem(name):
            return ctx.enter_context(nc.semaphore(name))

        widths = [D, D, D, D, H, D]
        table = [nc.dram_tensor(f"table{k}", (ROWS, w), F32).ap() for k, w in enumerate(widths)]
        table_nm = [t.rearrange("(p c) f -> p (c f)", p=P) for t in table]
        ew_dram = nc.dram_tensor("edge_term", (NT // HALF * P, HALF * D), F32).ap()
        mask_dram = nc.dram_tensor("scan_mask", (1, NT * P), BF16).ap()

        agg = sb("agg", [P, COLS])
        big = sb("big", [P, COLS])
        part_hm = big[:, 0:COLS // 2].bitcast(BF16)
        part_lo = big[0:D, COLS // 2:COLS].bitcast(BF16)
        x_nm = sb("x_nm", [P, CHUNKS * D])
        h_nm = sb("h_nm", [P, CHUNKS * D])
        src_idx = sb("src_idx", [P, NT + U], I32)
        base = sb("base", [1, NT + HALF], I32)
        rel = sb("rel", [P, NT + HALF], BF16)
        rel_end = sb("rel_end", [P, NT + HALF], BF16)
        deg = sb("deg", [P, CHUNKS])
        rdeg = sb("rdeg", [P, CHUNKS, 1])
        no_in = sb("no_in", [P, CHUNKS, 1])
        idxw = sb("idxw", [P, U], I32)
        W = sb("W", [P, WCOLS])
        one_eps = sb("one_eps", [P, 1])
        ident_b = sb("ident_b", [P, P], BF16)
        stat = sb("stat", [P, 4, C7, 1])
        AR = 7168
        arena = sb("arena", [P, AR])
        PS = ctx.enter_context(nc.psum_tensor("PS", [P, 8 * 512], F32))

        def w(name):
            r, c = PACK[name]
            return W[0:r, AT[name]:AT[name] + c]

        def carve(*sizes):
            at, got = 0, []
            for s in sizes:
                got.append(arena[:, at:at + s])
                at += s
            assert at <= AR, at
            return got

        def bank(b, n=512, o=0, rows=P):
            return PS[0:rows, b * 512 + o:b * 512 + o + n]

        def n3(ap):
            return ap.rearrange("p (c f) -> p c f", c=C7)

        msg_f, rest, S_f = arena[:, 0:U * H], arena[:, U * D:AR - U * P], arena[:, AR - U * P:AR]
        S = S_f.rearrange("p (t w) -> p t w", t=U)

        gathered = [sem(f"gathered{j}") for j in range(U)]
        phase = sem("phase")
        phases = dict(sp=0, act=0, pool=0, dve=0, pe=0)

        def hold(eng):
            eng.nop(nofuse=True)

        def barrier(eng, who):
            phases[who] += 1
            eng.drain().then_inc(phase, 1)
            eng.wait_ge(phase, 5 * phases[who])

        class Pass:

            def __init__(self, k, name, rows):
                self.k, self.rows, self.width = k, rows, widths[k]
                self.msg = (msg_f[:, 0:U * self.width]).rearrange("p (t f) -> p t f", t=U)
                self.idx_ready = sem(f"{name}_idx_ready")
                self.s_ready = sem(f"{name}_s_ready")
                self.summed = sem(f"{name}_summed")
                self.used = self.summed
                self.added = sem(f"{name}_added")

        PL0, PL1, PL2, PL3a, PL3b, PL3c = (Pass(k, n, r) for k, (n, r) in enumerate(
            [("l0", P), ("l1", D + 1), ("l2", D), ("l3a", D), ("l3b", H), ("l3c", D)]))
        PL1.used = sem("l1_used")
        PL2.used = sem("l2_used")

        def acc_slot(T, rows):
            return bank((2, 3, 6, 7)[T % 4], P, 0, rows)

        def pool_gathers(pool, ps, used, unit):
            n, q = U // unit, 4 // unit
            with pool.Fori(0, NIT) as i:
                for g in range(4):
                    pool.wait_ge(used, i * n + (g + 1) * q)
                    if g % 2 == 0:
                        pool.wait_ge(ps.idx_ready, i * 2 + g // 2 + 1)
                    hold(pool)
                    for j in range(4 * g, 4 * g + 4):
                        pool.indirect_dma_start(
                            out=ps.msg[:, j, :], out_offset=None, in_=table[ps.k],
                            in_offset=bass.IndirectOffsetOnAxis(ap=idxw[:, j:j + 1], axis=0)
                        ).then_inc(gathered[j], 16)

        def act_idx(act, ps, col, half):
            act.activation(idxw[:, half * HALF:(half + 1) * HALF], src_idx[:, bass.ds(col, HALF)],
                           ACT.Copy).then_inc(ps.idx_ready, 1)

        def tile_landed(eng, ps, i, j):
            eng.wait_ge(gathered[j], i * 16 + (ps.k * NIT + 1) * 16)

        def half_landed(eng, ps, i, half):
            for j in range(half * HALF, (half + 1) * HALF):
                tile_landed(eng, ps, i, j)

        def dve_bases(columns):
            _, b = nc.values_load_multi_w_load_instructions(
                base[0:1, columns], engines=[mybir.EngineType.DVE], min_val=0, max_val=N,
                skip_runtime_bounds_check_because="dst holds node numbers below N, the padding N")
            return b

        def dve_s(dve, ps, i, column, js):
            for j in js:
                dve.tensor_scalar(out=S[:, j % U, :], in0=w("iota"), scalar1=column[:, bass.ds(i * U + j, 1)],
                                  scalar2=None, op0=ALU.is_equal).then_inc(ps.s_ready, 1)

        def dve_add(dve, ps, b, i, js, first=0):
            for j in js:
                dve.wait_ge(ps.summed, i * U + j + 1 + U)
                dve.wait_ge(ps.added, i * U + j + 4)
                win = agg[0:ps.rows, bass.ds(b[first + j], P)]
                dve.tensor_tensor(out=win, in0=acc_slot(j, ps.rows), in1=win, op=ALU.add).then_inc(ps.added, 1)

        ea_in_sem = [sem(f"ea_loaded{h}") for h in range(2)]
        ef_in_sem = [sem(f"ef_loaded{h}") for h in range(2)]
        ew_mm = sem("ew_mm")
        ew_sb = sem("ew_sb")
        ew_stored = sem("ew_stored")
        ew_free = sem("ew_free")
        ew_in_sem = [sem(f"ew_loaded{h}") for h in range(2)]
        win_t = sem("win_t")
        win_sb = sem("win_sb")
        pre_mm = sem("pre_mm")
        pre_ew = sem("pre_ew")
        relued = sem("relued")
        mask_in_sem = [sem(f"mask_loaded{h}") for h in range(2)]
        scanned = sem("scanned")
        back_t = sem("back_t")
        back_sb = sem("back_sb")
        s_load = sem("s_load")
        s_setup = sem("s_setup")
        s_mask = sem("s_mask")
        s_zero = sem("s_zero")
        s_ones = sem("s_ones")

        ea_f, ef_f, ews_f = rest[:, 0:U * D], rest[:, U * D:3 * U * D], rest[:, 3 * U * D:4 * U * D]
        ea = ea_f.rearrange("p (t f) -> p t f", t=U)
        ef = ef_f.rearrange("p (h e) -> p h e", h=2)
        ews = ews_f.rearrange("p (h f) -> p h f", h=2)
        WIN = 3 * D + P
        at_l1 = [0, U * D, U * D + 4 * WIN, U * D + 4 * WIN + 8 * D, U * D + 4 * WIN + 8 * D + U * (D + 1)]
        ewl = rest[:, at_l1[0]:at_l1[1]].rearrange("p (h f) -> p h f", h=2)
        win = rest[:, at_l1[1]:at_l1[2]].bitcast(BF16).rearrange("p (t f) -> p t f", t=8)
        pre = rest[:, at_l1[2]:at_l1[3]].rearrange("p (g f) -> p g f", g=2)
        msg1 = rest[:, at_l1[3]:at_l1[4]].rearrange("p (t f) -> p t f", t=U)
        at_l2 = [0, U * P // 2, U * P // 2 + 8 * P, U * P // 2 + 8 * P + 8 * D]
        mask = rest[0:D, at_l2[0]:at_l2[1]].bitcast(BF16).rearrange("p (h e) -> p h e", h=2)
        run = rest[0:D, at_l2[1]:at_l2[2]].rearrange("p (g e) -> p g e", g=2)
        back = rest[:, at_l2[2]:at_l2[3]].rearrange("p (g f) -> p g f", g=2)

        class Stage:

            def __init__(self, name, **steps):
                self.steps = {who: names.split() for who, names in steps.items()}
                self.sem = {who: sem(f"{name}_{who}") for who in steps}
                self.told = {who: 0 for who in steps}

            def start(self, eng, who):
                if who in self.sem:
                    eng.sem_inc(self.sem[who], len(self.steps[who]))

            def done(self, ins, who, name):
                names = self.steps[who]
                assert names[self.told[who] % len(names)] == name, (who, name)
                self.told[who] += 1
                ins.then_inc(self.sem[who], 1)

            def after(self, eng, i, *whos):
                for what in whos:
                    who, name = what.rstrip("<").split(".")
                    k = len(self.steps[who])
                    ahead = 0 if what.endswith("<") else k
                    eng.wait_ge(self.sem[who], i * k + ahead + self.steps[who].index(name) + 1)

        def skewed(eng, who, stages, body):
            for stage in stages:
                stage.start(eng, who)
            body(0, True, False)
            with eng.Fori(1, NLOOP) as k:
                body(k, True, True)
            body(NLOOP, False, True)
            barrier(eng, who)

        NORM = "{0}sum {0}centred {0}sumsq {0}var {0}rstd {0}normed"
        AX_ = Stage("ax", dve=NORM.format("") + " tab", act="squared std", sp="stored")
        AY = Stage("ay", pe="HT", act="hT", pool="h")
        BX = Stage("bx", pe="U Z O", act="uT zT", dve="bias x", pool="zero")
        BY = Stage("by", pe="HT APT TAB", act="squared std hT high mid midlow tab", dve=NORM.format("") + " rest1",
                   pool="h lo", sp="stored")
        CX = Stage("cx", pe="AG H1T DEG RU O", act="hc agT h1T rT vsquared vstd",
                   dve="deg v " + NORM.format("v") + " scaled shifted x", pool="zero")
        CY = Stage("cy", pe="HT THPH", act="squared std hT tab", dve=NORM.format("") + " diff", sp="stored")
        DX = Stage("dx", pe="T", act="aggc", dve="zero y keep kept x", pool="zero")
        DY = Stage("dy", pe="HT SELF", act="squared std hT self", dve=NORM.format(""), sp="stored")
        EX = Stage("ex", pe="M", act="aggc", dve="mean sum", pool="zero")
        EY = Stage("ey", pe="ZT SELF", act="z zT", dve="self", sp="stored")
        FX = Stage("fx", pe="M", act="aggc", dve="mean sum", pool="zero")
        FY = Stage("fy", pe="ZT BOTH", act="z zT tab", dve="self", sp="stored")
        GX = Stage("gx", pe="T", act="aggc", dve="mean sum x", sp="stored")

        (hc_f, uT, zT, xc_f, sq_f, hs_f, hT, tb_f, v_f, r1, mid_f) = carve(
            NF, NC, NC, NF, NF, NF, NC, NF, NF, NC, NC // 2)
        hc, xc, sq, hs, tb, vv = (n3(a) for a in (hc_f, xc_f, sq_f, hs_f, tb_f, v_f))
        mid = mid_f[0:D].bitcast(BF16)
        aggc, z_f, zr_f, zT3, kept = uT, r1, zT, hT, zT[:, 0:NF]
        zr = zr_f.rearrange("p (c f) -> p c f", c=C7)

        def nf(i):
            return bass.ds(i * NF, NF)

        def ncol(i):
            return bass.ds(i * NC, NC)

        def halves():
            return [(0, 512), (512, NC)]

        def chunk(c, n=P):
            return slice(c * n, (c + 1) * n)

        block = ctx.enter_context(nc.Block())

        @block.sync
        def _(sp):
            sp.dma_start(W[:, :], pack_in).then_inc(s_load, 16)
            sp.dma_start(x_nm[:, :], x_in).then_inc(s_load, 16)
            sp.dma_start(src_idx[:, 0:NT], src_in).then_inc(s_load, 16)
            sp.dma_start(base[:, 0:NT], dst_in[0:1, :]).then_inc(s_load, 16)
            for k, a in enumerate((dst_in, next_in, dstrow_in, prevrow_in, dst_in[0:1, :].to_broadcast([P, NT]))):
                sp.dma_start(agg[:, k * NT:(k + 1) * NT].bitcast(I32), a).then_inc(s_load, 16)
            sp.wait_ge(s_mask, 1)
            sp.dma_start(mask_dram[0, :].rearrange("(c q e) -> q c e", q=P, e=P),
                         big[:, 0:NT // 2].bitcast(BF16).rearrange("q (c e) -> q c e", e=P)).then_inc(s_mask, 16)
            sp.wait_ge(s_mask, 17)
            barrier(sp, "sp")

            def store_loop(lp, what, src, dst, n):
                with sp.Fori(0, NLOOP) as i:
                    lp.after(sp, i, what)
                    sp.dma_start(dst[:, bass.ds(i * n, n)], src).then_inc(s_tab[lp], 16)
                    sp.wait_ge(s_tab[lp], i * 16 + 16)
                    sp.sem_inc(lp.sem["sp"], 1)
                barrier(sp, "sp")

            s_tab = {lp: sem(f"rows_stored{n}") for n, lp in enumerate((AX_, BY, CY, DY, EY, FY, GX))}
            for lp in s_tab:
                lp.start(sp, "sp")
            store_loop(AX_, "dve.tab", tb_f, table_nm[0], NF)

            def attributes_in(i, h):
                sp.wait_ge(PL0.summed, i * U + (h + 1) * HALF)
                sp.dma_start(ea_f[:, h * HALF * D:(h + 1) * HALF * D],
                             ea_in[bass.ds((i * 2 + h) * P, P), :]).then_inc(ea_in_sem[h], 16)
                sp.dma_start(ef[0:16, h, :], ef_in[:, bass.ds((i * 2 + h) * HALF * P, HALF * P)]
                             ).then_inc(ef_in_sem[h], 16)

            def terms_out(i, h):
                sp.wait_ge(ew_sb, i * 2 + h + 3)
                sp.dma_start(ew_dram[bass.ds((i * 2 + h) * P, P), :], ews[:, h, :]).then_inc(ew_stored, 16)
                sp.wait_ge(ew_stored, i * 32 + h * 16 + 16)
                sp.sem_inc(ew_free, 1)

            sp.wait_ge(s_ones, 1)
            attributes_in(0, 0)
            attributes_in(0, 1)
            terms_out(0, 0)
            with sp.Fori(1, NIT) as i:
                attributes_in(i, 0)
                terms_out(i - 1, 1)
                attributes_in(i, 1)
                terms_out(i, 0)
            terms_out(NIT - 1, 1)
            barrier(sp, "sp")
            store_loop(BY, "act.tab", tb_f, table_nm[1], NF)

            with sp.Fori(0, NIT) as i:
                for h in range(2):
                    sp.wait_ge(PL1.used, i * 4 + h * 2 + 2)
                    sp.dma_start(ewl[:, h, :], ew_dram[bass.ds((i * 2 + h) * P, P), :]).then_inc(ew_in_sem[h], 16)
            barrier(sp, "sp")
            store_loop(CY, "act.tab", tb_f, table_nm[2], NF)

            with sp.Fori(0, NIT) as i:
                for h in range(2):
                    sp.wait_ge(scanned, i * 4 + h * 2 + 2)
                    sp.dma_start(mask[:, h, :], mask_dram[0:1, bass.ds((i * 2 + h) * HALF * P, HALF * P)]
                                 .to_broadcast([D, HALF * P])).then_inc(mask_in_sem[h], 16)
            barrier(sp, "sp")
            store_loop(DY, "dve.normed", hs_f, table_nm[3], NF)
            barrier(sp, "sp")
            store_loop(EY, "act.z", zr_f, table_nm[4], NC)
            barrier(sp, "sp")
            store_loop(FY, "act.tab", tb_f, table_nm[5], NF)
            barrier(sp, "sp")
            store_loop(GX, "dve.x", tb_f, out, NF)

        @block.gpsimd
        def _(pool):
            pool.memset(src_idx[:, NT:NT + U], 0).then_inc(s_zero, 1)
            pool.memset(base[:, NT:NT + HALF], 0).then_inc(s_zero, 1)
            pool.memset(rel[:, NT:NT + HALF], 0.0).then_inc(s_zero, 1)
            pool.memset(rel_end[:, NT:NT + HALF], 0.0).then_inc(s_zero, 1)
            barrier(pool, "pool")
            pool.memset(agg[D:P, :], 0.0).then_inc(s_zero, 1)
            pool.memset(agg[0:D, ROWS:COLS], 0.0).then_inc(s_zero, 1)
            pool.wait_ge(s_zero, 6)

            def keep_h(stage, normed, i):
                stage.after(pool, i, "pool.h<")
                normed.after(pool, i, "dve.normed")
                stage.done(pool.tensor_copy(h_nm[:, nf(i)], hs_f), "pool", "h")

            def zeros(stage, consumer, i):
                stage.after(pool, i, consumer)
                stage.done(pool.tensor_copy(agg[:, ncol(i)], w("zero").to_broadcast([P, NC])), "pool", "zero")

            AY.start(pool, "pool")
            with pool.Fori(0, NLOOP) as i:
                keep_h(AY, AX_, i)
            barrier(pool, "pool")

            def loop_b(k, x, y):
                if x:
                    zeros(BX, "pe.U", k)
                if y:
                    keep_h(BY, BY, k - 1)
                    BY.after(pool, k - 1, "act.midlow")
                    BY.done(pool.tensor_tensor(part_lo[:, ncol(k - 1)], r1[0:D], mid, ALU.subtract), "pool", "lo")

            def zero_loop(stage, consumer):
                stage.start(pool, "pool")
                with pool.Fori(0, NLOOP) as i:
                    zeros(stage, consumer, i)
                barrier(pool, "pool")

            pool_gathers(pool, PL0, PL0.used, 1)
            barrier(pool, "pool")
            skewed(pool, "pool", (BX, BY), loop_b)
            pool_gathers(pool, PL1, PL1.used, 4)
            barrier(pool, "pool")
            zero_loop(CX, "pe.AG")
            pool_gathers(pool, PL2, PL2.used, 1)
            barrier(pool, "pool")
            zero_loop(DX, "act.aggc")
            pool_gathers(pool, PL3a, PL3a.used, 1)
            barrier(pool, "pool")
            zero_loop(EX, "act.aggc")
            pool_gathers(pool, PL3b, PL3b.used, 1)
            barrier(pool, "pool")
            zero_loop(FX, "act.aggc")
            pool_gathers(pool, PL3c, PL3c.used, 1)
            barrier(pool, "pool")
            barrier(pool, "pool")

        @block.scalar
        def _(act):
            def copy(lp, i, name, dst, src, *waits, func=ACT.Copy, **kw):
                lp.after(act, i, *waits)
                lp.done(act.activation(dst, src, func, **kw), "act", name)

            def norm_parts(lp, i, pre=""):
                copy(lp, i, pre + "squared", sq_f, xc_f, f"dve.{pre}centred", func=ACT.Square)
                copy(lp, i, pre + "std", stat[:, 3], stat[:, 2], f"dve.{pre}var", func=ACT.Sqrt)

            def sum_pass(ps):
                act_idx(act, ps, 0, 0)
                with act.Fori(0, NIT) as i:
                    act.wait_ge(ps.used, i * U + U)
                    act_idx(act, ps, i * U + HALF, 1)
                    act.wait_ge(ps.used, i * U + HALF + U)
                    act_idx(act, ps, i * U + U, 0)
                barrier(act, "act")

            barrier(act, "act")
            def loop_a(k, x, y):
                if x:
                    norm_parts(AX_, k)
                if y:
                    copy(AY, k - 1, "hT", agg[0:D, ncol(k - 1)], bank(0, NC, rows=D), "pe.HT",
                         scale=one_eps[0:D, :])

            skewed(act, "act", (AX_, AY), loop_a)

            def store_terms(i, h):
                act.wait_ge(ew_mm, i * 2 + h + 1)
                act.wait_ge(ew_free, i * 2 + h + 1)
                act.activation(ews[:, h, :], bank(4 + h), ACT.Copy).then_inc(ew_sb, 1)

            act.sem_inc(ew_sb, 2)
            act_idx(act, PL0, 0, 0)
            with act.Fori(0, NIT) as i:
                act.wait_ge(PL0.used, i * U + U)
                act_idx(act, PL0, i * U + HALF, 1)
                store_terms(i, 0)
                act.wait_ge(PL0.used, i * U + HALF + U)
                act_idx(act, PL0, i * U + U, 0)
                store_terms(i, 1)
            barrier(act, "act")

            def loop_b(k, x, y):
                m = k - 1
                if y:
                    copy(BY, m, "squared", sq_f, xc_f, "dve.centred", func=ACT.Square)
                if x:
                    copy(BX, k, "uT", uT[0:D], bank(0, NC, rows=D), "pe.U", "pe.Z<")
                if y:
                    copy(BY, m, "std", stat[:, 3], stat[:, 2], "dve.var", func=ACT.Sqrt)
                    copy(BY, m, "hT", hT[0:D], bank(5, NC, rows=D), "pe.HT", "pe.TAB<")
                if x:
                    copy(BX, k, "zT", zT, bank(2, NC), "pe.Z", "pe.O<", func=ACT.Relu, bias=w("b1"))
                if y:
                    copy(BY, m, "high", part_hm[:, ncol(m)], bank(5, NC), "pe.APT")
                    copy(BY, m, "mid", part_hm[D:P, ncol(m)], r1[D:P], "dve.rest1")
                    copy(BY, m, "midlow", mid, r1[0:D], "pool.lo<")
                    copy(BY, m, "tab", tb_f, bank(7, NF), "pe.TAB", "sp.stored<")

            skewed(act, "act", (BX, BY), loop_b)

            act.sem_inc(win_sb, 4)
            act.sem_inc(relued, 2)

            def win_copy(i, g):
                for j in range(4 * g, 4 * g + 4):
                    act.wait_ge(win_t, i * U + j + 1)
                    act.wait_ge(pre_mm, i * U + j + 1)
                    act.activation(win[:, j % 8, :], bank(j % 2, WIN), ACT.Copy).then_inc(win_sb, 1)

            def relu_sums(i, g):
                act.wait_ge(PL1.used, i * 4 + g + 5)
                act.wait_ge(PL1.summed, i * U + 4 * g + 4)
                act.activation(msg1[:, 4 * g:4 * g + 4, 0:D],
                               pre[:, g % 2, :].rearrange("p (t f) -> p t f", t=4), ACT.Relu).then_inc(relued, 1)

            act_idx(act, PL1, 0, 0)
            win_copy(0, 0)
            win_copy(0, 1)
            with act.Fori(0, NIT) as i:
                half_landed(act, PL1, i - 1, 1)
                act_idx(act, PL1, i * U + HALF, 1)
                relu_sums(i, 0)
                win_copy(i, 2)
                relu_sums(i, 1)
                half_landed(act, PL1, i, 0)
                act_idx(act, PL1, i * U + U, 0)
                win_copy(i, 3)
                relu_sums(i, 2)
                win_copy(i, 4)
                relu_sums(i, 3)
                win_copy(i, 5)
            barrier(act, "act")

            def loop_c(k, x, y):
                m = k - 1
                if x:
                    copy(CX, k, "hc", hc_f, h_nm[:, nf(k)], "pe.H1T<", "dve.v<")
                    copy(CX, k, "agT", uT[0:D + 1], bank(0, NC, rows=D + 1), "pe.AG", "pe.RU<")
                if y:
                    copy(CY, m, "squared", sq_f, xc_f, "dve.centred", func=ACT.Square)
                if x:
                    copy(CX, k, "h1T", r1[0:D], bank(2, NC, rows=D), "pe.H1T", "pe.RU<")
                if y:
                    copy(CY, m, "std", stat[:, 3], stat[:, 2], "dve.var", func=ACT.Sqrt)
                if x:
                    copy(CX, k, "rT", zT[0:D], bank(4, NC, rows=D), "pe.RU", "pe.O<", func=ACT.Relu, bias=w("bu1"))
                if y:
                    copy(CY, m, "hT", hT[0:D], bank(2, NC, rows=D), "pe.HT", "pe.THPH<")
                if x:
                    copy(CX, k, "vsquared", sq_f, xc_f, "dve.vcentred", func=ACT.Square)
                if y:
                    copy(CY, m, "tab", tb, bank(4, NC).rearrange("p (c f) -> p c f", c=C7)[:, :, 0:D],
                         "pe.THPH", "sp.stored<", "dve.diff<")
                if x:
                    copy(CX, k, "vstd", stat[:, 3], stat[:, 2], "dve.vvar", func=ACT.Sqrt)

            skewed(act, "act", (CX, CY), loop_c)

            def back_copy(i, g):
                act.wait_ge(back_t, i * 4 + g + 3)
                act.wait_ge(PL2.summed, i * U + 4 * g + 12)
                act.activation(back[:, g % 2, :], bank(4 + g % 2, 4 * D), ACT.Copy).then_inc(back_sb, 1)

            act.sem_inc(back_sb, 2)
            act_idx(act, PL2, 0, 0)
            act_idx(act, PL2, HALF, 1)

            def body2(i):
                back_copy(i, 0)
                half_landed(act, PL2, i, 0)
                act_idx(act, PL2, i * U + U, 0)
                back_copy(i, 1)
                back_copy(i, 2)

            body2(0)
            with act.Fori(1, NIT) as i:
                half_landed(act, PL2, i - 1, 1)
                act_idx(act, PL2, i * U + HALF, 1)
                back_copy(i - 1, 3)
                body2(i)
            back_copy(NIT - 1, 3)
            barrier(act, "act")

            def loop_d(k, x, y):
                m = k - 1
                if x:
                    copy(DX, k, "aggc", aggc[0:D], agg[0:D, ncol(k)], "pe.T<")
                if y:
                    norm_parts(DY, m)
                    copy(DY, m, "hT", hT[0:D], bank(2, NC, rows=D), "pe.HT", "pe.SELF<")
                    copy(DY, m, "self", big[:, ncol(m)], bank(4, NC), "pe.SELF")

            skewed(act, "act", (DX, DY), loop_d)
            sum_pass(PL3a)

            def loop_e(k, x, y):
                m = k - 1
                if x:
                    copy(EX, k, "aggc", aggc[0:D], agg[0:D, ncol(k)], "pe.M<")
                if y:
                    EX.after(act, m, "dve.sum")
                    copy(EY, m, "z", zr_f, z_f, "pe.ZT<", "sp.stored<", func=ACT.Relu)
                    copy(EY, m, "zT", zT3, bank(2, NC), "pe.ZT", "pe.SELF<")

            skewed(act, "act", (EX, EY), loop_e)
            sum_pass(PL3b)

            def loop_f(k, x, y):
                m = k - 1
                if x:
                    copy(FX, k, "aggc", aggc, agg[:, ncol(k)], "pe.M<")
                if y:
                    FX.after(act, m, "dve.sum")
                    copy(FY, m, "z", zr_f, z_f, "pe.ZT<", func=ACT.Relu)
                    copy(FY, m, "zT", zT3, bank(2, NC), "pe.ZT", "pe.BOTH<")
                    copy(FY, m, "tab", tb, bank(4, NC).rearrange("p (c f) -> p c f", c=C7)[:, :, 0:D],
                         "pe.BOTH", "sp.stored<")

            skewed(act, "act", (FX, FY), loop_f)
            sum_pass(PL3c)

            GX.start(act, "act")
            with act.Fori(0, NLOOP) as i:
                copy(GX, i, "aggc", aggc[0:D], agg[0:D, ncol(i)], "pe.T<")
            barrier(act, "act")

        @block.vector
        def _(dve):
            count = [0]

            def setup(ins):
                count[0] += 1
                ins.then_inc(s_setup, 1)
                dve.wait_ge(s_setup, count[0])

            def chain(lp, i, name, ins):
                lp.done(ins, "dve", name)
                lp.after(dve, i, "dve." + name)

            def norm_centre(lp, i, src, pre=""):
                chain(lp, i, pre + "sum", dve.reduce_sum(stat[:, 0], src, AX.X))
                chain(lp, i, pre + "centred", dve.scalar_tensor_tensor(
                    out=xc, in0=stat[:, 0].to_broadcast([P, C7, D]), scalar=-1.0 / D, in1=src, op0=ALU.mult, op1=ALU.add))

            def norm_var(lp, i, pre=""):
                lp.after(dve, i, f"act.{pre}squared")
                chain(lp, i, pre + "sumsq", dve.reduce_sum(stat[:, 1], sq, AX.X))
                chain(lp, i, pre + "var", dve.tensor_scalar(stat[:, 2], stat[:, 1], 1.0 / D, LN_EPS, ALU.mult, ALU.add))

            def norm_scale(lp, i, dst, pre="", relu=True):
                rstd = stat[:, 1]
                lp.after(dve, i, f"act.{pre}std")
                chain(lp, i, pre + "rstd", dve.reciprocal(rstd, stat[:, 3]))
                if relu:
                    ins = dve.scalar_tensor_tensor(out=dst, in0=xc, scalar=0.0, in1=rstd.to_broadcast([P, C7, D]),
                                                   op0=ALU.max, op1=ALU.mult)
                else:
                    ins = dve.tensor_tensor(dst, xc, rstd.to_broadcast([P, C7, D]), ALU.mult)
                chain(lp, i, pre + "normed", ins)

            def norm(lp, i, src, dst, pre="", relu=True):
                norm_centre(lp, i, src, pre)
                norm_var(lp, i, pre)
                norm_scale(lp, i, dst, pre, relu)

            def bcast(name, n=D):
                return w(name).rearrange("p (c f) -> p c f", c=1).to_broadcast([P, C7, n])

            dve.wait_ge(s_load, 9 * 16)
            dst, nxt, dstrow, prevrow, base_b = (agg[:, k * NT:(k + 1) * NT].bitcast(I32) for k in range(5))
            f0, f1 = agg[:, 5 * NT:6 * NT], agg[:, 6 * NT:7 * NT]
            rel_f, m_f = big[:, NT:2 * NT], big[:, 2 * NT:3 * NT]
            hi_i, lo_i = f0.bitcast(I32), f1.bitcast(I32)
            setup(dve.tensor_scalar(hi_i, src_idx[:, 0:NT], 7, None, ALU.logical_shift_right))
            setup(dve.tensor_scalar(lo_i, src_idx[:, 0:NT], P - 1, None, ALU.bitwise_and))
            setup(dve.scalar_tensor_tensor(out=src_idx[:, 0:NT], in0=lo_i, scalar=float(CHUNKS), in1=hi_i,
                                           op0=ALU.mult, op1=ALU.add))
            setup(dve.tensor_tensor(rel_f, dst, base_b, ALU.subtract))
            setup(dve.tensor_copy(rel[:, 0:NT], rel_f))
            setup(dve.tensor_tensor(m_f, dst, nxt, ALU.not_equal))
            setup(dve.scalar_tensor_tensor(out=rel_f, in0=rel_f, scalar=1.0, in1=m_f, op0=ALU.add, op1=ALU.mult))
            setup(dve.tensor_scalar(rel_end[:, 0:NT], rel_f, -1.0, None, ALU.add))
            setup(dve.tensor_tensor(m_f, dstrow, prevrow, ALU.is_equal))
            setup(dve.tensor_scalar(m_f, m_f, -0.5, 3.3895313892515355e38, ALU.add, ALU.mult))
            dve.tensor_scalar(big[:, 0:NT // 2].bitcast(BF16), m_f, 2.0, None, ALU.mult).then_inc(s_mask, 1)
            setup(dve.tensor_copy(ident_b[:, :], w("ident")))
            setup(dve.tensor_scalar(one_eps[:, :], w("eps"), 1.0, None, ALU.add))
            barrier(dve, "dve")

            def loop_a(k, x, y):
                if x:
                    AY.after(dve, k, "pe.HT<", "pool.h<")
                    norm(AX_, k, n3(x_nm[:, nf(k)]), hs)
                    AX_.after(dve, k, "sp.stored<")
                    chain(AX_, k, "tab", dve.tensor_tensor(tb, hs, bcast("we_b"), ALU.add))

            AX_.start(dve, "dve")
            with dve.Fori(0, NLOOP) as i:
                loop_a(i, True, False)
            barrier(dve, "dve")

            def sum_pass(ps):
                dve.sem_inc(ps.added, 4)
                dve_s(dve, ps, 0, rel, range(HALF))
                with dve.Fori(0, NIT) as i:
                    b = dve_bases(bass.ds(i * U, U))
                    for j in range(U):
                        dve_add(dve, ps, b, i, [j])
                        dve_s(dve, ps, i, rel, [j + HALF])
                barrier(dve, "dve")

            dve.memset(ef_f[:, :], 1.0).then_inc(s_ones, 1)
            sum_pass(PL0)

            setup(dve.memset(part_hm[:, ROWS:COLS], 0.0))
            setup(dve.memset(part_lo[:, ROWS:COLS], 0.0))

            def loop_b(k, x, y):
                m = k - 1
                if y:
                    BY.after(dve, m, "pe.HT<", "pool.h<")
                    norm(BY, m, n3(x_nm[:, nf(m)]), hs)
                if x:
                    xk = x_nm[:, nf(k)]
                    chain(BX, k, "bias", dve.tensor_tensor(n3(xk), n3(xk), bcast("b2"), ALU.add))
                if y:
                    BY.after(dve, m, "act.high", "act.midlow<", "pool.lo<")
                    chain(BY, m, "rest1", dve.tensor_tensor(r1, bank(5, NC), part_hm[:, ncol(m)], ALU.subtract))
                if x:
                    BX.after(dve, k, "pe.O")
                    chain(BX, k, "x", dve.tensor_tensor(xk, bank(4, NF), xk, ALU.add))

            skewed(dve, "dve", (BX, BY), loop_b)

            def lagging_adds(ps, column, step):
                def group(i, g):
                    step(i, g)
                    dve_s(dve, ps, i, column, range(4 * g + HALF, 4 * g + HALF + 4))

                dve_s(dve, ps, 0, column, range(HALF))
                b = dve_bases(slice(0, U))
                for g in range(4):
                    group(0, g)
                    if g > 0:
                        dve_add(dve, ps, b, 0, range(4 * g - 4, 4 * g))
                with dve.Fori(1, NIT) as i:
                    b = dve_bases(bass.ds(i * U - 4, U))
                    for g in range(4):
                        group(i, g)
                        dve_add(dve, ps, b, i, range(4 * g - 4, 4 * g), 4)
                b = dve_bases(slice(NT - 4, NT))
                dve_add(dve, ps, b, NIT, range(-4, 0), 4)

            setup(dve.memset(msg1[:, :, D:D + 1], 1.0))
            dve.sem_inc(PL1.added, 4)
            dve.sem_inc(PL1.used, 4)

            def edge_sums(i, g):
                dve.wait_ge(pre_mm, i * U + 4 * g + 4 + 8)
                dve.wait_ge(relued, i * 4 + g + 1)
                if g % 2 == 0:
                    dve.wait_ge(ew_in_sem[g // 2], i * 16 + 16)
                dve.tensor_tensor(pre[:, g % 2, :], bank(4 + g % 2, 4 * D),
                                  ewl[:, g // 2, (g % 2) * 4 * D:(g % 2 + 1) * 4 * D], ALU.add).then_inc(pre_ew, 1)
                dve.wait_ge(pre_ew, i * 4 + g + 1)
                for j in range(4 * g, 4 * g + 4):
                    tile_landed(dve, PL1, i, j)
                dve.tensor_tensor(pre[:, g % 2, :], pre[:, g % 2, :],
                                  msg_f[:, 4 * g * D:4 * (g + 1) * D], ALU.add).then_inc(PL1.used, 1)

            lagging_adds(PL1, rel, edge_sums)
            barrier(dve, "dve")

            setup(dve.memset(zT[D:D + 1], 1.0))
            setup(dve.memset(hT[D:D + 1], 1.0))

            def loop_c(k, x, y):
                m = k - 1
                if y:
                    CY.after(dve, m, "pe.HT<")
                    norm(CY, m, n3(x_nm[:, nf(m)]), hs)
                if x:
                    xk = x_nm[:, nf(k)]
                    CX.after(dve, k, "pe.DEG")
                    chain(CX, k, "deg", dve.tensor_copy(deg[:, bass.ds(k * C7, C7)], bank(7, C7 * (D + 1)).rearrange(
                        "p (c f) -> p c f", c=C7)[:, :, D]))
                    CX.after(dve, k, "pe.O", "act.hc")
                    chain(CX, k, "v", dve.tensor_tensor(vv, n3(bank(6, NF)), hc, ALU.add))
                    norm_centre(CX, k, vv, "v")
                    norm_var(CX, k, "v")
                if y:
                    CY.after(dve, m, "act.tab")
                    chain(CY, m, "diff", dve.tensor_tensor(
                        n3(h_nm[:, nf(m)]), bank(4, NC).rearrange("p (c f) -> p c f", c=C7)[:, :, D:2 * D], tb,
                        ALU.subtract))
                if x:
                    norm_scale(CX, k, vv, "v", relu=False)
                    chain(CX, k, "scaled", dve.tensor_tensor(vv, vv, bcast("gamma"), ALU.mult))
                    chain(CX, k, "shifted", dve.tensor_tensor(vv, vv, bcast("beta"), ALU.add))
                    chain(CX, k, "x", dve.tensor_tensor(xk, v_f, xk, ALU.add))

            skewed(dve, "dve", (CX, CY), loop_c)
            setup(dve.tensor_scalar(rdeg[:, :, 0], deg[:, :], 1.0, None, ALU.max))
            setup(dve.reciprocal(rdeg[:, :, 0], rdeg[:, :, 0]))
            setup(dve.tensor_scalar(no_in[:, :, 0], deg[:, :], 0.0, None, ALU.is_equal))

            setup(dve.memset(run[:, 1, :], 0.0))
            dve.sem_inc(PL2.added, 4)
            dve.sem_inc(scanned, 4)

            def scan(i, g):
                dve.wait_ge(PL2.used, i * U + 4 * g + 4 + U)
                dve.wait_ge(back_t, i * 4 + g + 1)
                dve.wait_ge(scanned, i * 4 + g + 4)
                if g % 2 == 0:
                    dve.wait_ge(mask_in_sem[g // 2], i * 16 + 16)
                dve.tensor_tensor_scan(out=run[:, g % 2, :], data0=mask[:, g // 2, (g % 2) * 4 * P:(g % 2 + 1) * 4 * P],
                                       data1=bank(g % 2, 4 * P, rows=D), initial=run[:, (g + 1) % 2, 4 * P - 1:4 * P],
                                       op0=ALU.min, op1=ALU.max).then_inc(scanned, 1)

            lagging_adds(PL2, rel_end, scan)
            barrier(dve, "dve")

            setup(dve.memset(hT[D:D + 1], 1.0))

            def loop_d(k, x, y):
                m = k - 1
                if y:
                    norm_centre(DY, m, n3(x_nm[:, nf(m)]))
                if x:
                    chain(DX, k, "zero", dve.memset(kept, 0.0))
                if y:
                    norm_var(DY, m)
                    DY.after(dve, m, "pe.HT<", "sp.stored<")
                    norm_scale(DY, m, hs)
                if x:
                    xk = x_nm[:, nf(k)]
                    DX.after(dve, k, "pe.T")
                    chain(DX, k, "y", dve.tensor_tensor(v_f, bank(0, NF), h_nm[:, nf(k)], ALU.add))
                    chain(DX, k, "keep", dve.scalar_tensor_tensor(
                        out=hc, in0=vv, scalar=0.0, in1=no_in[:, bass.ds(k * C7, C7), :].to_broadcast([P, C7, D]),
                        op0=ALU.mult, op1=ALU.is_equal))
                    hold(dve)
                    chain(DX, k, "kept", dve.copy_predicated(kept, hc_f.bitcast(I32), v_f))
                    chain(DX, k, "x", dve.tensor_tensor(xk, kept, xk, ALU.add))

            skewed(dve, "dve", (DX, DY), loop_d)

            def mean_and_self(stage, other, k):
                stage.after(dve, k, "pe.M")
                other.after(dve, k, "act.z<")
                chain(stage, k, "mean", dve.tensor_tensor(
                    z_f.rearrange("p (c f) -> p c f", c=C7), bank(0, NC).rearrange("p (c f) -> p c f", c=C7),
                    rdeg[:, bass.ds(k * C7, C7), :].to_broadcast([P, C7, H]), ALU.mult))
                chain(stage, k, "sum", dve.tensor_tensor(z_f, z_f, big[:, ncol(k)], ALU.add))

            def loop_e(k, x, y):
                if x:
                    mean_and_self(EX, EY, k)
                if y:
                    EY.after(dve, k - 1, "pe.SELF")
                    chain(EY, k - 1, "self", dve.tensor_tensor(
                        big[:, ncol(k - 1)].rearrange("p (c f) -> p c f", c=C7),
                        bank(4, NC).rearrange("p (c f) -> p c f", c=C7), bcast("sb1", H), ALU.add))

            def loop_f(k, x, y):
                if x:
                    mean_and_self(FX, FY, k)
                if y:
                    FY.after(dve, k - 1, "act.tab")
                    chain(FY, k - 1, "self", dve.tensor_tensor(
                        n3(h_nm[:, nf(k - 1)]), bank(4, NC).rearrange("p (c f) -> p c f", c=C7)[:, :, D:2 * D],
                        bcast("sb2"), ALU.add))

            sum_pass(PL3a)
            skewed(dve, "dve", (EX, EY), loop_e)
            sum_pass(PL3b)
            skewed(dve, "dve", (FX, FY), loop_f)
            sum_pass(PL3c)

            GX.start(dve, "dve")
            with dve.Fori(0, NLOOP) as i:
                GX.after(dve, i, "pe.T")
                chain(GX, i, "mean", dve.tensor_tensor(
                    vv, n3(bank(0, NF)), rdeg[:, bass.ds(i * C7, C7), :].to_broadcast([P, C7, D]), ALU.mult))
                chain(GX, i, "sum", dve.tensor_tensor(v_f, v_f, h_nm[:, nf(i)], ALU.add))
                GX.after(dve, i, "sp.stored<")
                chain(GX, i, "x", dve.scalar_tensor_tensor(out=tb_f, in0=v_f, scalar=0.0, in1=x_nm[:, nf(i)],
                                                           op0=ALU.max, op1=ALU.add))
            barrier(dve, "dve")

        @block.tensor
        def _(pe):
            def mm(out_, lhsT, rhs, start=True, stop=True):
                return pe.matmul(out_, lhsT, rhs, start=start, stop=stop)

            def transposes(dst_bank, src3, rows_in, cols_in):
                hold(pe)
                for c in range(C7):
                    last = pe.transpose(bank(dst_bank, rows_in, c * rows_in, cols_in), src3(c),
                                        w("ident")[0:rows_in, 0:rows_in])
                return last

            barrier(pe, "pe")
            AY.start(pe, "pe")
            with pe.Fori(0, NLOOP) as i:
                AX_.after(pe, i, "dve.normed")
                AY.after(pe, i, "act.hT<")
                AY.done(transposes(0, lambda c: hs[:, c, :], P, D), "pe", "HT")
            barrier(pe, "pe")

            def sum_tiles(ps, i, js, message, waits=None):
                for j in js:
                    if waits:
                        waits(j)
                    pe.wait_ge(ps.s_ready, i * U + j + 1)
                    pe.wait_ge(ps.added, i * U + j + 1)
                    mm(acc_slot(j, ps.rows), message(j), S[:, j, :]).then_inc(ps.summed, 1)

            pe.sem_inc(PL0.summed, U)
            pe.sem_inc(ew_free, 2)
            with pe.Fori(0, NIT) as i:
                for h in range(2):
                    pe.wait_ge(ef_in_sem[h], i * 16 + 16)
                    pe.wait_ge(ew_sb, i * 2 + h + 1)
                    for t in range(HALF):
                        last = mm(bank(4 + h, D, t * D), ef[0:17, h, t * P:(t + 1) * P], w("wc"))
                    last.then_inc(ew_mm, 1)
                    pe.wait_ge(ea_in_sem[h], i * 16 + 16)
                    for j in range(h * HALF, (h + 1) * HALF):
                        pe.wait_ge(PL0.s_ready, i * U + j + 1)
                        pe.wait_ge(PL0.added, i * U + j + 1)
                        mm(acc_slot(j, P)[D:P], ea[:, j, :], S[:, j, :])
                        tile_landed(pe, PL0, i, j)
                        mm(acc_slot(j, P)[0:D], PL0.msg[:, j, :], S[:, j, :]).then_inc(PL0.summed, 1)
            barrier(pe, "pe")

            def loop_b(k, x, y):
                m = k - 1
                if x:
                    BX.after(pe, k, "act.uT<")
                    for a, b in halves():
                        last = mm(bank(0, b - a, a, D), w("we"), agg[:, bass.ds(k * NC + a, b - a)])
                    BX.done(last, "pe", "U")
                if y:
                    BY.after(pe, m, "dve.normed", "act.high<", "dve.rest1<")
                    BY.done(transposes(5, lambda c: hs[:, c, :], P, D), "pe", "HT")
                if x:
                    BX.after(pe, k, "act.uT", "act.zT<")
                    for a, b in halves():
                        last = mm(bank(2, b - a, a), w("w1"), uT[0:D, a:b])
                    BX.done(last, "pe", "Z")
                if y:
                    BY.after(pe, m, "act.hT")
                    for a, b in halves():
                        last = mm(bank(5, b - a, a), w("wa2"), hT[0:D, a:b])
                    BY.done(last, "pe", "APT")
                if x:
                    BX.after(pe, k, "act.zT", "dve.x<")
                    for c in range(C7):
                        last = mm(bank(4, D, c * D), zT[:, chunk(c)], w("w2"))
                    BX.done(last, "pe", "O")
                if y:
                    BY.after(pe, m, "act.tab<")
                    hold(pe)
                    for c in range(C7):
                        last = mm(bank(7, D, c * D), hT[0:D, chunk(c)], w("wb"))
                    BY.done(last, "pe", "TAB")

            skewed(pe, "pe", (BX, BY), loop_b)

            pe.sem_inc(PL1.summed, U)
            pe.sem_inc(pre_mm, 8)

            def windows(i, b, g):
                for j in range(4 * g, 4 * g + 4):
                    pe.wait_ge(PL1.s_ready, i * U + j + 1)
                    pe.wait_ge(win_sb, i * U + j + 3)
                    at = bass.ds(b[j - HALF] if b else base0[j], P)
                    mm(bank(j % 2, P), part_hm[:, at], ident_b[:, :])
                    mm(bank(j % 2, D, P), part_lo[:, at], ident_b[0:D, 0:D])
                    pe.transpose(bank(j % 2, P, 3 * D), S[:, j % U, :], w("ident")).then_inc(win_t, 1)

            def dst_terms(i, g):
                pe.wait_ge(PL1.used, i * 4 + g + 3)
                for j in range(4 * g, 4 * g + 4):
                    pe.wait_ge(win_sb, i * U + j + 5)
                    for k in range(3):
                        last = mm(bank(4 + g % 2, D, j % 4 * D), win[:, j % 8, 3 * D:WIN],
                                  win[:, j % 8, k * D:(k + 1) * D], start=k == 0, stop=k == 2)
                    last.then_inc(pre_mm, 1)

            def sums1(i, g):
                pe.wait_ge(relued, i * 4 + g + 3)
                sum_tiles(PL1, i, range(4 * g, 4 * g + 4), lambda j: msg1[:, j, :])

            _, base0 = nc.values_load_multi_w_load_instructions(
                base[0:1, 0:HALF], engines=[mybir.EngineType.PE], min_val=0, max_val=N,
                skip_runtime_bounds_check_because="dst holds node numbers below N, the padding N")
            windows(0, None, 0)
            windows(0, None, 1)
            dst_terms(0, 0)
            with pe.Fori(0, NIT) as i:
                _, b = nc.values_load_multi_w_load_instructions(
                    base[0:1, bass.ds(i * U + HALF, U)], engines=[mybir.EngineType.PE], min_val=0, max_val=N,
                    skip_runtime_bounds_check_because="dst holds node numbers below N, the padding N")
                for g in range(4):
                    dst_terms(i, g + 1)
                    sums1(i, g)
                    windows(i, b, g + 2)
            barrier(pe, "pe")

            def loop_c(k, x, y):
                m = k - 1
                if x:
                    CX.after(pe, k, "act.agT<")
                    for a, b in halves():
                        last = mm(bank(0, b - a, a, D + 1), w("wm2"), agg[0:D + 1, bass.ds(k * NC + a, b - a)])
                    CX.done(last, "pe", "AG")
                    CX.after(pe, k, "act.hc")
                    if y:
                        CY.after(pe, m, "act.hT<")
                    CX.done(transposes(2, lambda c: hc[:, c, :], P, D), "pe", "H1T")
                    CX.after(pe, k, "act.agT", "dve.deg<")
                    hold(pe)
                    for c in range(C7):
                        last = pe.transpose(bank(7, D + 1, c * (D + 1)), uT[0:D + 1, chunk(c)],
                                            w("ident")[0:D + 1, 0:D + 1])
                    CX.done(last, "pe", "DEG")
                    CX.after(pe, k, "act.h1T", "act.rT<")
                    if y:
                        CY.after(pe, m, "act.tab<", "dve.diff<")
                    hold(pe)
                    for a, b in halves():
                        mm(bank(4, b - a, a, D), w("wu1a"), r1[0:D, a:b], stop=False)
                        last = mm(bank(4, b - a, a, D), w("wu1b"), uT[0:D, a:b], start=False)
                    CX.done(last, "pe", "RU")
                if y:
                    CY.after(pe, m, "dve.normed")
                    CX.after(pe, k if x else m, "act.h1T")
                    CY.done(transposes(2, lambda c: hs[:, c, :], P, D), "pe", "HT")
                if x:
                    CX.after(pe, k, "act.rT", "dve.v<")
                    for c in range(C7):
                        last = mm(bank(6, D, c * D), zT[0:D + 1, chunk(c)], w("wu2"))
                    CX.done(last, "pe", "O")
                if y:
                    CY.after(pe, m, "act.hT")
                    if x:
                        CX.after(pe, k, "act.rT")
                    for c in range(C7):
                        last = mm(bank(4, H, c * H), hT[0:D + 1, chunk(c)], w("thph"))
                    CY.done(last, "pe", "THPH")

            skewed(pe, "pe", (CX, CY), loop_c)

            pe.sem_inc(PL2.used, U)
            pe.sem_inc(PL2.summed, U)
            pe.sem_inc(back_t, 2)

            def forth(i, g):
                pe.wait_ge(scanned, i * 4 + g + 3)
                for j in range(4 * g, 4 * g + 4):
                    tile_landed(pe, PL2, i, j)
                    hold(pe)
                    pe.transpose(bank(g % 2, P, j % 4 * P, D), PL2.msg[:, j, :], w("ident")).then_inc(PL2.used, 1)

            def back_and_sums(i, g):
                pe.wait_ge(scanned, i * 4 + g + 5)
                pe.wait_ge(back_sb, i * 4 + g + 1)
                hold(pe)
                for j in range(4):
                    last = pe.transpose(bank(4 + g % 2, D, j * D), run[:, g % 2, j * P:(j + 1) * P],
                                        w("ident")[0:D, 0:D])
                last.then_inc(back_t, 1)
                pe.wait_ge(back_sb, i * 4 + g + 3)
                sum_tiles(PL2, i, range(4 * g, 4 * g + 4), lambda j: back[:, g % 2, j % 4 * D:(j % 4 + 1) * D])

            def group2(i, g, back=True):
                forth(i, g)
                if back:
                    back_and_sums(i if g else i - 1, (g - 1) % 4)

            for g in range(4):
                group2(0, g, back=g > 0)
            with pe.Fori(1, NIT) as i:
                for g in range(4):
                    group2(i, g)
            back_and_sums(NIT - 1, 3)
            barrier(pe, "pe")

            def loop_d(k, x, y):
                m = k - 1
                if x:
                    DX.after(pe, k, "act.aggc", "dve.y<")
                    hold(pe)
                    for c in range(C7):
                        last = pe.transpose(bank(0, D, c * D), aggc[0:D, chunk(c)], w("ident")[0:D, 0:D])
                    DX.done(last, "pe", "T")
                if y:
                    DY.after(pe, m, "dve.normed", "act.hT<")
                    DY.done(transposes(2, lambda c: hs[:, c, :], P, D), "pe", "HT")
                    DY.after(pe, m, "act.hT", "act.self<")
                    for c in range(C7):
                        last = mm(bank(4, H, c * H), hT[0:D + 1, chunk(c)], w("ws0"))
                    DY.done(last, "pe", "SELF")

            skewed(pe, "pe", (DX, DY), loop_d)

            def sage_pass(ps):
                pe.sem_inc(ps.summed, U)
                with pe.Fori(0, NIT) as i:
                    sum_tiles(ps, i, range(U), lambda j: ps.msg[:, j, :], waits=lambda j: tile_landed(pe, ps, i, j))
                barrier(pe, "pe")

            sage_pass(PL3a)
            def loop_e(k, x, y):
                m = k - 1
                if x:
                    EX.after(pe, k, "act.aggc", "dve.mean<")
                    for c in range(C7):
                        last = mm(bank(0, H, c * H), aggc[0:D, chunk(c)], w("wn0"))
                    EX.done(last, "pe", "M")
                if y:
                    EY.after(pe, m, "act.z", "act.zT<")
                    EY.done(transposes(2, lambda c: zr[:, c, :], P, H), "pe", "ZT")
                    EY.after(pe, m, "act.zT", "dve.self<")
                    for c in range(C7):
                        last = mm(bank(4, H, c * H), zT3[:, chunk(c)], w("ws1"))
                    EY.done(last, "pe", "SELF")

            skewed(pe, "pe", (EX, EY), loop_e)

            sage_pass(PL3b)
            def loop_f(k, x, y):
                m = k - 1
                if x:
                    FX.after(pe, k, "act.aggc", "dve.mean<")
                    for c in range(C7):
                        last = mm(bank(0, H, c * H), aggc[:, chunk(c)], w("wn1"))
                    FX.done(last, "pe", "M")
                if y:
                    FY.after(pe, m, "act.z", "act.zT<")
                    FY.done(transposes(2, lambda c: zr[:, c, :], P, H), "pe", "ZT")
                    FY.after(pe, m, "act.zT", "act.tab<", "dve.self<")
                    for c in range(C7):
                        last = mm(bank(4, H, c * H), zT3[:, chunk(c)], w("wns2"))
                    FY.done(last, "pe", "BOTH")

            skewed(pe, "pe", (FX, FY), loop_f)

            sage_pass(PL3c)
            GX.start(pe, "pe")
            with pe.Fori(0, NLOOP) as i:
                GX.after(pe, i, "act.aggc", "dve.mean<")
                hold(pe)
                for c in range(C7):
                    last = pe.transpose(bank(0, D, c * D), aggc[0:D, chunk(c)], w("ident")[0:D, 0:D])
                GX.done(last, "pe", "T")
            barrier(pe, "pe")


def kernel(x, src, dst, edge_attr_16, edge_attr_64, L0_gnn_We_w, L0_gnn_We_b, L0_gnn_eps, L0_gnn_W1, L0_gnn_b1,
           L0_gnn_W2, L0_gnn_b2, L1_gnn_W_m1, L1_gnn_b_m1, L1_gnn_W_m2, L1_gnn_b_m2, L1_gnn_W_u1, L1_gnn_b_u1,
           L1_gnn_W_u2, L1_gnn_b_u2, L1_gnn_gamma, L1_gnn_beta, L2_gnn_theta_w, L2_gnn_theta_b, L2_gnn_phi_w,
           L2_gnn_phi_b, L3_gnn_ws0, L3_gnn_wn0, L3_gnn_b0, L3_gnn_ws1, L3_gnn_wn1, L3_gnn_b1, L3_gnn_ws2,
           L3_gnn_wn2, L3_gnn_b2):
    import concourse.bacc as bacc
    from concourse.bass_utils import run_bass_kernel_spmd

    a = np.asarray
    pad = NT * P - E

    def tiles(v):
        return np.ascontiguousarray(v.reshape(NT, P).T)

    def rows(v):
        return np.ascontiguousarray(v.reshape(NT // P, P, P).transpose(1, 0, 2).reshape(P, NT))

    src_p = np.pad(a(src), (0, pad))
    dst_p = np.pad(a(dst), (0, pad), constant_values=N)
    next_p = np.concatenate([dst_p[1:], np.full(1, -1, dst_p.dtype)])
    prev_p = np.concatenate([np.full(1, -1, dst_p.dtype), dst_p[:-1]])
    x_p = np.pad(a(x), ((0, ROWS - N), (0, 0))).reshape(CHUNKS, P, D).transpose(1, 0, 2).reshape(P, CHUNKS * D)
    ea_p = np.pad(a(edge_attr_64), ((0, pad), (0, 0))).reshape(NT // HALF, HALF, P, D).transpose(0, 2, 1, 3)
    ef_p = np.pad(a(edge_attr_16), ((0, pad), (0, 0))).T

    eye = np.eye(P, dtype=np.float32)
    row = lambda v: a(v).reshape(1, -1)
    col = lambda v: a(v).reshape(-1, 1)
    every = lambda v, c: np.broadcast_to(a(v).reshape(1, -1), (P, c))
    wm1 = a(L1_gnn_W_m1)
    wm2 = np.zeros((D + 1, D + 1), np.float32)
    wm2[0:D, 0:D], wm2[D, 0:D], wm2[D, D] = a(L1_gnn_W_m2), a(L1_gnn_b_m2), 1.0
    parts = dict(
        ident=eye, iota=np.broadcast_to(np.arange(P, dtype=np.float32), (P, P)),
        we=np.concatenate([eye[0:D, 0:D], a(L0_gnn_We_w)]), w1=a(L0_gnn_W1), b1=col(L0_gnn_b1), w2=a(L0_gnn_W2),
        b2=every(L0_gnn_b2, D), we_b=every(L0_gnn_We_b, D), eps=every(L0_gnn_eps, 1),
        wa2=np.concatenate([wm1[0:D], wm1[0:D]], axis=1), wb=wm1[D:2 * D],
        wc=np.concatenate([wm1[2 * D:], row(L1_gnn_b_m1)]), wm2=wm2,
        wu1a=a(L1_gnn_W_u1)[0:D], wu1b=a(L1_gnn_W_u1)[D:], bu1=col(L1_gnn_b_u1),
        wu2=np.concatenate([a(L1_gnn_W_u2), row(L1_gnn_b_u2)]),
        gamma=every(L1_gnn_gamma, D), beta=every(L1_gnn_beta, D),
        thph=np.block([[a(L2_gnn_theta_w).T, a(L2_gnn_phi_w).T], [row(L2_gnn_theta_b), row(L2_gnn_phi_b)]]),
        ws0=np.concatenate([a(L3_gnn_ws0), row(L3_gnn_b0)]), wn0=a(L3_gnn_wn0), ws1=a(L3_gnn_ws1),
        sb1=every(L3_gnn_b1, H), wn1=a(L3_gnn_wn1), wns2=np.concatenate([a(L3_gnn_wn2), a(L3_gnn_ws2)], axis=1),
        sb2=every(L3_gnn_b2, D), zero=np.zeros((P, 1), np.float32))
    pack = np.zeros((P, WCOLS), np.float32)
    for name, (r, c) in PACK.items():
        pack[0:r, AT[name]:AT[name] + c] = parts[name]

    arrays = dict(x_nm_in=np.ascontiguousarray(x_p), src_in=tiles(src_p), dst_in=tiles(dst_p),
                  next_in=tiles(next_p), dstrow_in=rows(dst_p), prevrow_in=rows(prev_p),
                  ea_in=np.ascontiguousarray(ea_p.reshape(NT // HALF * P, HALF * D)),
                  ef_in=np.ascontiguousarray(ef_p), pack_in=pack)
    nc = bacc.Bacc("TRN2", target_bir_lowering=False, num_devices=1)
    args = [nc.dram_tensor(n, v.shape, mybir.dt.from_np(v.dtype), kind="ExternalInput").ap()
            for n, v in arrays.items()]
    out = nc.dram_tensor("x_out", (P, CHUNKS * D), F32, kind="ExternalOutput").ap()
    gnn(nc, *args, out)
    r = run_bass_kernel_spmd(nc, [arrays], core_ids=[0])
    y = np.asarray(r.results[0]["x_out"]).reshape(P, CHUNKS, D).transpose(1, 0, 2).reshape(ROWS, D)
    return np.ascontiguousarray(y[0:N])
```

```python
import numpy as np
import concourse.bass as bass
from concourse import mybir
from contextlib import ExitStack

N = 12500
E = 212500
D = 64
H = 128
P = 128
LN_EPS = 1e-5

U = 16
HALF = U // 2
NT = -(-E // (P * U)) * U
NIT = NT // U
CHUNKS = -(-N // P)
ROWS = CHUNKS * P
COLS = ROWS + P
C7 = 7
NLOOP = CHUNKS // C7
NC = C7 * P
NF = C7 * D
assert C7 * NLOOP == CHUNKS

F32 = mybir.dt.float32
BF16 = mybir.dt.bfloat16
I32 = mybir.dt.int32
ALU = mybir.AluOpType
ACT = mybir.ActivationFunctionType
AX = mybir.AxisListType

PACK = dict(ident=(128, 128), iota=(128, 128), we=(128, 64), w1=(64, 128), b1=(128, 1), w2=(128, 64), b2=(128, 64),
            we_b=(128, 64), eps=(128, 1), wa2=(64, 128), wb=(64, 64), wc=(17, 64), wm2t=(64, 65),
            wu1a=(64, 64), wu1b=(64, 64), bu1=(64, 1), wu2=(65, 64), gamma=(128, 64),
            beta=(128, 64), thph=(65, 128), ws0=(65, 128), wn0=(64, 128), ws1=(128, 128),
            sb1=(128, 128), wn1=(128, 128), wns2=(128, 128), sb2=(128, 64), zero=(128, 1))
AT = {}
WCOLS = 0
for _name, (_rows, _cols) in PACK.items():
    AT[_name] = WCOLS
    WCOLS += _cols


def gnn(nc, x_in, src_in, dst_in, next_in, dstrow_in, prevrow_in, ea_in, ef_in, pack_in, out):
    ctx = ExitStack()
    with ctx:
        def sb(name, shape, dt=F32):
            return ctx.enter_context(nc.sbuf_tensor(name, shape, dt))

        def sem(name):
            return ctx.enter_context(nc.semaphore(name))

        widths = [D, D, D, D, H, D]
        table = [nc.dram_tensor(f"table{k}", (ROWS, w), F32).ap() for k, w in enumerate(widths)]
        table_nm = [t.rearrange("(p c) f -> p (c f)", p=P) for t in table]
        ew_dram = nc.dram_tensor("edge_term", (NT // HALF * P, HALF * D), F32).ap()
        mask_dram = nc.dram_tensor("scan_mask", (1, NT * P), BF16).ap()

        agg = sb("agg", [P, COLS])
        big = sb("big", [P, COLS])
        part_hm = big[:, 0:COLS // 2].bitcast(BF16)
        part_lo = big[0:D, COLS // 2:COLS].bitcast(BF16)
        x_nm = sb("x_nm", [P, CHUNKS * D])
        h_nm = sb("h_nm", [P, CHUNKS * D])
        src_idx = sb("src_idx", [P, NT + U], I32)
        base = sb("base", [1, NT + HALF], I32)
        rel = sb("rel", [P, NT + HALF], BF16)
        rel_end = sb("rel_end", [P, NT + HALF], BF16)
        deg = sb("deg", [P, CHUNKS])
        rdeg = sb("rdeg", [P, CHUNKS, 1])
        no_in = sb("no_in", [P, CHUNKS, 1])
        idxw = sb("idxw", [P, U], I32)
        W = sb("W", [P, WCOLS])
        one_eps = sb("one_eps", [P, 1])
        ident_b = sb("ident_b", [P, P], BF16)
        stat = sb("stat", [P, 4, C7, 1])
        stat1 = sb("stat1", [P, 4, C7, 1])
        wcomb = sb("wcomb", [D + 1, D])
        AR = 7168
        arena = sb("arena", [P, AR])
        PS = ctx.enter_context(nc.psum_tensor("PS", [P, 8 * 512], F32))

        def w(name):
            r, c = PACK[name]
            return W[0:r, AT[name]:AT[name] + c]

        def carve(*sizes):
            at, got = 0, []
            for s in sizes:
                got.append(arena[:, at:at + s])
                at += s
            assert at <= AR, at
            return got

        def bank(b, n=512, o=0, rows=P):
            return PS[0:rows, b * 512 + o:b * 512 + o + n]

        def n3(ap):
            return ap.rearrange("p (c f) -> p c f", c=C7)

        msg_f, rest, S_f = arena[:, 0:U * H], arena[:, U * D:AR - U * P], arena[:, AR - U * P:AR]
        S = S_f.rearrange("p (t w) -> p t w", t=U)

        gathered = [sem(f"gathered{j}") for j in range(U)]
        phase = sem("phase")
        phases = dict(sp=0, act=0, pool=0, dve=0, pe=0)

        def hold(eng):
            eng.nop(nofuse=True)

        def barrier(eng, who):
            phases[who] += 1
            eng.drain().then_inc(phase, 1)
            eng.wait_ge(phase, 5 * phases[who])

        class Pass:

            def __init__(self, k, name, rows):
                self.k, self.rows, self.width = k, rows, widths[k]
                self.msg = (msg_f[:, 0:U * self.width]).rearrange("p (t f) -> p t f", t=U)
                self.idx_ready = sem(f"{name}_idx_ready")
                self.s_ready = sem(f"{name}_s_ready")
                self.summed = sem(f"{name}_summed")
                self.used = self.summed
                self.added = sem(f"{name}_added")

        PL0, PL1, PL2, PL3a, PL3b, PL3c = (Pass(k, n, r) for k, (n, r) in enumerate(
            [("l0", P), ("l1", D + 1), ("l2", D), ("l3a", D), ("l3b", H), ("l3c", D)]))
        PL1.used = sem("l1_used")
        PL2.used = sem("l2_used")

        def acc_slot(T, rows):
            return bank((2, 3, 6, 7)[T % 4], P, 0, rows)

        def pool_gathers(pool, ps, used, unit):
            n, q = U // unit, 4 // unit
            with pool.Fori(0, NIT) as i:
                for g in range(4):
                    pool.wait_ge(used, i * n + (g + 1) * q)
                    if g % 2 == 0:
                        pool.wait_ge(ps.idx_ready, i * 2 + g // 2 + 1)
                    hold(pool)
                    for j in range(4 * g, 4 * g + 4):
                        pool.indirect_dma_start(
                            out=ps.msg[:, j, :], out_offset=None, in_=table[ps.k],
                            in_offset=bass.IndirectOffsetOnAxis(ap=idxw[:, j:j + 1], axis=0)
                        ).then_inc(gathered[j], 16)

        def act_idx(act, ps, col, half):
            act.activation(idxw[:, half * HALF:(half + 1) * HALF], src_idx[:, bass.ds(col, HALF)],
                           ACT.Copy).then_inc(ps.idx_ready, 1)

        def tile_landed(eng, ps, i, j):
            eng.wait_ge(gathered[j], i * 16 + (ps.k * NIT + 1) * 16)

        def half_landed(eng, ps, i, half):
            for j in range(half * HALF, (half + 1) * HALF):
                tile_landed(eng, ps, i, j)

        def dve_bases(columns):
            _, b = nc.values_load_multi_w_load_instructions(
                base[0:1, columns], engines=[mybir.EngineType.DVE], min_val=0, max_val=N,
                skip_runtime_bounds_check_because="dst holds node numbers below N, the padding N")
            return b

        def dve_s(dve, ps, i, column, js):
            for j in js:
                dve.tensor_scalar(out=S[:, j % U, :], in0=w("iota"), scalar1=column[:, bass.ds(i * U + j, 1)],
                                  scalar2=None, op0=ALU.is_equal).then_inc(ps.s_ready, 1)

        def dve_add(dve, ps, b, i, js, first=0):
            for j in js:
                dve.wait_ge(ps.summed, i * U + j + 1 + U)
                dve.wait_ge(ps.added, i * U + j + 4)
                win = agg[0:ps.rows, bass.ds(b[first + j], P)]
                dve.tensor_tensor(out=win, in0=acc_slot(j, ps.rows), in1=win, op=ALU.add).then_inc(ps.added, 1)

        ea_in_sem = [sem(f"ea_loaded{h}") for h in range(2)]
        ef_in_sem = [sem(f"ef_loaded{h}") for h in range(2)]
        ew_mm = sem("ew_mm")
        ew_sb = sem("ew_sb")
        ew_stored = sem("ew_stored")
        ew_free = sem("ew_free")
        ew_in_sem = [sem(f"ew_loaded{h}") for h in range(2)]
        win_t = sem("win_t")
        win_sb = sem("win_sb")
        pre_mm = sem("pre_mm")
        pre_ew = sem("pre_ew")
        relued = sem("relued")
        mask_in_sem = [sem(f"mask_loaded{h}") for h in range(2)]
        scanned = sem("scanned")
        back_t = sem("back_t")
        back_sb = sem("back_sb")
        s_load_x = sem("s_load_x")
        s_load = sem("s_load")
        s_comb = sem("s_comb")
        out_stored = sem("out_stored")
        s_setup = sem("s_setup")
        s_mask = sem("s_mask")
        s_zero = sem("s_zero")
        s_ones = sem("s_ones")

        ea_f, ef_f, ews_f = rest[:, 0:U * D], rest[:, U * D:3 * U * D], rest[:, 3 * U * D:4 * U * D]
        ea = ea_f.rearrange("p (t f) -> p t f", t=U)
        ef = ef_f.rearrange("p (h e) -> p h e", h=2)
        ews = ews_f.rearrange("p (h f) -> p h f", h=2)
        WIN = 3 * D + P
        at_l1 = [0, U * D, U * D + 4 * WIN, U * D + 4 * WIN + 8 * D, U * D + 4 * WIN + 8 * D + U * (D + 1)]
        ewl = rest[:, at_l1[0]:at_l1[1]].rearrange("p (h f) -> p h f", h=2)
        win = rest[:, at_l1[1]:at_l1[2]].bitcast(BF16).rearrange("p (t f) -> p t f", t=8)
        pre = rest[:, at_l1[2]:at_l1[3]].rearrange("p (g f) -> p g f", g=2)
        msg1 = rest[:, at_l1[3]:at_l1[4]].rearrange("p (t f) -> p t f", t=U)
        mask_f = h_nm[:, 2 * NT:2 * NT + NT // 2].bitcast(BF16)
        at_l2 = [0, U * P // 2, U * P // 2 + 8 * P, U * P // 2 + 8 * P + 8 * D]
        mask = rest[0:D, at_l2[0]:at_l2[1]].bitcast(BF16).rearrange("p (h e) -> p h e", h=2)
        run = rest[0:D, at_l2[1]:at_l2[2]].rearrange("p (g e) -> p g e", g=2)
        back = rest[:, at_l2[2]:at_l2[3]].rearrange("p (g f) -> p g f", g=2)

        class Stage:

            def __init__(self, name, **steps):
                self.steps = {who: names.split() for who, names in steps.items()}
                self.sem = {who: sem(f"{name}_{who}") for who in steps}
                self.told = {who: 0 for who in steps}

            def start(self, eng, who):
                if who in self.sem:
                    eng.sem_inc(self.sem[who], len(self.steps[who]))

            def done(self, ins, who, name):
                names = self.steps[who]
                assert names[self.told[who] % len(names)] == name, (who, name)
                self.told[who] += 1
                ins.then_inc(self.sem[who], 1)

            def after(self, eng, i, *whos):
                for what in whos:
                    who, name = what.rstrip("<").split(".")
                    k = len(self.steps[who])
                    ahead = 0 if what.endswith("<") else k
                    eng.wait_ge(self.sem[who], i * k + ahead + self.steps[who].index(name) + 1)

        def skewed(eng, who, stages, body, count=NLOOP):
            n = len(stages)
            for stage in stages:
                stage.start(eng, who)
            for k in range(n - 1):
                body(k, *(k - j >= 0 for j in range(n)))
            with eng.Fori(n - 1, count) as k:
                body(k, *[True] * n)
            for k in range(count, count + n - 1):
                body(k, *(k - j < count for j in range(n)))
            barrier(eng, who)

        NORM = "{0}sum {0}centred {0}sumsq {0}var {0}rstd {0}normed"
        AX0 = Stage("ax0", dve=NORM.format("") + " tab", act="squared std")
        AX1 = Stage("ax1", dve=NORM.format("") + " tab", act="squared std", sp="stored")
        AY = Stage("ay", pe="HT0 HT1", act="hT0 hT1")
        BX = Stage("bx", pe="U Z O", act="uT zT", dve="bias x", pool="zero")
        BY = Stage("by", pe="HT APT TAB", act="squared std hT high tab", dve=NORM.format(""), pool="h", sp="stored")
        BZ = Stage("bz", act="mid midlow", dve="rest1", pool="lo")
        CX = Stage("cx", pe="H1T RU DEG O", act="hc agT h1T rT vsquared vstd",
                   dve="deg v " + NORM.format("v") + " scaled shifted x", pool="zero")
        CY = Stage("cy", pe="HT THPH", act="squared std hT", dve=NORM.format(""))
        CZ = Stage("cz", act="tab", dve="diff", sp="stored")
        DX = Stage("dx", pe="T", act="aggc", dve="zero y keep kept x", pool="zero")
        DY = Stage("dy", pe="HT SELF", act="squared std hT", dve=NORM.format(""), sp="stored")
        DZ = Stage("dz", act="self")
        EX = Stage("ex", pe="M", act="aggc", dve="mean sum", pool="zero")
        EY = Stage("ey", pe="ZT SELF", act="z zT", dve="self", sp="stored")
        FX = Stage("fx", pe="M", act="aggc", dve="mean sum", pool="zero")
        FY = Stage("fy", pe="ZT BOTH", act="z zT")
        FZ = Stage("fz", act="tab", dve="self", sp="stored")
        GX = Stage("gx", pe="T", act="aggc", dve="mean sum x")

        (hc_f, uT, zT, xc_f, sq_f, hs_f, hT, tb_f, v_f, r1, mid_f) = carve(
            NF, NC, NC, NF, NF, NF, NC, NF, NF, NC, NC // 2)
        hc, xc, sq, hs, tb, vv = (n3(a) for a in (hc_f, xc_f, sq_f, hs_f, tb_f, v_f))
        mid = mid_f[0:D].bitcast(BF16)
        a_xc, a_sq, a_hs, a_tb = (a.rearrange("p (h c f) -> p h c f", h=2, c=C7) for a in carve(*[2 * NF] * 4))
        a_tb_f = arena[:, 6 * NF:8 * NF]
        aggc, z_f, zr_f, zT3, kept = uT, r1, zT, hT, zT[:, 0:NF]
        zr = zr_f.rearrange("p (c f) -> p c f", c=C7)

        def nf(i):
            return bass.ds(i * NF, NF)

        def ncol(i):
            return bass.ds(i * NC, NC)

        def halves():
            return [(0, 512), (512, NC)]

        def chunk(c, n=P):
            return slice(c * n, (c + 1) * n)

        block = ctx.enter_context(nc.Block())

        @block.sync
        def _(sp):
            sp.dma_start(W[:, :], pack_in).then_inc(s_load_x, 16)
            sp.dma_start(x_nm[:, :], x_in).then_inc(s_load_x, 16)
            sp.dma_start(src_idx[:, 0:NT], src_in).then_inc(s_load, 16)
            sp.dma_start(base[:, 0:NT], dst_in[0:1, :]).then_inc(s_load, 16)
            for k, a in enumerate((dst_in, next_in, dstrow_in, prevrow_in, dst_in[0:1, :].to_broadcast([P, NT]))):
                sp.dma_start(big[:, k * NT:(k + 1) * NT].bitcast(I32), a).then_inc(s_load, 16)
            barrier(sp, "sp")

            def store_loop(lp, what, src, dst, n, count=NLOOP):
                with sp.Fori(0, count) as i:
                    lp.after(sp, i, what)
                    sp.dma_start(dst[:, bass.ds(i * n, n)], src).then_inc(s_tab[lp], 16)
                    sp.wait_ge(s_tab[lp], i * 16 + 16)
                    sp.sem_inc(lp.sem["sp"], 1)

            s_tab = {lp: sem(f"rows_stored{n}") for n, lp in enumerate((AX1, BY, CZ, DY, EY, FZ))}
            for lp in s_tab:
                lp.start(sp, "sp")
            store_loop(AX1, "dve.tab", a_tb_f, table_nm[0], 2 * NF, NLOOP // 2)
            barrier(sp, "sp")

            def attributes_in(i, h):
                sp.wait_ge(PL0.summed, i * U + (h + 1) * HALF)
                sp.dma_start(ea_f[:, h * HALF * D:(h + 1) * HALF * D],
                             ea_in[bass.ds((i * 2 + h) * P, P), :]).then_inc(ea_in_sem[h], 16)
                sp.dma_start(ef[0:16, h, :], ef_in[:, bass.ds((i * 2 + h) * HALF * P, HALF * P)]
                             ).then_inc(ef_in_sem[h], 16)

            def terms_out(i, h):
                sp.wait_ge(ew_sb, i * 2 + h + 3)
                sp.dma_start(ew_dram[bass.ds((i * 2 + h) * P, P), :], ews[:, h, :]).then_inc(ew_stored, 16)
                sp.wait_ge(ew_stored, i * 32 + h * 16 + 16)
                sp.sem_inc(ew_free, 1)

            sp.wait_ge(s_ones, 1)
            attributes_in(0, 0)
            attributes_in(0, 1)
            sp.wait_ge(s_mask, 1)
            sp.dma_start(mask_dram[0, :].rearrange("(c q e) -> q c e", q=P, e=P),
                         mask_f.rearrange("q (c e) -> q c e", e=P)).then_inc(s_mask, 16)
            sp.wait_ge(s_mask, 17)
            terms_out(0, 0)
            with sp.Fori(1, NIT) as i:
                attributes_in(i, 0)
                terms_out(i - 1, 1)
                attributes_in(i, 1)
                terms_out(i, 0)
            terms_out(NIT - 1, 1)
            barrier(sp, "sp")
            store_loop(BY, "act.tab", tb_f, table_nm[1], NF)
            barrier(sp, "sp")

            with sp.Fori(0, NIT) as i:
                for h in range(2):
                    sp.wait_ge(PL1.used, i * 4 + h * 2 + 2)
                    sp.dma_start(ewl[:, h, :], ew_dram[bass.ds((i * 2 + h) * P, P), :]).then_inc(ew_in_sem[h], 16)
            barrier(sp, "sp")
            store_loop(CZ, "act.tab", tb_f, table_nm[2], NF)
            barrier(sp, "sp")

            with sp.Fori(0, NIT) as i:
                for h in range(2):
                    sp.wait_ge(scanned, i * 4 + h * 2 + 2)
                    sp.dma_start(mask[:, h, :], mask_dram[0:1, bass.ds((i * 2 + h) * HALF * P, HALF * P)]
                                 .to_broadcast([D, HALF * P])).then_inc(mask_in_sem[h], 16)
            barrier(sp, "sp")
            store_loop(DY, "dve.normed", hs_f, table_nm[3], NF)
            barrier(sp, "sp")
            barrier(sp, "sp")
            store_loop(EY, "act.z", zr_f, table_nm[4], NC)
            barrier(sp, "sp")
            barrier(sp, "sp")
            store_loop(FZ, "act.tab", tb_f, table_nm[5], NF)
            barrier(sp, "sp")
            barrier(sp, "sp")
            with sp.Fori(0, NLOOP) as i:
                GX.after(sp, i, "dve.x")
                sp.dma_start(out[:, nf(i)], x_nm[:, nf(i)]).then_inc(out_stored, 16)
            sp.wait_ge(out_stored, 16 * NLOOP)
            barrier(sp, "sp")

        @block.gpsimd
        def _(pool):
            pool.memset(src_idx[:, NT:NT + U], 0).then_inc(s_zero, 1)
            pool.memset(base[:, NT:NT + HALF], 0).then_inc(s_zero, 1)
            pool.memset(rel[:, NT:NT + HALF], 0.0).then_inc(s_zero, 1)
            pool.memset(rel_end[:, NT:NT + HALF], 0.0).then_inc(s_zero, 1)
            pool.wait_ge(s_zero, 4)
            pool.memset(agg[D:P, :], 0.0).then_inc(s_zero, 1)
            pool.memset(agg[0:D, ROWS:COLS], 0.0).then_inc(s_zero, 1)
            pool.wait_ge(s_zero, 6)
            barrier(pool, "pool")

            def keep_h(stage, i):
                stage.after(pool, i, "pool.h<", "dve.normed")
                stage.done(pool.tensor_copy(h_nm[:, nf(i)], hs_f), "pool", "h")

            def zeros(stage, i, *consumers):
                stage.after(pool, i, *consumers)
                stage.done(pool.tensor_copy(agg[:, ncol(i)], w("zero").to_broadcast([P, NC])), "pool", "zero")

            barrier(pool, "pool")

            def loop_b(k, x, y, z):
                if x:
                    zeros(BX, k, "pe.U")
                if y:
                    keep_h(BY, k - 1)
                if z:
                    BZ.after(pool, k - 2, "act.midlow")
                    BZ.done(pool.tensor_tensor(part_lo[:, ncol(k - 2)], r1[0:D], mid, ALU.subtract), "pool", "lo")

            def zero_loop(stage, *consumers):
                stage.start(pool, "pool")
                with pool.Fori(0, NLOOP) as i:
                    zeros(stage, i, *consumers)
                barrier(pool, "pool")

            pool_gathers(pool, PL0, PL0.used, 1)
            barrier(pool, "pool")
            skewed(pool, "pool", (BX, BY, BZ), loop_b)
            pool_gathers(pool, PL1, PL1.used, 4)
            barrier(pool, "pool")
            zero_loop(CX, "pe.RU", "act.agT")
            pool_gathers(pool, PL2, PL2.used, 1)
            barrier(pool, "pool")
            zero_loop(DX, "act.aggc")
            pool_gathers(pool, PL3a, PL3a.used, 1)
            barrier(pool, "pool")
            zero_loop(EX, "act.aggc")
            pool_gathers(pool, PL3b, PL3b.used, 1)
            barrier(pool, "pool")
            zero_loop(FX, "act.aggc")
            pool_gathers(pool, PL3c, PL3c.used, 1)
            barrier(pool, "pool")
            barrier(pool, "pool")

        @block.scalar
        def _(act):
            def copy(lp, i, name, dst, src, *waits, func=ACT.Copy, **kw):
                lp.after(act, i, *waits)
                lp.done(act.activation(dst, src, func, **kw), "act", name)

            def norm_parts(lp, i, pre=""):
                copy(lp, i, pre + "squared", sq_f, xc_f, f"dve.{pre}centred", func=ACT.Square)
                copy(lp, i, pre + "std", stat[:, 3], stat[:, 2], f"dve.{pre}var", func=ACT.Sqrt)

            def sum_pass(ps):
                act_idx(act, ps, 0, 0)
                with act.Fori(0, NIT) as i:
                    act.wait_ge(ps.used, i * U + U)
                    act_idx(act, ps, i * U + HALF, 1)
                    act.wait_ge(ps.used, i * U + HALF + U)
                    act_idx(act, ps, i * U + U, 0)
                barrier(act, "act")

            barrier(act, "act")
            def loop_a(k, x, y):
                if x:
                    for h, lp in enumerate((AX0, AX1)):
                        copy(lp, k, "squared", a_sq[:, h], a_xc[:, h], "dve.centred", func=ACT.Square)
                    copy(AX0, k, "std", stat[:, 3], stat[:, 2], "dve.var", func=ACT.Sqrt)
                    copy(AX1, k, "std", stat1[:, 3], stat1[:, 2], "dve.var", func=ACT.Sqrt)
                if y:
                    for h in range(2):
                        copy(AY, k - 1, f"hT{h}", agg[0:D, ncol((k - 1) * 2 + h)], bank(2 * h, NC, rows=D),
                             f"pe.HT{h}", scale=one_eps[0:D, :])

            AX0.start(act, "act")
            skewed(act, "act", (AX1, AY), loop_a, NLOOP // 2)

            def store_terms(i, h):
                act.wait_ge(ew_mm, i * 2 + h + 1)
                act.wait_ge(ew_free, i * 2 + h + 1)
                act.activation(ews[:, h, :], bank(4 + h), ACT.Copy).then_inc(ew_sb, 1)

            act.sem_inc(ew_sb, 2)
            act_idx(act, PL0, 0, 0)
            with act.Fori(0, NIT) as i:
                act.wait_ge(PL0.used, i * U + U)
                act_idx(act, PL0, i * U + HALF, 1)
                store_terms(i, 0)
                act.wait_ge(PL0.used, i * U + HALF + U)
                act_idx(act, PL0, i * U + U, 0)
                store_terms(i, 1)
            barrier(act, "act")

            def loop_b(k, x, y, z):
                m = k - 1
                if y:
                    copy(BY, m, "squared", sq_f, xc_f, "dve.centred", func=ACT.Square)
                if x:
                    copy(BX, k, "uT", uT[0:D], bank(0, NC, rows=D), "pe.U", "pe.Z<")
                if y:
                    copy(BY, m, "std", stat[:, 3], stat[:, 2], "dve.var", func=ACT.Sqrt)
                if x:
                    copy(BX, k, "zT", zT, bank(2, NC), "pe.Z", "pe.O<", func=ACT.Relu, bias=w("b1"))
                if z:
                    copy(BZ, m - 1, "mid", part_hm[D:P, ncol(m - 1)], r1[D:P], "dve.rest1")
                    copy(BZ, m - 1, "midlow", mid, r1[0:D], "pool.lo<")
                if y:
                    copy(BY, m, "hT", hT[0:D], bank(5, NC, rows=D), "pe.HT", "pe.TAB<")
                    copy(BY, m, "high", part_hm[:, ncol(m)], bank(5, NC), "pe.APT")
                    copy(BY, m, "tab", tb_f, bank(7, NF), "pe.TAB", "sp.stored<")

            skewed(act, "act", (BX, BY, BZ), loop_b)

            act.sem_inc(win_sb, 4)
            act.sem_inc(relued, 2)

            def win_copy(i, g):
                for j in range(4 * g, 4 * g + 4):
                    act.wait_ge(win_t, i * U + j + 1)
                    act.wait_ge(pre_mm, i * U + j + 1)
                    act.activation(win[:, j % 8, :], bank(j % 2, WIN), ACT.Copy).then_inc(win_sb, 1)

            def relu_sums(i, g):
                act.wait_ge(PL1.used, i * 4 + g + 5)
                act.wait_ge(PL1.summed, i * U + 4 * g + 4)
                act.activation(msg1[:, 4 * g:4 * g + 4, 0:D],
                               pre[:, g % 2, :].rearrange("p (t f) -> p t f", t=4), ACT.Relu).then_inc(relued, 1)

            act_idx(act, PL1, 0, 0)
            win_copy(0, 0)
            win_copy(0, 1)
            with act.Fori(0, NIT) as i:
                half_landed(act, PL1, i - 1, 1)
                act_idx(act, PL1, i * U + HALF, 1)
                relu_sums(i, 0)
                win_copy(i, 2)
                relu_sums(i, 1)
                half_landed(act, PL1, i, 0)
                act_idx(act, PL1, i * U + U, 0)
                win_copy(i, 3)
                relu_sums(i, 2)
                win_copy(i, 4)
                relu_sums(i, 3)
                win_copy(i, 5)
            barrier(act, "act")

            def loop_c(k, x, y, z):
                m = k - 1
                if x:
                    copy(CX, k, "hc", hc_f, h_nm[:, nf(k)], "pe.H1T<", "dve.v<")
                if z:
                    CY.after(act, m - 1, "pe.THPH")
                    copy(CZ, m - 1, "tab", tb, n3(bank(0, NC))[:, :, 0:D], "sp.stored<", "dve.diff<")
                if x:
                    copy(CX, k, "agT", uT[0:D + 1], agg[0:D + 1, ncol(k)], "pe.DEG<")
                    copy(CX, k, "h1T", r1[0:D], bank(2, NC, rows=D), "pe.H1T", "pe.RU<")
                if y:
                    copy(CY, m, "squared", sq_f, xc_f, "dve.centred", func=ACT.Square)
                    copy(CY, m, "std", stat[:, 3], stat[:, 2], "dve.var", func=ACT.Sqrt)
                if x:
                    copy(CX, k, "rT", zT[0:D], bank(4, NC, rows=D), "pe.RU", "pe.O<", func=ACT.Relu, bias=w("bu1"))
                if y:
                    copy(CY, m, "hT", hT[0:D], bank(2, NC, rows=D), "pe.HT", "pe.THPH<")
                if x:
                    norm_parts(CX, k, "v")

            skewed(act, "act", (CX, CY, CZ), loop_c)

            def back_copy(i, g):
                act.wait_ge(back_t, i * 4 + g + 3)
                act.wait_ge(PL2.summed, i * U + 4 * g + 12)
                act.activation(back[:, g % 2, :], bank(4 + g % 2, 4 * D), ACT.Copy).then_inc(back_sb, 1)

            act.sem_inc(back_sb, 2)
            act_idx(act, PL2, 0, 0)
            act_idx(act, PL2, HALF, 1)

            def body2(i):
                back_copy(i, 0)
                half_landed(act, PL2, i, 0)
                act_idx(act, PL2, i * U + U, 0)
                back_copy(i, 1)
                back_copy(i, 2)

            body2(0)
            with act.Fori(1, NIT) as i:
                half_landed(act, PL2, i - 1, 1)
                act_idx(act, PL2, i * U + HALF, 1)
                back_copy(i - 1, 3)
                body2(i)
            back_copy(NIT - 1, 3)
            barrier(act, "act")

            def loop_d(k, x, y, z):
                m = k - 1
                if x:
                    copy(DX, k, "aggc", aggc[0:D], agg[0:D, ncol(k)], "pe.T<")
                if y:
                    copy(DY, m, "squared", sq_f, xc_f, "dve.centred", func=ACT.Square)
                if z:
                    DY.after(act, m - 1, "pe.SELF")
                    copy(DZ, m - 1, "self", big[:, ncol(m - 1)], bank(4, NC))
                if y:
                    copy(DY, m, "std", stat[:, 3], stat[:, 2], "dve.var", func=ACT.Sqrt)
                    copy(DY, m, "hT", hT[0:D], bank(2, NC, rows=D), "pe.HT", "pe.SELF<")

            skewed(act, "act", (DX, DY, DZ), loop_d)
            sum_pass(PL3a)

            def loop_e(k, x, y):
                m = k - 1
                if x:
                    copy(EX, k, "aggc", aggc[0:D], agg[0:D, ncol(k)], "pe.M<")
                if y:
                    EX.after(act, m, "dve.sum")
                    copy(EY, m, "z", zr_f, z_f, "pe.ZT<", "sp.stored<", func=ACT.Relu)
                    copy(EY, m, "zT", zT3, bank(2, NC), "pe.ZT", "pe.SELF<")

            skewed(act, "act", (EX, EY), loop_e)
            sum_pass(PL3b)

            def loop_f(k, x, y, z):
                m = k - 1
                if x:
                    copy(FX, k, "aggc", aggc, agg[:, ncol(k)], "pe.M<")
                if y:
                    FX.after(act, m, "dve.sum")
                    copy(FY, m, "z", zr_f, z_f, "pe.ZT<", func=ACT.Relu)
                if z:
                    FY.after(act, m - 1, "pe.BOTH")
                    copy(FZ, m - 1, "tab", tb, n3(bank(4, NC))[:, :, 0:D], "sp.stored<")
                if y:
                    copy(FY, m, "zT", zT3, bank(2, NC), "pe.ZT", "pe.BOTH<")

            skewed(act, "act", (FX, FY, FZ), loop_f)
            sum_pass(PL3c)

            GX.start(act, "act")
            with act.Fori(0, NLOOP) as i:
                copy(GX, i, "aggc", aggc[0:D], agg[0:D, ncol(i)], "pe.T<")
            barrier(act, "act")

        @block.vector
        def _(dve):
            count = [0]

            def setup(ins):
                count[0] += 1
                ins.then_inc(s_setup, 1)
                dve.wait_ge(s_setup, count[0])

            def chain(lp, i, name, ins):
                lp.done(ins, "dve", name)
                lp.after(dve, i, "dve." + name)

            def norm_centre(lp, i, src, pre="", xc=xc, stat=stat):
                chain(lp, i, pre + "sum", dve.reduce_sum(stat[:, 0], src, AX.X))
                chain(lp, i, pre + "centred", dve.scalar_tensor_tensor(
                    out=xc, in0=stat[:, 0].to_broadcast([P, C7, D]), scalar=-1.0 / D, in1=src, op0=ALU.mult,
                    op1=ALU.add))

            def norm_var(lp, i, pre="", sq=sq, stat=stat):
                lp.after(dve, i, f"act.{pre}squared")
                chain(lp, i, pre + "sumsq", dve.reduce_sum(stat[:, 1], sq, AX.X))
                chain(lp, i, pre + "var", dve.tensor_scalar(stat[:, 2], stat[:, 1], 1.0 / D, LN_EPS, ALU.mult, ALU.add))

            def norm_scale(lp, i, dst, pre="", relu=True, xc=xc, stat=stat):
                rstd = stat[:, 1]
                lp.after(dve, i, f"act.{pre}std")
                chain(lp, i, pre + "rstd", dve.reciprocal(rstd, stat[:, 3]))
                if relu:
                    ins = dve.scalar_tensor_tensor(out=dst, in0=xc, scalar=0.0, in1=rstd.to_broadcast([P, C7, D]),
                                                   op0=ALU.max, op1=ALU.mult)
                else:
                    ins = dve.tensor_tensor(dst, xc, rstd.to_broadcast([P, C7, D]), ALU.mult)
                chain(lp, i, pre + "normed", ins)

            def bcast(name, n=D):
                return w(name).rearrange("p (c f) -> p c f", c=1).to_broadcast([P, C7, n])

            dve.wait_ge(s_load_x, 2 * 16)
            setup(dve.tensor_copy(ident_b[:, :], w("ident")))
            setup(dve.tensor_scalar(one_eps[:, :], w("eps"), 1.0, None, ALU.add))
            barrier(dve, "dve")

            AX0.start(dve, "dve")
            AX1.start(dve, "dve")
            with dve.Fori(0, NLOOP // 2) as k:
                two = [(h, lp, st, n3(x_nm[:, nf(k * 2 + h)])) for h, lp, st in ((0, AX0, stat), (1, AX1, stat1))]
                for h, lp, st, xk in two:
                    norm_centre(lp, k, xk, xc=a_xc[:, h], stat=st)
                for h, lp, st, _ in two:
                    norm_var(lp, k, sq=a_sq[:, h], stat=st)
                for h, lp, st, _ in two:
                    AY.after(dve, k, f"pe.HT{h}<")
                    norm_scale(lp, k, a_hs[:, h], xc=a_xc[:, h], stat=st)
                for h, lp, _, _ in two:
                    AX1.after(dve, k, "sp.stored<")
                    chain(lp, k, "tab", dve.tensor_tensor(a_tb[:, h], a_hs[:, h], bcast("we_b"), ALU.add))

            dve.wait_ge(s_load, 7 * 16)
            dst, nxt, dstrow, prevrow, base_b = (big[:, k * NT:(k + 1) * NT].bitcast(I32) for k in range(5))
            f0, f1 = big[:, 5 * NT:6 * NT], big[:, 6 * NT:7 * NT]
            rel_f, m_f = h_nm[:, 0:NT], h_nm[:, NT:2 * NT]
            hi_i, lo_i = f0.bitcast(I32), f1.bitcast(I32)
            setup(dve.tensor_scalar(hi_i, src_idx[:, 0:NT], 7, None, ALU.logical_shift_right))
            setup(dve.tensor_scalar(lo_i, src_idx[:, 0:NT], P - 1, None, ALU.bitwise_and))
            setup(dve.scalar_tensor_tensor(out=src_idx[:, 0:NT], in0=lo_i, scalar=float(CHUNKS), in1=hi_i,
                                           op0=ALU.mult, op1=ALU.add))
            setup(dve.tensor_tensor(rel_f, dst, base_b, ALU.subtract))
            setup(dve.tensor_copy(rel[:, 0:NT], rel_f))
            barrier(dve, "dve")

            def sum_pass(ps):
                dve.sem_inc(ps.added, 4)
                dve_s(dve, ps, 0, rel, range(HALF))
                with dve.Fori(0, NIT) as i:
                    b = dve_bases(bass.ds(i * U, U))
                    for j in range(U):
                        dve_add(dve, ps, b, i, [j])
                        dve_s(dve, ps, i, rel, [j + HALF])
                barrier(dve, "dve")

            dve.memset(ef_f[:, :], 1.0).then_inc(s_ones, 1)
            setup(dve.tensor_tensor(m_f, dst, nxt, ALU.not_equal))
            setup(dve.scalar_tensor_tensor(out=rel_f, in0=rel_f, scalar=1.0, in1=m_f, op0=ALU.add, op1=ALU.mult))
            setup(dve.tensor_scalar(rel_end[:, 0:NT], rel_f, -1.0, None, ALU.add))
            setup(dve.tensor_tensor(m_f, dstrow, prevrow, ALU.is_equal))
            setup(dve.tensor_scalar(m_f, m_f, -0.5, 3.3895313892515355e38, ALU.add, ALU.mult))
            dve.tensor_scalar(mask_f, m_f, 2.0, None, ALU.mult).then_inc(s_mask, 1)
            sum_pass(PL0)

            setup(dve.memset(part_hm[:, ROWS:COLS], 0.0))
            setup(dve.memset(part_lo[:, ROWS:COLS], 0.0))

            def loop_b(k, x, y, z):
                m = k - 1
                if y:
                    norm_centre(BY, m, n3(x_nm[:, nf(m)]))
                if z:
                    BY.after(dve, m - 1, "act.high")
                    BZ.after(dve, m - 1, "act.midlow<", "pool.lo<")
                    chain(BZ, m - 1, "rest1", dve.tensor_tensor(r1, bank(5, NC), part_hm[:, ncol(m - 1)],
                                                                ALU.subtract))
                if y:
                    norm_var(BY, m)
                    BY.after(dve, m, "pe.HT<", "pool.h<")
                    norm_scale(BY, m, hs)
                if x:
                    xk = x_nm[:, nf(k)]
                    chain(BX, k, "bias", dve.tensor_tensor(n3(xk), n3(xk), bcast("b2"), ALU.add))
                    BX.after(dve, k, "pe.O")
                    chain(BX, k, "x", dve.tensor_tensor(xk, bank(4, NF), xk, ALU.add))

            skewed(dve, "dve", (BX, BY, BZ), loop_b)

            def lagging_adds(ps, column, step):
                def group(i, g):
                    step(i, g)
                    dve_s(dve, ps, i, column, range(4 * g + HALF, 4 * g + HALF + 4))

                dve_s(dve, ps, 0, column, range(HALF))
                b = dve_bases(slice(0, U))
                for g in range(4):
                    group(0, g)
                    if g > 0:
                        dve_add(dve, ps, b, 0, range(4 * g - 4, 4 * g))
                with dve.Fori(1, NIT) as i:
                    b = dve_bases(bass.ds(i * U - 4, U))
                    for g in range(4):
                        group(i, g)
                        dve_add(dve, ps, b, i, range(4 * g - 4, 4 * g), 4)
                b = dve_bases(slice(NT - 4, NT))
                dve_add(dve, ps, b, NIT, range(-4, 0), 4)

            setup(dve.memset(msg1[:, :, D:D + 1], 1.0))
            dve.sem_inc(PL1.added, 4)
            dve.sem_inc(PL1.used, 4)

            def edge_sums(i, g):
                dve.wait_ge(pre_mm, i * U + 4 * g + 4 + 8)
                dve.wait_ge(relued, i * 4 + g + 1)
                if g % 2 == 0:
                    dve.wait_ge(ew_in_sem[g // 2], i * 16 + 16)
                dve.tensor_tensor(pre[:, g % 2, :], bank(4 + g % 2, 4 * D),
                                  ewl[:, g // 2, (g % 2) * 4 * D:(g % 2 + 1) * 4 * D], ALU.add).then_inc(pre_ew, 1)
                dve.wait_ge(pre_ew, i * 4 + g + 1)
                for j in range(4 * g, 4 * g + 4):
                    tile_landed(dve, PL1, i, j)
                dve.tensor_tensor(pre[:, g % 2, :], pre[:, g % 2, :],
                                  msg_f[:, 4 * g * D:4 * (g + 1) * D], ALU.add).then_inc(PL1.used, 1)

            lagging_adds(PL1, rel, edge_sums)
            barrier(dve, "dve")

            dve.wait_ge(s_comb, 1)
            dve.tensor_copy(wcomb[:, :], bank(0, D, rows=D + 1)).then_inc(s_comb, 1)
            setup(dve.memset(zT[D:D + 1], 1.0))
            setup(dve.memset(hT[D:D + 1], 1.0))

            def loop_c(k, x, y, z):
                m = k - 1
                if y:
                    norm_centre(CY, m, n3(x_nm[:, nf(m)]))
                if z:
                    CZ.after(dve, m - 1, "act.tab")
                    chain(CZ, m - 1, "diff", dve.tensor_tensor(n3(h_nm[:, nf(m - 1)]), n3(bank(0, NC))[:, :, D:2 * D],
                                                               tb, ALU.subtract))
                if y:
                    norm_var(CY, m)
                    CY.after(dve, m, "pe.HT<")
                    norm_scale(CY, m, hs)
                if x:
                    xk = x_nm[:, nf(k)]
                    CX.after(dve, k, "pe.DEG")
                    chain(CX, k, "deg", dve.tensor_copy(deg[:, bass.ds(k * C7, C7)], bank(7, C7 * (D + 1)).rearrange(
                        "p (c f) -> p c f", c=C7)[:, :, D]))
                    CX.after(dve, k, "pe.O", "act.hc")
                    chain(CX, k, "v", dve.tensor_tensor(vv, n3(bank(6, NF)), hc, ALU.add))
                    norm_centre(CX, k, vv, "v")
                    norm_var(CX, k, "v")
                    norm_scale(CX, k, vv, "v", relu=False)
                    chain(CX, k, "scaled", dve.tensor_tensor(vv, vv, bcast("gamma"), ALU.mult))
                    chain(CX, k, "shifted", dve.tensor_tensor(vv, vv, bcast("beta"), ALU.add))
                    chain(CX, k, "x", dve.tensor_tensor(xk, v_f, xk, ALU.add))

            skewed(dve, "dve", (CX, CY, CZ), loop_c)
            setup(dve.tensor_scalar(rdeg[:, :, 0], deg[:, :], 1.0, None, ALU.max))
            setup(dve.reciprocal(rdeg[:, :, 0], rdeg[:, :, 0]))
            setup(dve.tensor_scalar(no_in[:, :, 0], deg[:, :], 0.0, None, ALU.is_equal))

            setup(dve.memset(run[:, 1, :], 0.0))
            dve.sem_inc(PL2.added, 4)
            dve.sem_inc(scanned, 4)

            def scan(i, g):
                dve.wait_ge(PL2.used, i * U + 4 * g + 4 + U)
                dve.wait_ge(back_t, i * 4 + g + 1)
                dve.wait_ge(scanned, i * 4 + g + 4)
                if g % 2 == 0:
                    dve.wait_ge(mask_in_sem[g // 2], i * 16 + 16)
                dve.tensor_tensor_scan(out=run[:, g % 2, :], data0=mask[:, g // 2, (g % 2) * 4 * P:(g % 2 + 1) * 4 * P],
                                       data1=bank(g % 2, 4 * P, rows=D), initial=run[:, (g + 1) % 2, 4 * P - 1:4 * P],
                                       op0=ALU.min, op1=ALU.max).then_inc(scanned, 1)

            lagging_adds(PL2, rel_end, scan)
            barrier(dve, "dve")

            setup(dve.memset(hT[D:D + 1], 1.0))

            def loop_d(k, x, y):
                m = k - 1
                if y:
                    norm_centre(DY, m, n3(x_nm[:, nf(m)]))
                if x:
                    chain(DX, k, "zero", dve.memset(kept, 0.0))
                if y:
                    norm_var(DY, m)
                    DY.after(dve, m, "pe.HT<", "sp.stored<")
                    norm_scale(DY, m, hs)
                if x:
                    xk = x_nm[:, nf(k)]
                    DX.after(dve, k, "pe.T")
                    chain(DX, k, "y", dve.tensor_tensor(v_f, bank(0, NF), h_nm[:, nf(k)], ALU.add))
                    chain(DX, k, "keep", dve.scalar_tensor_tensor(
                        out=hc, in0=vv, scalar=0.0, in1=no_in[:, bass.ds(k * C7, C7), :].to_broadcast([P, C7, D]),
                        op0=ALU.mult, op1=ALU.is_equal))
                    hold(dve)
                    chain(DX, k, "kept", dve.copy_predicated(kept, hc_f.bitcast(I32), v_f))
                    chain(DX, k, "x", dve.tensor_tensor(xk, kept, xk, ALU.add))

            skewed(dve, "dve", (DX, DY), loop_d)

            def mean_and_self(stage, other, k):
                stage.after(dve, k, "pe.M")
                other.after(dve, k, "act.z<")
                chain(stage, k, "mean", dve.tensor_tensor(
                    z_f.rearrange("p (c f) -> p c f", c=C7), bank(0, NC).rearrange("p (c f) -> p c f", c=C7),
                    rdeg[:, bass.ds(k * C7, C7), :].to_broadcast([P, C7, H]), ALU.mult))
                chain(stage, k, "sum", dve.tensor_tensor(z_f, z_f, big[:, ncol(k)], ALU.add))

            def loop_e(k, x, y):
                if x:
                    mean_and_self(EX, EY, k)
                if y:
                    EY.after(dve, k - 1, "pe.SELF")
                    chain(EY, k - 1, "self", dve.tensor_tensor(
                        big[:, ncol(k - 1)].rearrange("p (c f) -> p c f", c=C7),
                        bank(4, NC).rearrange("p (c f) -> p c f", c=C7), bcast("sb1", H), ALU.add))

            def loop_f(k, x, y, z):
                if x:
                    mean_and_self(FX, FY, k)
                if z:
                    FZ.after(dve, k - 2, "act.tab")
                    chain(FZ, k - 2, "self", dve.tensor_tensor(
                        n3(h_nm[:, nf(k - 2)]), n3(bank(4, NC))[:, :, D:2 * D], bcast("sb2"), ALU.add))

            sum_pass(PL3a)
            skewed(dve, "dve", (EX, EY), loop_e)
            sum_pass(PL3b)
            skewed(dve, "dve", (FX, FY, FZ), loop_f)
            sum_pass(PL3c)

            GX.start(dve, "dve")
            with dve.Fori(0, NLOOP) as i:
                GX.after(dve, i, "pe.T")
                chain(GX, i, "mean", dve.tensor_tensor(
                    vv, n3(bank(0, NF)), rdeg[:, bass.ds(i * C7, C7), :].to_broadcast([P, C7, D]), ALU.mult))
                chain(GX, i, "sum", dve.tensor_tensor(v_f, v_f, h_nm[:, nf(i)], ALU.add))
                chain(GX, i, "x", dve.scalar_tensor_tensor(out=x_nm[:, nf(i)], in0=v_f, scalar=0.0, in1=x_nm[:, nf(i)],
                                                           op0=ALU.max, op1=ALU.add))
            barrier(dve, "dve")

        @block.tensor
        def _(pe):
            def mm(out_, lhsT, rhs, start=True, stop=True):
                return pe.matmul(out_, lhsT, rhs, start=start, stop=stop)

            def transposes(dst_bank, src3, rows_in, cols_in):
                hold(pe)
                for c in range(C7):
                    last = pe.transpose(bank(dst_bank, rows_in, c * rows_in, cols_in), src3(c),
                                        w("ident")[0:rows_in, 0:rows_in])
                return last

            barrier(pe, "pe")
            AY.start(pe, "pe")
            with pe.Fori(0, NLOOP // 2) as i:
                for h, lp in enumerate((AX0, AX1)):
                    lp.after(pe, i, "dve.normed")
                    AY.after(pe, i, f"act.hT{h}<")
                    AY.done(transposes(2 * h, lambda c, h=h: a_hs[:, h, c, :], P, D), "pe", f"HT{h}")
            barrier(pe, "pe")

            def sum_tiles(ps, i, js, message, waits=None):
                for j in js:
                    if waits:
                        waits(j)
                    pe.wait_ge(ps.s_ready, i * U + j + 1)
                    pe.wait_ge(ps.added, i * U + j + 1)
                    mm(acc_slot(j, ps.rows), message(j), S[:, j, :]).then_inc(ps.summed, 1)

            pe.sem_inc(PL0.summed, U)
            pe.sem_inc(ew_free, 2)
            with pe.Fori(0, NIT) as i:
                for h in range(2):
                    pe.wait_ge(ef_in_sem[h], i * 16 + 16)
                    pe.wait_ge(ew_sb, i * 2 + h + 1)
                    for t in range(HALF):
                        last = mm(bank(4 + h, D, t * D), ef[0:17, h, t * P:(t + 1) * P], w("wc"))
                    last.then_inc(ew_mm, 1)
                    pe.wait_ge(ea_in_sem[h], i * 16 + 16)
                    for j in range(h * HALF, (h + 1) * HALF):
                        pe.wait_ge(PL0.s_ready, i * U + j + 1)
                        pe.wait_ge(PL0.added, i * U + j + 1)
                        mm(acc_slot(j, P)[D:P], ea[:, j, :], S[:, j, :])
                        tile_landed(pe, PL0, i, j)
                        mm(acc_slot(j, P)[0:D], PL0.msg[:, j, :], S[:, j, :]).then_inc(PL0.summed, 1)
            barrier(pe, "pe")

            def loop_b(k, x, y, z):
                m = k - 1
                if x:
                    BX.after(pe, k, "act.uT<")
                    for a, b in halves():
                        last = mm(bank(0, b - a, a, D), w("we"), agg[:, bass.ds(k * NC + a, b - a)])
                    BX.done(last, "pe", "U")
                if x:
                    BX.after(pe, k, "act.uT", "act.zT<")
                    for a, b in halves():
                        last = mm(bank(2, b - a, a), w("w1"), uT[0:D, a:b])
                    BX.done(last, "pe", "Z")
                if y:
                    BY.after(pe, m, "dve.normed", "act.high<")
                    if z:
                        BZ.after(pe, m - 1, "dve.rest1")
                    BY.done(transposes(5, lambda c: hs[:, c, :], P, D), "pe", "HT")
                if x:
                    BX.after(pe, k, "act.zT", "dve.x<")
                    for c in range(C7):
                        last = mm(bank(4, D, c * D), zT[:, chunk(c)], w("w2"))
                    BX.done(last, "pe", "O")
                if y:
                    BY.after(pe, m, "act.hT")
                    for a, b in halves():
                        last = mm(bank(5, b - a, a), w("wa2"), hT[0:D, a:b])
                    BY.done(last, "pe", "APT")
                    BY.after(pe, m, "act.tab<")
                    hold(pe)
                    for c in range(C7):
                        last = mm(bank(7, D, c * D), hT[0:D, chunk(c)], w("wb"))
                    BY.done(last, "pe", "TAB")

            skewed(pe, "pe", (BX, BY, BZ), loop_b)

            pe.sem_inc(PL1.summed, U)
            pe.sem_inc(pre_mm, 8)

            def windows(i, b, g):
                for j in range(4 * g, 4 * g + 4):
                    pe.wait_ge(PL1.s_ready, i * U + j + 1)
                    pe.wait_ge(win_sb, i * U + j + 3)
                    at = bass.ds(b[j - HALF] if b else base0[j], P)
                    mm(bank(j % 2, P), part_hm[:, at], ident_b[:, :])
                    mm(bank(j % 2, D, P), part_lo[:, at], ident_b[0:D, 0:D])
                    pe.transpose(bank(j % 2, P, 3 * D), S[:, j % U, :], w("ident")).then_inc(win_t, 1)

            def dst_terms(i, g):
                pe.wait_ge(PL1.used, i * 4 + g + 3)
                for j in range(4 * g, 4 * g + 4):
                    pe.wait_ge(win_sb, i * U + j + 5)
                    for k in range(3):
                        last = mm(bank(4 + g % 2, D, j % 4 * D), win[:, j % 8, 3 * D:WIN],
                                  win[:, j % 8, k * D:(k + 1) * D], start=k == 0, stop=k == 2)
                    last.then_inc(pre_mm, 1)

            def sums1(i, g):
                pe.wait_ge(relued, i * 4 + g + 3)
                sum_tiles(PL1, i, range(4 * g, 4 * g + 4), lambda j: msg1[:, j, :])

            _, base0 = nc.values_load_multi_w_load_instructions(
                base[0:1, 0:HALF], engines=[mybir.EngineType.PE], min_val=0, max_val=N,
                skip_runtime_bounds_check_because="dst holds node numbers below N, the padding N")
            windows(0, None, 0)
            windows(0, None, 1)
            dst_terms(0, 0)
            with pe.Fori(0, NIT) as i:
                _, b = nc.values_load_multi_w_load_instructions(
                    base[0:1, bass.ds(i * U + HALF, U)], engines=[mybir.EngineType.PE], min_val=0, max_val=N,
                    skip_runtime_bounds_check_because="dst holds node numbers below N, the padding N")
                for g in range(4):
                    dst_terms(i, g + 1)
                    sums1(i, g)
                    windows(i, b, g + 2)
            barrier(pe, "pe")

            mm(bank(0, D, rows=D + 1), w("wm2t"), w("wu1b")).then_inc(s_comb, 1)
            pe.wait_ge(s_comb, 2)
            hold(pe)

            def loop_c(k, x, y):
                m = k - 1
                if x:
                    CX.after(pe, k, "act.hc")
                    if y:
                        CY.after(pe, m, "act.hT<")
                    CX.done(transposes(2, lambda c: hc[:, c, :], P, D), "pe", "H1T")
                    CX.after(pe, k, "act.rT<")
                    for a, b in halves():
                        mm(bank(4, b - a, a, D), wcomb[:, :], agg[0:D + 1, bass.ds(k * NC + a, b - a)], stop=False)
                    CX.after(pe, k, "act.h1T")
                    hold(pe)
                    for a, b in halves():
                        last = mm(bank(4, b - a, a, D), w("wu1a"), r1[0:D, a:b], start=False)
                    CX.done(last, "pe", "RU")
                if y:
                    CY.after(pe, m, "dve.normed")
                    CX.after(pe, k if x else m, "act.h1T")
                    CY.done(transposes(2, lambda c: hs[:, c, :], P, D), "pe", "HT")
                if x:
                    CX.after(pe, k, "act.agT", "dve.deg<")
                    hold(pe)
                    for c in range(C7):
                        last = pe.transpose(bank(7, D + 1, c * (D + 1)), uT[0:D + 1, chunk(c)],
                                            w("ident")[0:D + 1, 0:D + 1])
                    CX.done(last, "pe", "DEG")
                    CX.after(pe, k, "act.rT", "dve.v<")
                    for c in range(C7):
                        last = mm(bank(6, D, c * D), zT[0:D + 1, chunk(c)], w("wu2"))
                    CX.done(last, "pe", "O")
                if y:
                    CY.after(pe, m, "act.hT")
                    CZ.after(pe, m, "act.tab<", "dve.diff<")
                    for c in range(C7):
                        last = mm(bank(0, H, c * H), hT[0:D + 1, chunk(c)], w("thph"))
                    CY.done(last, "pe", "THPH")

            skewed(pe, "pe", (CX, CY), loop_c)

            pe.sem_inc(PL2.used, U)
            pe.sem_inc(PL2.summed, U)
            pe.sem_inc(back_t, 2)

            def forth(i, g):
                pe.wait_ge(scanned, i * 4 + g + 3)
                for j in range(4 * g, 4 * g + 4):
                    tile_landed(pe, PL2, i, j)
                    hold(pe)
                    pe.transpose(bank(g % 2, P, j % 4 * P, D), PL2.msg[:, j, :], w("ident")).then_inc(PL2.used, 1)

            def back_and_sums(i, g):
                pe.wait_ge(scanned, i * 4 + g + 5)
                pe.wait_ge(back_sb, i * 4 + g + 1)
                hold(pe)
                for j in range(4):
                    last = pe.transpose(bank(4 + g % 2, D, j * D), run[:, g % 2, j * P:(j + 1) * P],
                                        w("ident")[0:D, 0:D])
                last.then_inc(back_t, 1)
                pe.wait_ge(back_sb, i * 4 + g + 3)
                sum_tiles(PL2, i, range(4 * g, 4 * g + 4), lambda j: back[:, g % 2, j % 4 * D:(j % 4 + 1) * D])

            def group2(i, g, back=True):
                forth(i, g)
                if back:
                    back_and_sums(i if g else i - 1, (g - 1) % 4)

            for g in range(4):
                group2(0, g, back=g > 0)
            with pe.Fori(1, NIT) as i:
                for g in range(4):
                    group2(i, g)
            back_and_sums(NIT - 1, 3)
            barrier(pe, "pe")

            def loop_d(k, x, y):
                m = k - 1
                if x:
                    DX.after(pe, k, "act.aggc", "dve.y<")
                    hold(pe)
                    for c in range(C7):
                        last = pe.transpose(bank(0, D, c * D), aggc[0:D, chunk(c)], w("ident")[0:D, 0:D])
                    DX.done(last, "pe", "T")
                if y:
                    DY.after(pe, m, "dve.normed", "act.hT<")
                    DY.done(transposes(2, lambda c: hs[:, c, :], P, D), "pe", "HT")
                    DY.after(pe, m, "act.hT")
                    DZ.after(pe, m, "act.self<")
                    for c in range(C7):
                        last = mm(bank(4, H, c * H), hT[0:D + 1, chunk(c)], w("ws0"))
                    DY.done(last, "pe", "SELF")

            skewed(pe, "pe", (DX, DY), loop_d)

            def sage_pass(ps):
                pe.sem_inc(ps.summed, U)
                with pe.Fori(0, NIT) as i:
                    sum_tiles(ps, i, range(U), lambda j: ps.msg[:, j, :], waits=lambda j: tile_landed(pe, ps, i, j))
                barrier(pe, "pe")

            sage_pass(PL3a)
            def loop_e(k, x, y):
                m = k - 1
                if x:
                    EX.after(pe, k, "act.aggc", "dve.mean<")
                    for c in range(C7):
                        last = mm(bank(0, H, c * H), aggc[0:D, chunk(c)], w("wn0"))
                    EX.done(last, "pe", "M")
                if y:
                    EY.after(pe, m, "act.z", "act.zT<")
                    EY.done(transposes(2, lambda c: zr[:, c, :], P, H), "pe", "ZT")
                    EY.after(pe, m, "act.zT", "dve.self<")
                    for c in range(C7):
                        last = mm(bank(4, H, c * H), zT3[:, chunk(c)], w("ws1"))
                    EY.done(last, "pe", "SELF")

            skewed(pe, "pe", (EX, EY), loop_e)

            sage_pass(PL3b)
            def loop_f(k, x, y):
                m = k - 1
                if x:
                    FX.after(pe, k, "act.aggc", "dve.mean<")
                    for c in range(C7):
                        last = mm(bank(0, H, c * H), aggc[:, chunk(c)], w("wn1"))
                    FX.done(last, "pe", "M")
                if y:
                    FY.after(pe, m, "act.z", "act.zT<")
                    FY.done(transposes(2, lambda c: zr[:, c, :], P, H), "pe", "ZT")
                    FY.after(pe, m, "act.zT")
                    FZ.after(pe, m, "act.tab<", "dve.self<")
                    for c in range(C7):
                        last = mm(bank(4, H, c * H), zT3[:, chunk(c)], w("wns2"))
                    FY.done(last, "pe", "BOTH")

            skewed(pe, "pe", (FX, FY), loop_f)

            sage_pass(PL3c)
            GX.start(pe, "pe")
            with pe.Fori(0, NLOOP) as i:
                GX.after(pe, i, "act.aggc", "dve.mean<")
                hold(pe)
                for c in range(C7):
                    last = pe.transpose(bank(0, D, c * D), aggc[0:D, chunk(c)], w("ident")[0:D, 0:D])
                GX.done(last, "pe", "T")
            barrier(pe, "pe")


def kernel(x, src, dst, edge_attr_16, edge_attr_64, L0_gnn_We_w, L0_gnn_We_b, L0_gnn_eps, L0_gnn_W1, L0_gnn_b1,
           L0_gnn_W2, L0_gnn_b2, L1_gnn_W_m1, L1_gnn_b_m1, L1_gnn_W_m2, L1_gnn_b_m2, L1_gnn_W_u1, L1_gnn_b_u1,
           L1_gnn_W_u2, L1_gnn_b_u2, L1_gnn_gamma, L1_gnn_beta, L2_gnn_theta_w, L2_gnn_theta_b, L2_gnn_phi_w,
           L2_gnn_phi_b, L3_gnn_ws0, L3_gnn_wn0, L3_gnn_b0, L3_gnn_ws1, L3_gnn_wn1, L3_gnn_b1, L3_gnn_ws2,
           L3_gnn_wn2, L3_gnn_b2):
    import concourse.bacc as bacc
    from concourse.bass_utils import run_bass_kernel_spmd

    a = np.asarray
    pad = NT * P - E

    def tiles(v):
        return np.ascontiguousarray(v.reshape(NT, P).T)

    def rows(v):
        return np.ascontiguousarray(v.reshape(NT // P, P, P).transpose(1, 0, 2).reshape(P, NT))

    src_p = np.pad(a(src), (0, pad))
    dst_p = np.pad(a(dst), (0, pad), constant_values=N)
    next_p = np.concatenate([dst_p[1:], np.full(1, -1, dst_p.dtype)])
    prev_p = np.concatenate([np.full(1, -1, dst_p.dtype), dst_p[:-1]])
    x_p = np.pad(a(x), ((0, ROWS - N), (0, 0))).reshape(CHUNKS, P, D).transpose(1, 0, 2).reshape(P, CHUNKS * D)
    ea_p = np.pad(a(edge_attr_64), ((0, pad), (0, 0))).reshape(NT // HALF, HALF, P, D).transpose(0, 2, 1, 3)
    ef_p = np.pad(a(edge_attr_16), ((0, pad), (0, 0))).T

    eye = np.eye(P, dtype=np.float32)
    row = lambda v: a(v).reshape(1, -1)
    col = lambda v: a(v).reshape(-1, 1)
    every = lambda v, c: np.broadcast_to(a(v).reshape(1, -1), (P, c))
    wm1 = a(L1_gnn_W_m1)
    parts = dict(
        ident=eye, iota=np.broadcast_to(np.arange(P, dtype=np.float32), (P, P)),
        we=np.concatenate([eye[0:D, 0:D], a(L0_gnn_We_w)]), w1=a(L0_gnn_W1), b1=col(L0_gnn_b1), w2=a(L0_gnn_W2),
        b2=every(L0_gnn_b2, D), we_b=every(L0_gnn_We_b, D), eps=every(L0_gnn_eps, 1),
        wa2=np.concatenate([wm1[0:D], wm1[0:D]], axis=1), wb=wm1[D:2 * D],
        wc=np.concatenate([wm1[2 * D:], row(L1_gnn_b_m1)]),
        wm2t=np.concatenate([a(L1_gnn_W_m2).T, col(L1_gnn_b_m2)], axis=1),
        wu1a=a(L1_gnn_W_u1)[0:D], wu1b=a(L1_gnn_W_u1)[D:], bu1=col(L1_gnn_b_u1),
        wu2=np.concatenate([a(L1_gnn_W_u2), row(L1_gnn_b_u2)]),
        gamma=every(L1_gnn_gamma, D), beta=every(L1_gnn_beta, D),
        thph=np.block([[a(L2_gnn_theta_w).T, a(L2_gnn_phi_w).T], [row(L2_gnn_theta_b), row(L2_gnn_phi_b)]]),
        ws0=np.concatenate([a(L3_gnn_ws0), row(L3_gnn_b0)]), wn0=a(L3_gnn_wn0), ws1=a(L3_gnn_ws1),
        sb1=every(L3_gnn_b1, H), wn1=a(L3_gnn_wn1), wns2=np.concatenate([a(L3_gnn_wn2), a(L3_gnn_ws2)], axis=1),
        sb2=every(L3_gnn_b2, D), zero=np.zeros((P, 1), np.float32))
    pack = np.zeros((P, WCOLS), np.float32)
    for name, (r, c) in PACK.items():
        pack[0:r, AT[name]:AT[name] + c] = parts[name]

    arrays = dict(x_nm_in=np.ascontiguousarray(x_p), src_in=tiles(src_p), dst_in=tiles(dst_p),
                  next_in=tiles(next_p), dstrow_in=rows(dst_p), prevrow_in=rows(prev_p),
                  ea_in=np.ascontiguousarray(ea_p.reshape(NT // HALF * P, HALF * D)),
                  ef_in=np.ascontiguousarray(ef_p), pack_in=pack)
    nc = bacc.Bacc("TRN2", target_bir_lowering=False, num_devices=1)
    args = [nc.dram_tensor(n, v.shape, mybir.dt.from_np(v.dtype), kind="ExternalInput").ap()
            for n, v in arrays.items()]
    out = nc.dram_tensor("x_out", (P, CHUNKS * D), F32, kind="ExternalOutput").ap()
    gnn(nc, *args, out)
    r = run_bass_kernel_spmd(nc, [arrays], core_ids=[0])
    y = np.asarray(r.results[0]["x_out"]).reshape(P, CHUNKS, D).transpose(1, 0, 2).reshape(ROWS, D)
    return np.ascontiguousarray(y[0:N])
```
